# Optimizing a Trainium2 kernel written in Bass

```python
import numpy as np
import jax
import jax.numpy as jnp

def _softmax(x, axis=-1):
    return jax.nn.softmax(x, axis=axis)

def _gelu(x):
    return jax.nn.gelu(x, approximate=True)

def _silu(x):
    return jax.nn.silu(x)

def _sigmoid(x):
    return jax.nn.sigmoid(x)

def _layernorm(x, axis=-1, eps=1e-05):
    m = jnp.mean(x, axis=axis, keepdims=True)
    v = jnp.var(x, axis=axis, keepdims=True)
    return (x - m) / jnp.sqrt(v + eps)

def _scatter_add(tgt, idx, src, axis=0):
    return tgt.at[idx].add(src)

def _segment_sum(src, seg, n):
    return jax.ops.segment_sum(src, seg, n)
kernel_name = 'mk_gnn_preln_d2_gnn_r32_064d61'

def setup_inputs(seed: int=0):
    np.random.seed(seed)
    _w = jnp.asarray

    def _rec_inputs():
        import jax
        import jax.numpy as jnp
        _gk = jax.random.key(seed)
        x = 7.22e-05 + 1 * jax.random.normal(jax.random.fold_in(_gk, 1), (3125, 128), jnp.float32)
        _s = jax.random.randint(jax.random.fold_in(_gk, 2), (50000,), 0, 3125, jnp.int32)
        _d = jax.random.randint(jax.random.fold_in(_gk, 3), (50000,), 0, 3125, jnp.int32)
        _loop = jnp.arange(3125, dtype=jnp.int32)
        src = jnp.concatenate([_s, _d, _loop])
        dst = jnp.concatenate([_d, _s, _loop])
        _o = jnp.argsort(dst, stable=True)
        src = src[_o]
        dst = dst[_o]
        edge_type_16 = jax.random.randint(jax.random.fold_in(_gk, 13), (103125,), 0, 16, jnp.int32)
        edge_weight = jax.random.uniform(jax.random.fold_in(_gk, 14), (103125,), jnp.float32, 0.0, 1)
        edge_weight1 = jax.random.uniform(jax.random.fold_in(_gk, 15), (103125, 1), jnp.float32, 0.0, 1)
        return (x, src, dst, edge_type_16, edge_weight, edge_weight1)
    x, src, dst, edge_type_16, edge_weight, edge_weight1 = _rec_inputs()

    def _L0_gnn_setup():
        import jax, jax.numpy as jnp
        import numpy as np
        N_NODES = 2048
        N_EDGES = 32768
        IN_F = 128
        HID_F = 128
        OUT_F = 128

        def _degrees(src, dst, n_nodes):
            ones = jnp.ones(src.shape[0], dtype=jnp.float32)
            deg_out = jax.ops.segment_sum(ones, src, num_segments=n_nodes)
            deg_in = jax.ops.segment_sum(ones, dst, num_segments=n_nodes)
            return (jnp.clip(deg_out, 1.0, None), jnp.clip(deg_in, 1.0, None))

        def _graph_conv(feat, W, b, src, dst, out_norm, in_norm, n_nodes):
            h = feat * out_norm[:, None]
            h = h @ W
            agg = jax.ops.segment_sum(h[src], dst, num_segments=n_nodes)
            return agg * in_norm[:, None] + b
        key = jax.random.key(seed)
        ks = jax.random.split(key, 8)
        feat = jax.random.normal(ks[0], (N_NODES, IN_F), dtype=jnp.float32)
        eweight = jax.random.uniform(ks[1], (N_EDGES, 1), dtype=jnp.float32)
        W1 = jax.random.normal(ks[2], (IN_F, HID_F), dtype=jnp.float32) * (1.0 / np.sqrt(IN_F))
        b1 = jnp.zeros((HID_F,), dtype=jnp.float32)
        W2 = jax.random.normal(ks[3], (HID_F, OUT_F), dtype=jnp.float32) * (1.0 / np.sqrt(HID_F))
        b2 = jnp.zeros((OUT_F,), dtype=jnp.float32)
        src = jax.random.randint(ks[4], (N_EDGES,), 0, N_NODES, dtype=jnp.int32)
        dst = jax.random.randint(ks[5], (N_EDGES,), 0, N_NODES, dtype=jnp.int32)
        return {'feat': feat, 'eweight': eweight, 'W1': W1, 'b1': b1, 'W2': W2, 'b2': b2, 'src': src, 'dst': dst}
    _L0_gnn_all = _L0_gnn_setup()
    _L0_gnn_in = {k: v for k, v in _L0_gnn_all.items() if k in ('W1', 'b1', 'W2', 'b2')}
    del _L0_gnn_all

    def _L1_gnn_setup():
        import jax, jax.numpy as jnp
        import numpy as np
        N, D, R, NB, E = (50000, 128, 16, 10, 50000)
        DECAY_RATE = 0.1
        LN_EPS = 1e-05
        key = jax.random.key(seed)
        ks = jax.random.split(key, 12)
        x = jax.random.normal(ks[0], (N, D), dtype=jnp.float32)
        edge_index = jax.random.randint(ks[1], (2, E), 0, N, dtype=jnp.int64)
        edge_type = jax.random.randint(ks[2], (E,), 0, R, dtype=jnp.int64)
        edge_time = jax.random.uniform(ks[3], (E,), dtype=jnp.float32)
        s = 1.0 / np.sqrt(D)
        basis = jax.random.normal(ks[4], (NB, D, D), dtype=jnp.float32) * s
        comp = jax.random.normal(ks[5], (R, NB), dtype=jnp.float32) * (1.0 / np.sqrt(NB))
        root = jax.random.normal(ks[6], (D, D), dtype=jnp.float32) * s
        bias = jnp.zeros((D,), dtype=jnp.float32)
        tp_w = jax.random.normal(ks[7], (D, D), dtype=jnp.float32) * s
        tp_b = jnp.zeros((D,), dtype=jnp.float32)
        gamma = jnp.ones((D,), dtype=jnp.float32)
        beta = jnp.zeros((D,), dtype=jnp.float32)
        return {'x': x, 'edge_index': edge_index, 'edge_type': edge_type, 'edge_time': edge_time, 'basis': basis, 'comp': comp, 'root': root, 'bias': bias, 'tp_w': tp_w, 'tp_b': tp_b, 'gamma': gamma, 'beta': beta}
    _L1_gnn_all = _L1_gnn_setup()
    _L1_gnn_in = {k: v for k, v in _L1_gnn_all.items() if k in ('basis', 'comp', 'root', 'bias', 'tp_w', 'tp_b', 'gamma', 'beta')}
    del _L1_gnn_all
    return {'x': x, 'src': src, 'dst': dst, 'edge_type_16': edge_type_16, 'edge_weight': edge_weight, 'edge_weight1': edge_weight1, 'L0_gnn_W1': _L0_gnn_in['W1'], 'L0_gnn_b1': _L0_gnn_in['b1'], 'L0_gnn_W2': _L0_gnn_in['W2'], 'L0_gnn_b2': _L0_gnn_in['b2'], 'L1_gnn_basis': _L1_gnn_in['basis'], 'L1_gnn_comp': _L1_gnn_in['comp'], 'L1_gnn_root': _L1_gnn_in['root'], 'L1_gnn_bias': _L1_gnn_in['bias'], 'L1_gnn_tp_w': _L1_gnn_in['tp_w'], 'L1_gnn_tp_b': _L1_gnn_in['tp_b'], 'L1_gnn_gamma': _L1_gnn_in['gamma'], 'L1_gnn_beta': _L1_gnn_in['beta']}

def reference(x, src, dst, edge_type_16, edge_weight, edge_weight1, L0_gnn_W1, L0_gnn_b1, L0_gnn_W2, L0_gnn_b2, L1_gnn_basis, L1_gnn_comp, L1_gnn_root, L1_gnn_bias, L1_gnn_tp_w, L1_gnn_tp_b, L1_gnn_gamma, L1_gnn_beta):
    import jax
    import jax.numpy as jnp

    def _L0_gnn_ref(feat, eweight, W1, b1, W2, b2, src, dst):
        import jax, jax.numpy as jnp
        import numpy as np
        N_NODES = 2048
        N_EDGES = 32768
        IN_F = 128
        HID_F = 128
        OUT_F = 128

        def _degrees(src, dst, n_nodes):
            ones = jnp.ones(src.shape[0], dtype=jnp.float32)
            deg_out = jax.ops.segment_sum(ones, src, num_segments=n_nodes)
            deg_in = jax.ops.segment_sum(ones, dst, num_segments=n_nodes)
            return (jnp.clip(deg_out, 1.0, None), jnp.clip(deg_in, 1.0, None))

        def _graph_conv(feat, W, b, src, dst, out_norm, in_norm, n_nodes):
            h = feat * out_norm[:, None]
            h = h @ W
            agg = jax.ops.segment_sum(h[src], dst, num_segments=n_nodes)
            return agg * in_norm[:, None] + b
        n = feat.shape[0]
        deg_out, deg_in = _degrees(src, dst, n)
        out_norm = jax.lax.rsqrt(deg_out)
        in_norm = jax.lax.rsqrt(deg_in)
        h = _graph_conv(feat, W1, b1, src, dst, out_norm, in_norm, n)
        h = jax.nn.relu(h)
        h = _graph_conv(h, W2, b2, src, dst, out_norm, in_norm, n)
        msg = h[src] * eweight
        return jax.ops.segment_sum(msg, dst, num_segments=n)

    def _L1_gnn_ref(x, edge_index, edge_type, edge_time, basis, comp, root, bias, tp_w, tp_b, gamma, beta):
        import jax, jax.numpy as jnp
        import numpy as np
        N, D, R, NB, E = (50000, 128, 16, 10, 50000)
        DECAY_RATE = 0.1
        LN_EPS = 1e-05
        n, d = x.shape
        r = comp.shape[0]
        src, dst = (edge_index[0], edge_index[1])
        W = jnp.einsum('rb,bio->rio', comp, basis)
        msg = x[src]
        seg = dst * r + edge_type
        agg = jax.ops.segment_sum(msg, seg, num_segments=n * r)
        cnt = jax.ops.segment_sum(jnp.ones_like(seg, dtype=x.dtype), seg, num_segments=n * r)
        agg = (agg / jnp.maximum(cnt, 1.0)[:, None]).reshape(n, r, d)
        x_rgcn = jnp.einsum('nrd,rdo->no', agg, W) + x @ root + bias
        td = edge_time.max() - edge_time
        td = td / (td.max() + 1e-08)
        w = jnp.exp(-DECAY_RATE * td)
        w = w / (w.sum() + 1e-08)
        agg_t = jax.ops.segment_sum(msg * w[:, None], dst, num_segments=n)
        deg = jax.ops.segment_sum(jnp.ones_like(dst, dtype=x.dtype), dst, num_segments=n)
        x_time = agg_t / jnp.clip(deg, 1.0)[:, None]
        xc = x_rgcn + x_time @ tp_w + tp_b
        h = jax.nn.relu(xc)
        mu = h.mean(-1, keepdims=True)
        var = ((h - mu) ** 2).mean(-1, keepdims=True)
        return (h - mu) * jax.lax.rsqrt(var + LN_EPS) * gamma + beta
    edge_index = jnp.stack([src, dst])
    h = jnp.maximum(_layernorm(x, axis=-1), 0.0)
    x = x + _L0_gnn_ref(h, edge_weight1, L0_gnn_W1, L0_gnn_b1, L0_gnn_W2, L0_gnn_b2, src, dst)
    h = jnp.maximum(_layernorm(x, axis=-1), 0.0)
    x = x + _L1_gnn_ref(h, edge_index, edge_type_16, edge_weight, L1_gnn_basis, L1_gnn_comp, L1_gnn_root, L1_gnn_bias, L1_gnn_tp_w, L1_gnn_tp_b, L1_gnn_gamma, L1_gnn_beta)
    return x

_drawn_inputs = setup_inputs


def setup_inputs(seed=0):
    import zlib

    import numpy as np

    out = dict(_drawn_inputs(seed))
    spreads = {'L0_gnn_b1': (0.0, 0.1),
     'L0_gnn_b2': (0.0, 0.1),
     'L1_gnn_bias': (0.0, 0.713),
     'L1_gnn_tp_b': (0.0, 0.683),
     'L1_gnn_gamma': (1.0, 0.2),
     'L1_gnn_beta': (0.0, 0.346)}
    factors = {'edge_weight': 8.0, 'L1_gnn_tp_w': 8.0}
    for name, (base, spread) in spreads.items():
        noise = np.random.default_rng([zlib.crc32(name.encode()), seed]).standard_normal(out[name].shape)
        drawn = base * np.exp(spread * noise) if base else spread * noise
        out[name] = jnp.asarray(drawn.astype(out[name].dtype))
    for name, factor in factors.items():
        out[name] = (out[name] * factor).astype(out[name].dtype)
    return out
```

```python
from contextlib import ExitStack

import concourse.bass as bass
from concourse import mybir

F32 = mybir.dt.float32
BF16 = mybir.dt.bfloat16
I32 = mybir.dt.int32
I16 = mybir.dt.int16
ALU = mybir.AluOpType
ACT = mybir.ActivationFunctionType
AX_X = mybir.AxisListType.X
RMAX = bass.bass_isa.ReduceOp.max
RADD = bass.bass_isa.ReduceOp.add
ds = bass.ds

P = 128
LN_EPS = 1e-5
TINY = 1e-8
DECAY = 0.1


class Chain:

    def __init__(self, eng, sem):
        self.eng, self.sem, self.n = eng, sem, 0

    def step(self, ins):
        self.n += 1
        ins.then_inc(self.sem, 1)

    def here(self):
        self.eng.wait_ge(self.sem, self.n)


def gnn_kernel(nc, x, src, dst, etype, eweight, eweight1, W1, b1, W2, b2, basis, comp, root, bias, tp_w, tp_b,
               gamma, beta, out):
    N, F = x.shape
    E = src.shape[0]
    NB = basis.shape[0]
    R = comp.shape[0]
    NT = (N + P - 1) // P
    NPAD = NT * P
    NLAST = N - (NT - 1) * P
    EP = 125
    EC = E // EP
    assert EP * EC == E and F == P

    WD = 5
    WC = WD * NT
    NW = NPAD // WD
    HALF = 2
    CAP = HALF * P
    WT = NW // P
    SLOTS = NW * HALF
    BW = 4
    BS = BW * HALF
    NBATCH = NW // BW
    NG = 8
    GB = NBATCH // NG
    GD = NPAD // NG
    GROUP = GB * BW * WC
    HB = 2 * BS
    ORDER = (tuple(range(NG)), (4, 5, 6, 7, 0, 1, 2, 3), tuple(range(NG)))

    RD = 16
    RC = R * RD
    RW = NPAD // RD
    RJ = 5
    RCAP = RJ * P
    RT = 2
    RP = RW // RT
    RSLOTS = RW * RJ
    BLW = P // RD
    BLC = BLW * RJ
    RING = 20
    QU = 10
    FS = R + 9

    HCOL = 33
    HSTEPS = EC // HCOL

    start_dram = nc.dram_tensor("start_scratch", (NPAD,), F32, kind="Internal").ap()
    spill_dram = nc.dram_tensor("spill_scratch", (4, P, GROUP), BF16, kind="Internal").ap()
    table_dram = nc.dram_tensor("table_scratch", (NPAD, F), F32, kind="Internal").ap()
    y_dram = nc.dram_tensor("y_scratch", (NPAD, R * F), F32, kind="Internal").ap()
    inv_dram = nc.dram_tensor("inv_scratch", (R * NPAD,), F32, kind="Internal").ap()
    table3 = nc.dram_tensor("table3_scratch", (NPAD, 3 * F), BF16, kind="Internal").ap()

    def col(v):
        return v.rearrange("(e o) -> e o", o=1)

    src_col, dst_col, type_col, ew_col = col(src), col(dst), col(etype), col(eweight)

    with ExitStack() as ctx:
        def sb(name, shape, dt=F32):
            return ctx.enter_context(nc.sbuf_tensor(name, shape, dt))[tuple(slice(None) for _ in shape)]

        def sem(name):
            return ctx.enter_context(nc.semaphore("s_" + name))

        xN = sb("xN", [P, NT, F])
        H = sb("H", [P, NT, F])
        aggT = sb("aggT", [P, NPAD])
        H3 = sb("H3", [P, NT, 3 * F], BF16)
        loB, keyB = sb("loB", [P, SLOTS], BF16), sb("keyB", [P, SLOTS], BF16)
        ew1C = sb("ew1C", [P, SLOTS])
        colR = sb("colR", [P, RSLOTS, 3])
        srcC = sb("srcC", [P, RSLOTS], I32)
        W1s, W2s, roots, tpws = (sb(n, [P, F]) for n in ("W1s", "W2s", "roots", "tpws"))
        b1b, b2b, biasb, tpbb, gammab, betab = (sb(n, [P, F]) for n in ("b1b", "b2b", "biasb", "tpbb", "gammab", "betab"))
        Wr = sb("Wr", [P, R, F])
        ident = sb("ident", [P, P])
        onesf = sb("onesf", [P, P])
        onesb = sb("onesb", [P, P], BF16)
        upper = sb("upper", [P, P])
        iota_f = sb("iota_f", [P, P])
        iota_16 = sb("iota_16", [P, P, HB], BF16)
        nowA = sb("nowA", [P, 4 * BS, 3])
        iota_h = sb("iota_h", [P, RC], I16)
        degin, invdeg, innorm, onorm = (sb(n, [P, NT]) for n in ("degin", "invdeg", "innorm", "onorm"))
        lnscale, lnbias, sc1, sc2, sc3 = (sb(n, [P, NT]) for n in ("lnscale", "lnbias", "sc1", "sc2", "sc3"))
        stats = sb("stats", [P, NT, 6])
        aggr = sb("aggr", [P, NT, 2])
        st5, st16 = sb("st5", [P, WT]), sb("st16", [P, RT])
        ix5, ix16 = sb("ix5", [P, WT], I32), sb("ix16", [P, RT], I32)
        base5, base16 = sb("base5", [P, WT]), sb("base16", [P, RT])
        ibase = sb("ibase", [P, WT + RT], I32)
        compb = sb("compb", [P, R * NB])
        tw = sb("tw", [P, 12])
        matched = sb("matched", [P, 4])
        flag = sb("flag", [1, 1], I32)
        startT = sb("startT", [NT, P])
        rowstat = sb("rowstat", [P, 6])
        rowaggr = sb("rowaggr", [P, 2])
        rowsc = sb("rowsc", [P, 3])

        ARENA = 83 * 1024 // 4
        arena = sb("arena", [P, ARENA])
        at = [0]

        def carve(shape, dt=F32, reset=False):
            if reset:
                at[0] = 0
            n = 1
            for s in shape[1:]:
                n *= s
            w = n if dt in (F32, I32) else (n + 1) // 2
            v = arena[0:shape[0], at[0]:at[0] + w]
            at[0] += w
            assert at[0] <= ARENA, at[0]
            if dt is not F32:
                v = v.bitcast(dt)[:, 0:n]
            if len(shape) == 3:
                v = v.rearrange("p (a b) -> p a b", b=shape[2])
            elif len(shape) == 4:
                v = v.rearrange("p (a b c) -> p a b c", b=shape[2], c=shape[3])
            return v

        dst_rows = carve([EP, EC], I32, reset=True)
        src_rows = carve([EP, EC], I32)
        ew_rows = carve([EP, EC])
        tmp_rows = carve([EP, EC], I32)
        digits = carve([EP, 4, EC + 1], BF16)
        iota_rep = carve([EP, P, HCOL], BF16)
        ohlo = carve([EP, 4, P * HCOL], BF16)
        ohhi = carve([EP, 4, NT * HCOL + 1], BF16)
        iota_i = carve([P, RC], I32)
        ramp_i = carve([P, P], I32)
        basis_s = carve([P, NB, F])
        basis_from = at[0] - NB * F
        dst5 = carve([P, WT, CAP], I32, reset=True)
        src5 = carve([P, WT, CAP], I32)
        ew15 = carve([P, WT, CAP])
        key5 = carve([P, WT, CAP])
        tmp5 = carve([P, WT, CAP], I32)
        dst16 = carve([RP, RT, RCAP], I32)
        src16 = carve([RP, RT, RCAP], I32)
        typ16 = carve([RP, RT, RCAP], I32)
        ew16 = carve([RP, RT, RCAP])
        rel16 = carve([RP, RT, RCAP])
        seg16 = carve([RP, RT, RCAP])
        assert at[0] <= basis_from
        lo5 = tmp5.bitcast(F32)
        ok5 = dst5.bitcast(F32)
        ok16 = dst16.bitcast(F32)
        srf16 = typ16.bitcast(F32)
        AT = carve([P, 2, GROUP], reset=True)
        ATB = carve([P, 4, GROUP], BF16, reset=True)
        h2T = carve([P, NPAD], reset=True)
        h2T_end = at[0]
        ring = carve([P, RING, 3 * F], BF16)
        oh_seg = carve([P, 2, RJ, RC], BF16)
        oh_tim = carve([P, 2, 3 * RD * RJ], BF16)
        oh_rel = carve([P, 2, RD * RJ], BF16)
        iota_t = carve([P, RD * RJ], BF16)
        now = carve([P, BLC, 3])
        wpart = carve([P, 3, BLC], BF16)
        idxs = carve([P, BLC], I32)
        aggn = carve([P, R, P])
        cnt_row = carve([1, R, P])
        inv = carve([P, 2, R])
        timeT = carve([P, 3, P])
        h2Tt = carve([P, P])
        fin = carve([P, 5, F])
        outt = carve([P, F])

        at[0] = h2T_end
        g_src, g_dst, g_typ = (carve([EP, EC], I32) for _ in range(3))
        g_ew, g_ew1 = carve([EP, EC]), carve([EP, EC])
        g_yix, g_cix = carve([EP, EC], I32), carve([EP, EC], I32)
        g_dstf, g_typf = g_dst.bitcast(F32), g_typ.bitcast(F32)
        g_oh = carve([EP, NPAD])
        g_iota = carve([EP, NPAD])
        g_row = carve([EP, F])
        g_ix, g_cx = carve([EP, 1], I32), carve([EP, 1], I32)
        g_w = carve([EP, 1])
        g_toh = carve([EP, R])
        g_zero = carve([EP, P])
        g_tile = carve([P, P])
        g_y = carve([P, 4 * F])
        g_fin = carve([P, 5, F])
        g_out = carve([P, F])

        oh_words = sb("oh_words", [P, 2 * BS * (P + WC)])
        oh_lo = oh_words[:, 0:2 * BS * P].rearrange("p (a b c) -> p a b c", a=2, b=BS)
        oh_dh = oh_words[:, 2 * BS * P:].rearrange("p (a b c) -> p a b c", a=2, b=BS)
        oh_half = oh_words.bitcast(BF16)
        oh_lo_b = oh_half[:, 0:2 * HB * P].rearrange("p (a j c) -> p a j c", a=2, c=HB)
        oh_dh_b = oh_half[:, 2 * HB * P:].rearrange("p (a j c) -> p a j c", a=2, c=HB)

        bank = [ctx.enter_context(nc.psum_tensor(f"bank{i}", [P, 512], F32))[:, :] for i in range(8)]

        s_rows, s_x, s_w, s_basis = sem("rows"), sem("x"), sem("w"), sem("basis")
        s_pad, s_iota, s_const, s_wr, s_poolch = sem("pad"), sem("iota"), sem("const"), sem("wr"), sem("poolch")
        s_hoh, s_hmm, s_deg, s_cum, s_cumps, s_start, s_startT = (
            sem(n) for n in ("hoh", "hmm", "deg", "cum", "cumps", "start", "startT"))
        s_sout, s_sin, s_ix, s_slots = sem("sout"), sem("sin"), sem("ix"), sem("slots")
        s_dve = sem("dve")
        s_twmax, s_twred, s_twsum, s_twred2 = sem("twmax"), sem("twred"), sem("twsum"), sem("twred2")
        s_sqd, s_sqr, s_lnv, s_lns, s_lnr, s_h = (sem(n) for n in ("sqd", "sqr", "lnv", "lns", "lnr", "h"))
        s_wexp, s_win, s_tps, s_tpf, s_cols, s_wparts = (sem(n) for n in ("wexp", "win", "tps", "tpf", "cols", "wparts"))
        s_oh, s_built, s_evac, s_applied, s_agg = (sem(n) for n in ("oh", "built", "evac", "applied", "agg"))
        s_pmm, s_pdv = sem("pmm"), sem("pdv")
        s_h3, s_table, s_htp, s_htd = sem("h3"), sem("table"), sem("htp"), sem("htd")
        s_idx, s_ohr, s_used, s_wins, s_wind = (sem(n) for n in ("idx", "ohr", "used", "wins", "wind"))
        s_nowa, s_now, s_rel = sem("nowa"), sem("now"), sem("rel")
        s_gate, s_gate2, s_gate3 = sem("gate"), sem("gate2"), sem("gate3")
        s_timd, s_blk, s_fin, s_var, s_rt, s_res, s_out = (
            sem(n) for n in ("timd", "blk", "fin", "var", "rt", "res", "out"))
        landed = [sem(f"landed{i}") for i in range(RING)]
        spilled = [sem(f"spilled{i}") for i in range(4)]
        reloaded = [sem(f"reloaded{i}") for i in range(4)]
        s_match, s_matchps, s_flag = sem("match"), sem("matchps"), sem("flag")
        g_rows, g_ready, g_tab, g_init = sem("g_rows"), sem("g_ready"), sem("g_tab"), sem("g_init")
        g_landed = sem("g_landed_first"), sem("g_landed_second")
        g_wland, g_ixr, g_ohr, g_mm, g_sum = (
            sem(n) for n in ("g_wland", "g_ixr", "g_ohr", "g_mm", "g_sum"))
        g_taken, g_inv, g_invd, g_tcopy, g_ymm, g_ycopy, g_yout = (
            sem(n) for n in ("g_taken", "g_inv", "g_invd", "g_tcopy", "g_ymm", "g_ycopy", "g_yout"))
        g_res2, g_dve = sem("g_res2"), sem("g_dve")
        g_trn, g_rel, g_blk, g_chain, g_var, g_rt, g_res, g_store = (
            sem(n) for n in ("g_trn", "g_rel", "g_blk", "g_chain", "g_var", "g_rt", "g_res", "g_store"))
        block = ctx.enter_context(nc.Block())

        GBANKS = [(i, min(512, NPAD - 512 * i)) for i in range((NPAD + 511) // 512)]

        def is_fast(eng):
            eng.wait_ge(s_flag, 1)
            return eng.value_load(flag[0:1, 0:1], min_val=0, max_val=1)

        @block.sync
        def _(sp):
            for t, d in ((dst_rows, dst), (src_rows, src), (ew_rows, eweight)):
                sp.dma_start(t, d.rearrange("(p c) -> p c", p=EP)).then_inc(s_rows, 16)
            sp.wait_ge(s_pad, 1)
            sp.dma_start(xN[:, 0:NT - 1, :], x[0:(NT - 1) * P, :].rearrange("(t p) f -> p t f", p=P)).then_inc(s_x, 16)
            sp.dma_start(xN[0:NLAST, NT - 1, :], x[(NT - 1) * P:N, :]).then_inc(s_x, 16)
            sp.dma_start(basis_s, basis.rearrange("b i o -> i b o")).then_inc(s_basis, 16)
            sp.dma_start(compb, comp.rearrange("r b -> (r b)").partition_broadcast(P)).then_inc(s_basis, 16)
            for t, d in ((W1s, W1), (W2s, W2), (roots, root), (tpws, tp_w)):
                sp.dma_start(t, d).then_inc(s_w, 16)
            for t, d in ((b1b, b1), (b2b, b2), (biasb, bias), (tpbb, tp_b), (gammab, gamma), (betab, beta)):
                sp.dma_start(t, d.partition_broadcast(P)).then_inc(s_w, 16)
            sp.wait_ge(s_startT, 1)
            sp.dma_start(start_dram.rearrange("(h l) -> h l", l=P), startT).then_inc(s_sout, 16)
            sp.wait_ge(s_sout, 16)
            for t in range(WT):
                sp.dma_start(st5[:, t:t + 1], start_dram[t * P * WD:(t + 1) * P * WD].rearrange(
                    "(p o) -> p o", o=WD)[:, 0:1], allow_slow_non_contiguous=True).then_inc(s_sin, 16)
            for t in range(RT):
                sp.dma_start(st16[0:RP, t:t + 1], start_dram[t * RP * RD:(t + 1) * RP * RD].rearrange(
                    "(p o) -> p o", o=RD)[:, 0:1], allow_slow_non_contiguous=True).then_inc(s_sin, 16)
            fast = is_fast(sp)
            with sp.If(fast == 1):
                for g in range(4):
                    sp.wait_ge(s_evac, (g + 1) * GB)
                    sp.dma_start(spill_dram[g], ATB[:, g, :]).then_inc(spilled[g], 16)
                for g in range(4):
                    sp.wait_ge(s_applied, 2 + NG + g + 1)
                    sp.dma_start(ATB[:, g, :], spill_dram[g]).then_inc(reloaded[g], 16)
                sp.wait_ge(s_h3, 3)
                sp.dma_start(table3.rearrange("(t p) f -> p t f", p=P), H3).then_inc(s_table, 16)
                sp.sem_inc(s_out, 16)
                with sp.Fori(0, NT - 1) as b:
                    sp.wait_ge(s_res, b + 1)
                    sp.dma_start(out[ds(b * P, P), :], outt).then_inc(s_out, 16)
                sp.wait_ge(s_res, NT)
                sp.dma_start(out[(NT - 1) * P:N, :], outt[0:NLAST, :]).then_inc(s_out, 16)
                sp.wait_ge(s_out, 16 + 16 * NT)
            with sp.Else():
                sp.wait_ge(s_cols, 1)
                for t, d in ((g_src, src), (g_dst, dst), (g_typ, etype), (g_ew, eweight),
                             (g_ew1, eweight1.rearrange("e o -> (e o)"))):
                    sp.dma_start(t, d.rearrange("(p c) -> p c", p=EP)).then_inc(g_rows, 16)
                nodes = table_dram.rearrange("(t p) f -> p t f", p=P)
                for q in range(4):
                    if q == 2:
                        sp.wait_ge(s_pdv, 2 * NT)
                    else:
                        sp.wait_ge(s_h, min(q, 2) + 1)
                    sp.dma_start(nodes, H).then_inc(g_tab, 16)
                sp.sem_inc(g_yout, 16)
                with sp.Fori(0, NT) as t:
                    for k in range(R // 4):
                        sp.wait_ge(g_ycopy, t * (R // 4) + (k + 3))
                        sp.dma_start(y_dram[ds(t * P, P), k * 4 * F:(k + 1) * 4 * F], g_y).then_inc(g_yout, 16)
                sp.wait_ge(g_inv, 1)
                sp.dma_start(inv_dram.rearrange("(r n) -> r n", r=R), aggT[0:R, :]).then_inc(g_invd, 16)
                sp.sem_inc(g_store, 16)
                with sp.Fori(0, NT - 1) as b:
                    sp.wait_ge(g_res, b + 2)
                    sp.dma_start(out[ds(b * P, P), :], g_out).then_inc(g_store, 16)
                sp.wait_ge(g_res, NT + 1)
                sp.dma_start(out[(NT - 1) * P:N, :], g_out[0:NLAST, :]).then_inc(g_store, 16)
                sp.wait_ge(g_store, 16 + 16 * NT)

        @block.gpsimd
        def _(pool):
            g = nc.gpsimd
            ch = Chain(pool, s_poolch)
            g.memset(xN[:, NT - 1, :], 0.0).then_inc(s_pad, 1)
            g.iota(iota_i, [[1, RC]], base=0, channel_multiplier=0).then_inc(s_iota, 1)
            g.iota(ramp_i, [[1, P]], base=0, channel_multiplier=-1).then_inc(s_iota, 1)
            g.iota(ibase[:, 0:WT], [[P * WD, WT]], base=0, channel_multiplier=WD).then_inc(s_iota, 1)
            g.iota(ibase[:, WT:WT + RT], [[RP * RD, RT]], base=0, channel_multiplier=RD).then_inc(s_iota, 1)
            pool.wait_ge(s_basis, 32)
            prod = aggT[:, 0:R * F].rearrange("p (r f) -> p r f", f=F)
            cb = compb.rearrange("p (r b) -> p r b", b=NB)
            for b in range(NB):
                first = basis_s[:, b, :].unsqueeze(1).to_broadcast([P, R, F])
                coef = cb[:, :, b:b + 1].to_broadcast([P, R, F])
                if b == 0:
                    ch.step(g.tensor_tensor(Wr, first, coef, ALU.mult))
                    ch.here()
                    continue
                ch.step(g.tensor_tensor(prod, first, coef, ALU.mult))
                ch.here()
                ch.step(g.tensor_tensor(Wr, Wr, prod, ALU.add))
                ch.here()
                if b == 4:
                    pool.wait_ge(s_twmax, 1)
                    g.partition_all_reduce(tw[0:EP, 2:4], tw[0:EP, 0:2], EP, RMAX).then_inc(s_twred, 1)
                if b == 6:
                    pool.wait_ge(s_twsum, 1)
                    g.partition_all_reduce(tw[0:EP, 8:9], tw[0:EP, 7:8], EP, RADD).then_inc(s_twred2, 1)
            pool.sem_inc(s_wr, 1)
            pool.wait_ge(s_ix, 1)
            ew1_col = eweight1
            for t in range(WT):
                for to, of in ((dst5, dst_col), (src5, src_col), (ew15, ew1_col)):
                    g.indirect_dma_start(to[:, t, :], None, of,
                                         bass.IndirectOffsetOnAxis(ap=ix5[:, t:t + 1], axis=0)).then_inc(s_slots, 16)
            for t in range(RT):
                for to, of in ((dst16, dst_col), (src16, src_col), (typ16, type_col), (ew16, ew_col)):
                    g.indirect_dma_start(to[:, t, :], None, of,
                                         bass.IndirectOffsetOnAxis(ap=ix16[0:RP, t:t + 1], axis=0)).then_inc(s_slots, 16)
            fast = is_fast(pool)
            with pool.If(fast == 1):
                pool.wait_ge(s_table, 16)
                with pool.Fori(0, NT) as b:
                    for n in range(BLC):
                        if n % QU == 0:
                            pool.wait_ge(s_idx, b * (BLC // QU) + (n // QU + 1))
                        if n % RJ == 0:
                            pool.wait_ge(s_used, b * BLC + (n + RJ))
                            pool.sem_inc(s_gate, 1)
                        g.indirect_dma_start(ring[:, n % RING, :], None, table3,
                                             bass.IndirectOffsetOnAxis(ap=idxs[:, n:n + 1], axis=0)
                                             ).then_inc(landed[n % RING], 16)
            with pool.Else():
                y_rows = y_dram.rearrange("n (r f) -> (n r) f", f=F)
                pool.wait_ge(s_cols, 1)
                g.iota(g_iota.bitcast(I32), [[1, NPAD]], base=0, channel_multiplier=0).then_inc(g_init, 1)
                for n, q in enumerate((0, 1, 2, 4, 5)):
                    if q < 4:
                        pool.wait_ge(g_tab, 16 * (q + 1))
                    elif q == 4:
                        pool.wait_ge(g_tab, 16 * 4)
                        pool.wait_ge(g_yout, 16 + 16 * NT * (R // 4))
                        pool.wait_ge(g_invd, 16)
                    with pool.Fori(0, EC) as c:
                        pool.wait_ge(g_ixr, c + (n * EC + 1))
                        pool.sem_inc(s_gate, 1)
                        if q == 4:
                            g.indirect_dma_start(g_w, None, col(inv_dram),
                                                 bass.IndirectOffsetOnAxis(ap=g_cx, axis=0)).then_inc(g_wland, 16)
                        g.indirect_dma_start(g_row, None, y_rows if q == 4 else table_dram,
                                             bass.IndirectOffsetOnAxis(ap=g_ix, axis=0)).then_inc(g_landed[q > 2], 16)

        @block.vector
        def _(dve):
            v = nc.vector
            ch, gch = Chain(dve, s_dve), Chain(dve, g_dve)
            v.memset(matched, 0.0)
            dve.wait_ge(s_iota, 4)
            v.tensor_copy(base5, ibase[:, 0:WT])
            v.tensor_copy(base16, ibase[:, WT:WT + RT])
            v.tensor_copy(iota_f, iota_i[:, 0:P])
            v.tensor_copy(iota_16, iota_i[:, 0:P].unsqueeze(2).to_broadcast([P, P, HB]))
            v.tensor_copy(iota_h, iota_i)
            v.memset(onesf, 1.0)
            v.memset(onesb, 1.0)
            v.memset(ohlo[:, 0, 0:P], 0.0)
            v.tensor_copy(iota_rep, iota_i[0:EP, 0:P].unsqueeze(2).to_broadcast([EP, P, HCOL]))
            v.tensor_scalar(ident, ramp_i, 0, None, ALU.is_equal)
            v.tensor_scalar(upper, ramp_i, 0, None, ALU.is_gt).then_inc(s_const, 1)
            dve.wait_ge(s_rows, 48)
            for a, rows in enumerate((dst_rows, src_rows)):
                ch.step(v.tensor_scalar(tmp_rows, rows, P - 1, None, ALU.bitwise_and))
                ch.here()
                ch.step(v.tensor_copy(digits[:, 2 * a, 0:EC], tmp_rows))
                ch.here()
                ch.step(v.tensor_scalar(tmp_rows, rows, 7, None, ALU.logical_shift_right))
                ch.here()
                ch.step(v.tensor_copy(digits[:, 2 * a + 1, 0:EC], tmp_rows))
                ch.here()
            v.tensor_reduce(tw[0:EP, 0:1], ew_rows, AX_X, ALU.max)
            ch.step(v.tensor_reduce(tw[0:EP, 1:2], ew_rows, AX_X, ALU.min))
            ch.here()
            v.tensor_scalar(tw[0:EP, 1:2], tw[0:EP, 1:2], -1.0, None, ALU.mult).then_inc(s_twmax, 1)

            def histogram_step(step, par):
                dve.wait_ge(s_hmm, step + 1)
                for a in range(2):
                    lo = digits[:, 2 * a, ds(step * HCOL, HCOL)]
                    hi = digits[:, 2 * a + 1, ds(step * HCOL, HCOL)]
                    v.tensor_tensor(ohlo[:, 2 * par + a, :].rearrange("p (j c) -> p j c", c=HCOL), iota_rep,
                                    lo.unsqueeze(1).to_broadcast([EP, P, HCOL]), ALU.is_equal)
                    last = v.tensor_tensor(ohhi[:, 2 * par + a, 0:NT * HCOL].rearrange("p (j c) -> p j c", c=HCOL),
                                           iota_rep[:, 0:NT, :], hi.unsqueeze(1).to_broadcast([EP, NT, HCOL]),
                                           ALU.is_equal)
                last.then_inc(s_hoh, 1)

            with dve.Fori(0, HSTEPS // 2) as i:
                for par in range(2):
                    histogram_step(i * 2 + par, par)
            histogram_step(HSTEPS - 1, 0)

            dve.wait_ge(s_twred, 1)
            ch.step(v.tensor_tensor(tw[0:EP, 4:5], tw[0:EP, 2:3], tw[0:EP, 3:4], ALU.add))
            ch.here()
            ch.step(v.tensor_scalar(tw[0:EP, 4:5], tw[0:EP, 4:5], TINY, None, ALU.add))
            ch.here()
            ch.step(v.reciprocal(tw[0:EP, 4:5], tw[0:EP, 4:5]))
            ch.here()
            ch.step(v.tensor_scalar(tw[0:EP, 5:6], tw[0:EP, 4:5], DECAY, None, ALU.mult))
            ch.here()
            v.scalar_tensor_tensor(tw[0:EP, 6:7], tw[0:EP, 5:6], -1.0, tw[0:EP, 2:3], ALU.mult,
                                   ALU.mult).then_inc(s_wexp, 1)

            dve.wait_ge(s_x, 32)
            for t in range(NT):
                last = v.bn_stats(stats[:, t, :], xN[:, t, :])
            ch.step(last)
            ch.here()
            for t in range(NT):
                last = v.bn_aggr(aggr[:, t, :], stats[:, t, :])
            ch.step(last)
            ch.here()
            v.tensor_scalar(sc1, aggr[:, :, 1], LN_EPS, None, ALU.add).then_inc(s_lnv, 1)

            dve.wait_ge(s_hmm, 2 + HSTEPS)
            v.tensor_copy(degin, bank[0][:, 0:NT]).then_inc(s_deg, 1)
            v.tensor_scalar(sc2, bank[0][:, 0:NT], 1.0, None, ALU.max)
            ch.step(v.tensor_scalar(sc3, bank[1][:, 0:NT], 1.0, None, ALU.max))
            ch.here()
            v.reciprocal(invdeg, sc2).then_inc(s_sqd, 1)
            dve.wait_ge(s_cumps, 1)
            ch.step(v.tensor_copy(innorm, bank[2][:, 64:64 + NT]))
            ch.here()
            ch.step(v.tensor_tensor_scan(onorm, onesf[:, 0:NT], innorm, 0.0, ALU.mult, ALU.add))
            ch.here()
            ch.step(v.tensor_tensor(onorm, onorm, innorm, ALU.subtract))
            ch.here()
            v.tensor_tensor(lnbias, onorm, bank[2][:, 0:NT], ALU.add).then_inc(s_start, 1)
            dve.wait_ge(s_cumps, 2)
            v.tensor_copy(startT, bank[3][0:NT, 0:P]).then_inc(s_startT, 1)
            dve.wait_ge(s_sqr, 1)
            v.reciprocal(innorm, sc2)
            dve.wait_ge(s_lns, 1)
            v.reciprocal(onorm, sc3)
            ch.step(v.reciprocal(sc1, sc1))
            ch.here()
            ch.step(v.tensor_tensor(lnscale, sc1, onorm, ALU.mult))
            ch.here()
            v.scalar_tensor_tensor(lnbias, aggr[:, :, 0], -1.0, lnscale, ALU.mult, ALU.mult).then_inc(s_lnr, 1)

            dve.wait_ge(s_sin, 16 * (WT + RT))
            v.tensor_scalar(ix5, st5, float(E - CAP), None, ALU.min)
            v.tensor_scalar(ix16[0:RP, :], st16[0:RP, :], float(E - RCAP), None, ALU.min).then_inc(s_ix, 1)

            dve.wait_ge(s_slots, 16 * (3 * WT + 4 * RT))
            for t in range(WT):
                last = v.tensor_scalar(key5[:, t, :], dst5[:, t, :], base5[:, t:t + 1], float(NT),
                                       ALU.subtract, ALU.mult)
            v.tensor_scalar(tmp5, src5, 7, None, ALU.logical_shift_right)
            for t in range(RT):
                v.tensor_scalar(rel16[:, t, :], dst16[:, t, :], base16[0:RP, t:t + 1], None, ALU.subtract)
            ch.step(v.tensor_scalar(src5, src5, P - 1, None, ALU.bitwise_and))
            ch.here()
            v.scalar_tensor_tensor(seg16, typ16, float(RD), rel16, ALU.mult, ALU.add)
            v.tensor_scalar(ok16, rel16, 0.0, None, ALU.is_ge)
            ch.step(v.tensor_tensor(key5, key5, tmp5, ALU.add))
            ch.here()
            v.scalar_tensor_tensor(ok16, rel16, float(RD), ok16, ALU.is_lt, ALU.mult)
            v.tensor_copy(srf16, src16)
            v.tensor_scalar(ok5, key5, 0.0, None, ALU.is_ge)
            ch.step(v.tensor_copy(lo5, src5))
            ch.here()
            v.scalar_tensor_tensor(ok5, key5, float(WC), ok5, ALU.is_lt, ALU.mult)
            ch.step(v.scalar_tensor_tensor(seg16, seg16, 1.0, ok16, ALU.add, ALU.mult))
            ch.here()
            v.scalar_tensor_tensor(key5, key5, 1.0, ok5, ALU.add, ALU.mult)
            v.tensor_reduce(matched[:, 0:1], ok5.rearrange("p t c -> p (t c)"), AX_X, ALU.add)
            v.tensor_reduce(matched[0:RP, 1:2], ok16.rearrange("p t c -> p (t c)"), AX_X, ALU.add).then_inc(s_match, 1)
            ch.step(v.tensor_scalar(seg16, seg16, -1.0, None, ALU.add))
            ch.here()
            ch.step(v.tensor_scalar(key5, key5, -1.0, None, ALU.add))
            ch.here()
            dve.wait_ge(s_twred2, 1)
            ch.step(v.tensor_scalar(tw[0:EP, 9:10], tw[0:EP, 8:9], TINY, None, ALU.add))
            ch.here()
            ch.step(v.reciprocal(tw[0:EP, 10:11], tw[0:EP, 9:10]))
            ch.here()
            dve.wait_ge(s_wexp, 2)
            v.tensor_scalar(ew16, ew16, tw[0:RP, 10:11], None, ALU.mult).then_inc(s_win, 1)
            dve.wait_ge(s_matchps, 1)
            ch.step(v.tensor_scalar(matched[0:1, 2:4], bank[3][0:1, 0:2], float(E), None, ALU.is_equal))
            ch.here()
            v.tensor_tensor(flag, matched[0:1, 2:3], matched[0:1, 3:4], ALU.mult).then_inc(s_flag, 1)
            fast = is_fast(dve)

            left = aggT.rearrange("p (t f) -> p t f", f=F)

            def split(t0, t1):
                w, r = H[:, t0:t1, :], left[:, t0:t1, :]
                ch.step(v.tensor_copy(H3[:, t0:t1, 0:F], w))
                ch.here()
                ch.step(v.tensor_tensor(r, w, H3[:, t0:t1, 0:F], ALU.subtract))
                ch.here()
                ch.step(v.tensor_copy(H3[:, t0:t1, F:2 * F], r))
                ch.here()
                ch.step(v.tensor_tensor(r, r, H3[:, t0:t1, F:2 * F], ALU.subtract))
                ch.here()
                return v.tensor_copy(H3[:, t0:t1, 2 * F:3 * F], r)

            def onehots_bf16(c0, half, n):
                dve.wait_ge(s_built, n)
                v.tensor_tensor(oh_lo_b[:, half], iota_16, loB[:, ds(c0, HB)].unsqueeze(1).to_broadcast([P, P, HB]),
                                ALU.is_equal)
                v.tensor_tensor(oh_dh_b[:, half], iota_16[:, 0:WC, :],
                                keyB[:, ds(c0, HB)].unsqueeze(1).to_broadcast([P, WC, HB]),
                                ALU.is_equal).then_inc(s_oh, 2)

            def onehots_f32(b, k):
                dve.wait_ge(s_built, b * 4 + (NBATCH + 4 + k - 1))
                for s in range(BS):
                    c = k * BS + s
                    v.tensor_scalar(oh_lo[:, k % 2, s, :], iota_f, nowA[:, c, 0:1], None, ALU.is_equal)
                    last = v.tensor_scalar(oh_dh[:, k % 2, s, :], iota_f[:, 0:WC], nowA[:, c, 1:2],
                                           nowA[:, c, 2:3], ALU.is_equal, ALU.mult)
                last.then_inc(s_oh, 1)

            dve.wait_ge(s_cols, 1)
            dve.wait_ge(s_h, 1)
            dve.wait_ge(s_wr, 1)
            split(0, NT).then_inc(s_h3, 1)

            def general_onehots(n, q):
                with dve.Fori(0, EC) as c:
                    dve.wait_ge(g_mm, c + (n * EC + 1))
                    if q == 4:
                        v.tensor_copy(g_cx, g_cix[:, ds(c, 1)])
                    if q != 3:
                        v.tensor_copy(g_ix, (g_yix if q == 4 else g_src)[:, ds(c, 1)]).then_inc(
                            g_ixr, 1)
                    else:
                        v.tensor_scalar(g_toh, iota_f[0:EP, 0:R], g_typf[:, ds(c, 1)], None, ALU.is_equal)
                    here = g_dstf[:, ds(c, 1)]
                    if q in (0, 1, 3):
                        last = v.tensor_scalar(g_oh, g_iota, here, None, ALU.is_equal)
                    elif q == 4:
                        dve.wait_ge(g_wland, c * 16 + 16)
                        last = v.tensor_scalar(g_oh, g_iota, here, g_w, ALU.is_equal, ALU.mult)
                    else:
                        weight = (g_ew1 if q == 2 else g_ew)[:, ds(c, 1)]
                        last = v.tensor_scalar(g_oh, g_iota, here, weight, ALU.is_equal, ALU.mult)
                    last.then_inc(g_ohr, 1)

            def general_start():
                dve.wait_ge(g_rows, 80)
                dve.wait_ge(g_init, 1)
                v.memset(g_zero, 0.0)
                v.scalar_tensor_tensor(g_yix, g_src, float(R), g_typ, ALU.mult, ALU.add)
                gch.step(v.scalar_tensor_tensor(g_cix, g_typ, float(NPAD), g_dst, ALU.mult, ALU.add))
                gch.here()
                v.tensor_copy(g_iota, g_iota.bitcast(I32))
                v.tensor_copy(g_dstf, g_dst)
                gch.step(v.tensor_copy(g_typf, g_typ))
                gch.here()
                dve.wait_ge(g_ready, 1)
                v.tensor_scalar(g_ew, g_ew, tw[0:EP, 10:11], None, ALU.mult).then_inc(g_ready, 1)

            def fast_onehots():
                with dve.Fori(0, NBATCH // 4) as b:
                    for k in range(2):
                        onehots_bf16(b * (2 * HB) + k * HB, k, b * 4 + (2 * k + 2))

            def fast_weighted_onehots():
                dve.wait_ge(s_built, NBATCH + 4)
                with dve.Fori(0, NBATCH // 4) as b:
                    dve.wait_ge(s_oh, b * 4 + NBATCH)
                    for f, of in enumerate((loB, keyB, ew1C)):
                        last = v.tensor_copy(nowA[:, :, f], of[:, ds(b * (4 * BS), 4 * BS)])
                    last.then_inc(s_nowa, 1)
                    dve.wait_ge(s_nowa, b + 1)
                    for k in range(4):
                        onehots_f32(b, k)

            for q in range(3):
                with dve.If(fast == 1):
                    if q == 0:
                        fast_onehots()
                    if q == 1:
                        dve.wait_ge(s_h3, 2)
                    if q == 2:
                        fast_weighted_onehots()
                with dve.Else():
                    if q == 0:
                        general_start()
                    general_onehots(q, q)
                for t in range(NT):
                    dve.wait_ge(s_pmm, q * NT + t + 1)
                    ps = bank[6 + t % 2][:, 0:F]
                    if q < 2:
                        v.scalar_tensor_tensor(H[:, t, :], ps, innorm[:, t:t + 1], (b1b, b2b)[q],
                                               ALU.mult, ALU.add).then_inc(s_pdv, 1)
                    else:
                        v.tensor_tensor(xN[:, t, :], xN[:, t, :], ps, ALU.add).then_inc(s_pdv, 1)
                if q == 0:
                    dve.wait_ge(s_h, 2)
                    split(0, NT).then_inc(s_h3, 1)

            dve.wait_ge(s_pdv, 3 * NT)
            for t in range(NT):
                last = v.bn_stats(stats[:, t, :], xN[:, t, :])
            ch.step(last)
            ch.here()
            for t in range(NT):
                last = v.bn_aggr(aggr[:, t, :], stats[:, t, :])
            ch.step(last)
            ch.here()
            v.tensor_scalar(sc1, aggr[:, :, 1], LN_EPS, None, ALU.add).then_inc(s_lnv, 1)
            dve.wait_ge(s_lns, 2)
            ch.step(v.reciprocal(lnscale, sc1))
            ch.here()
            v.scalar_tensor_tensor(lnbias, aggr[:, :, 0], -1.0, lnscale, ALU.mult, ALU.mult).then_inc(s_lnr, 1)
            dve.wait_ge(s_h, 3)
            split(0, NT).then_inc(s_h3, 1)
            v.tensor_tensor(biasb, biasb, tpbb, ALU.add).then_inc(s_wparts, 1)

            with dve.If(fast == 1):
                dve.wait_ge(s_table, 16)
                v.tensor_copy(iota_t.rearrange("p (d j) -> p d j", j=RJ), iota_16[:, 0:RD, 0:RJ]).then_inc(s_wparts, 1)
                dve.wait_ge(s_wparts, 2)

                def block_columns(b):
                    dve.wait_ge(s_ohr, b * BLW)
                    v.tensor_copy(now, colR[:, ds(b * BLC, BLC), :]).then_inc(s_now, 1)
                    dve.wait_ge(s_now, b * 5 + 1)
                    rest = now[:, :, 2]
                    for k in range(2):
                        v.tensor_copy(wpart[:, k, :], rest).then_inc(s_now, 1)
                        dve.wait_ge(s_now, b * 5 + (2 * k + 2))
                        v.tensor_tensor(rest, rest, wpart[:, k, :], ALU.subtract).then_inc(s_now, 1)
                        dve.wait_ge(s_now, b * 5 + (2 * k + 3))
                    v.tensor_copy(wpart[:, 2, :], rest)

                def window(b, wv):
                    dve.wait_ge(s_used, b * BLC + (RING + RJ * (wv - 1)))
                    n = wv * RJ
                    rel = now[:, n:n + RJ, 1].unsqueeze(1).to_broadcast([P, RD, RJ])
                    v.tensor_tensor(oh_rel[:, wv % 2, :].rearrange("p (d j) -> p d j", j=RJ), iota_t.rearrange("p (d j) -> p d j", j=RJ),
                                    rel, ALU.is_equal).then_inc(s_rel, 1)
                    for j in range(RJ):
                        v.tensor_scalar(oh_seg[:, wv % 2, j, :], iota_h, now[:, n + j, 0:1], None, ALU.is_equal)
                    dve.wait_ge(s_rel, b * BLW + (wv + 1))
                    for k in range(3):
                        last = v.tensor_tensor(
                            oh_tim[:, wv % 2, k * RD * RJ:(k + 1) * RD * RJ].rearrange("p (d j) -> p d j", j=RJ),
                            oh_rel[:, wv % 2, :].rearrange("p (d j) -> p d j", j=RJ),
                            wpart[:, k, n:n + RJ].unsqueeze(1).to_broadcast([P, RD, RJ]), ALU.mult)
                    last.then_inc(s_ohr, 1)

                def result(b):
                    def there(k):
                        dve.wait_ge(s_fin, b * FS + (FS + k))
                        return k
                    dve.wait_ge(s_blk, b + 1)
                    mixed = bank[3]
                    v.scalar_tensor_tensor(fin[:, 0, :], mixed[:, F:2 * F], invdeg[:, ds(b, 1)], biasb, ALU.mult, ALU.add)
                    v.tensor_scalar(inv[:, 0, :], mixed[:, 2 * F:2 * F + R], 1.0, None, ALU.max).then_inc(s_fin, 1)
                    there(1)
                    v.tensor_tensor(fin[:, 1, :], mixed[:, 0:F], fin[:, 0, :], ALU.add)
                    v.reciprocal(inv[:, 1, :], inv[:, 0, :]).then_inc(s_fin, 1)
                    for r in range(R):
                        there(2 + r)
                        v.scalar_tensor_tensor(fin[:, r % 2, :], bank[4 + r // 4][:, (r % 4) * F:(r % 4 + 1) * F],
                                               inv[:, 1, r:r + 1], fin[:, (r + 1) % 2, :], ALU.mult,
                                               ALU.add).then_inc(s_fin, 1)
                    k = there(2 + R)
                    v.tensor_scalar(fin[:, 2, :], fin[:, (R - 1) % 2, :], 0.0, None, ALU.max).then_inc(s_fin, 1)
                    there(k + 1)
                    v.bn_stats(rowstat, fin[:, 2, :]).then_inc(s_fin, 1)
                    there(k + 2)
                    dve.sem_inc(s_gate2, 1)
                    v.bn_aggr(rowaggr, rowstat).then_inc(s_fin, 1)
                    there(k + 3)
                    v.tensor_scalar(rowsc[:, 0:1], rowaggr[:, 1:2], LN_EPS, None, ALU.add).then_inc(s_var, 1)
                    dve.wait_ge(s_rt, b + 1)
                    v.reciprocal(rowsc[:, 2:3], rowsc[:, 1:2]).then_inc(s_fin, 1)
                    there(k + 4)
                    v.tensor_scalar(fin[:, 3, :], fin[:, 2, :], rowaggr[:, 0:1], rowsc[:, 2:3], ALU.subtract,
                                    ALU.mult).then_inc(s_fin, 1)
                    there(k + 5)
                    v.tensor_tensor(fin[:, 4, :], fin[:, 3, :], gammab, ALU.mult).then_inc(s_fin, 1)
                    there(k + 6)
                    v.tensor_tensor(fin[:, 3, :], fin[:, 4, :], betab, ALU.add).then_inc(s_fin, 1)
                    assert there(k + 7) == FS

                def store(b):
                    dve.wait_ge(s_out, b * 16 + 16)
                    v.tensor_tensor(outt, fin[:, 3, :], xN[:, ds(b, 1), :].rearrange("p o f -> p (o f)"),
                                    ALU.add).then_inc(s_res, 1)

                dve.sem_inc(s_fin, FS)
                block_columns(0)
                for wv in range(BLW):
                    window(0, wv)
                with dve.Fori(1, NT) as b:
                    block_columns(b)
                    for wv in range(BLW):
                        window(b, wv)
                        if wv == 2:
                            result(b - 1)
                            store(b - 1)
                result(NT - 1)
                store(NT - 1)
            with dve.Else():
                GS = 9
                general_onehots(3, 3)
                dve.wait_ge(g_taken, 1)
                gch.step(v.tensor_scalar(aggT[0:R, :], aggT[0:R, :], 1.0, None, ALU.max))
                gch.here()
                v.reciprocal(aggT[0:R, :], aggT[0:R, :]).then_inc(g_inv, 1)
                general_onehots(4, 4)
                dve.wait_ge(g_tab, 64)
                for t in range(NT):
                    dve.wait_ge(g_trn, t + 1)
                    v.tensor_copy(H[:, t, :], bank[7][:, 0:F]).then_inc(g_rel, 1)
                general_onehots(5, 5)
                dve.sem_inc(g_res, 1)
                with dve.Fori(0, NT) as t:
                    def there(k):
                        dve.wait_ge(g_chain, t * GS + k)
                    dve.wait_ge(g_res, t + 1)
                    dve.wait_ge(g_blk, t + 1)
                    v.scalar_tensor_tensor(g_fin[:, 0, :], bank[7][:, F:2 * F], invdeg[:, ds(t, 1)], biasb, ALU.mult,
                                           ALU.add).then_inc(g_chain, 1)
                    there(1)
                    v.tensor_tensor(g_fin[:, 1, :], bank[7][:, 0:F], g_fin[:, 0, :], ALU.add).then_inc(g_chain, 1)
                    there(2)
                    v.tensor_tensor(g_fin[:, 2, :], g_fin[:, 1, :], H[:, ds(t, 1), :].rearrange("p o f -> p (o f)"),
                                    ALU.add).then_inc(g_chain, 1)
                    there(3)
                    v.tensor_scalar(g_fin[:, 3, :], g_fin[:, 2, :], 0.0, None, ALU.max).then_inc(g_chain, 1)
                    there(4)
                    v.bn_stats(rowstat, g_fin[:, 3, :]).then_inc(g_chain, 1)
                    there(5)
                    dve.sem_inc(s_gate2, 1)
                    v.bn_aggr(rowaggr, rowstat).then_inc(g_chain, 1)
                    there(6)
                    v.tensor_scalar(rowsc[:, 0:1], rowaggr[:, 1:2], LN_EPS, None, ALU.add).then_inc(g_var, 1)
                    dve.wait_ge(g_rt, t + 1)
                    v.reciprocal(rowsc[:, 2:3], rowsc[:, 1:2]).then_inc(g_chain, 1)
                    there(7)
                    v.tensor_scalar(g_fin[:, 4, :], g_fin[:, 3, :], rowaggr[:, 0:1], rowsc[:, 2:3], ALU.subtract,
                                    ALU.mult).then_inc(g_chain, 1)
                    there(8)
                    v.tensor_tensor(g_fin[:, 4, :], g_fin[:, 4, :], gammab, ALU.mult).then_inc(g_chain, 1)
                    there(9)
                    v.tensor_tensor(g_fin[:, 0, :], g_fin[:, 4, :], betab, ALU.add).then_inc(g_res2, 1)
                    dve.wait_ge(g_res2, t + 1)
                    dve.wait_ge(g_store, t * 16 + 16)
                    v.tensor_tensor(g_out, g_fin[:, 0, :], xN[:, ds(t, 1), :].rearrange("p o f -> p (o f)"),
                                    ALU.add).then_inc(g_res, 1)

        @block.scalar
        def _(act):
            a = nc.scalar
            act.wait_ge(s_wexp, 1)
            a.activation(tmp_rows.bitcast(F32), ew_rows, ACT.Exp, bias=tw[0:EP, 6:7], scale=tw[0:EP, 5:6],
                         accum_out=tw[0:EP, 7:8]).then_inc(s_twsum, 1)
            act.wait_ge(s_lnv, 1)
            act.wait_ge(s_sqd, 1)
            a.activation(sc2, sc2, ACT.Sqrt).then_inc(s_sqr, 1)
            a.activation(sc3, sc3, ACT.Sqrt)
            a.activation(sc1, sc1, ACT.Sqrt).then_inc(s_lns, 1)
            act.wait_ge(s_lnr, 1)
            for t in range(NT):
                last = a.activation(H[:, t, :], xN[:, t, :], ACT.Relu, bias=lnbias[:, t:t + 1],
                                    scale=lnscale[:, t:t + 1])
            last.then_inc(s_h, 1)
            act.wait_ge(s_slots, 16 * (3 * WT + 4 * RT))
            a.activation(ew16, ew16, ACT.Exp, bias=tw[0:RP, 6:7], scale=tw[0:RP, 5:6]).then_inc(s_wexp, 1)
            u = 0
            for to in (keyB, loB, ew1C):
                for t in range(WT):
                    act.wait_ge(s_tps, u + 1)
                    a.copy(to[:, t * CAP:(t + 1) * CAP].rearrange("p (w h) -> p h w", h=HALF),
                           bank[4 + u % 4][:, 0:CAP].rearrange("p (h w) -> p h w", h=HALF)).then_inc(s_tpf, 1)
                    u += 1
            for to in (colR[:, :, 0], colR[:, :, 1], colR[:, :, 2], srcC):
                for t in range(RT):
                    act.wait_ge(s_tps, u + 1)
                    a.copy(to[:, t * RP * RJ:(t + 1) * RP * RJ].rearrange("p (w j) -> p j w", j=RJ),
                           bank[4 + u % 4][:, 0:RP * RJ].rearrange("p (j w) -> p j w", j=RJ)).then_inc(s_tpf, 1)
                    u += 1
            act.wait_ge(s_tpf, 4 + u)
            act.sem_inc(s_cols, 1)
            act.wait_ge(s_wr, 1)
            fast = is_fast(act)

            def take(q, g, j):
                for k in range(4):
                    m = (min(q, 1) * NG + g) * GB + 4 * j + k
                    act.wait_ge(s_built, m + 5)
                    if j == 0 and k == 0 and q == 0 and g >= 4:
                        act.wait_ge(s_applied, 2 + g - 3)
                        act.wait_ge(spilled[g - 4], 16)
                    if j == 0 and k == 0 and q == 2:
                        act.wait_ge(s_applied, 2 * NG + max(g - 1, 0) + 2)
                    to = ATB[:, g % 4, :] if q == 0 else AT[:, g % 2, :]
                    a.copy(to[:, (4 * j + k) * BW * WC:(4 * j + k + 1) * BW * WC],
                           bank[k][:, 0:BW * WC]).then_inc(s_evac, 1)

            def take_agg(q, n):
                g = ORDER[q][n]
                act.wait_ge(s_applied, q * NG + n + 3)
                if q == 0 and n == 0:
                    act.wait_ge(s_h3, 1)
                if q == 1 and n == 0:
                    act.wait_ge(s_h3, 2)
                a.copy(aggT[:, g * GD:(g + 1) * GD], bank[4 + n % 2][:, 0:GD]).then_inc(s_agg, 1)

            def general_take(n, q):
                act.wait_ge(g_sum, n + 1)
                if q < 2:
                    act.wait_ge(s_h3, q + 1)
                rows = R if q == 3 else P
                for i, w in GBANKS:
                    last = a.copy(aggT[0:rows, 512 * i:512 * i + w], bank[i][0:rows, 0:w])
                return last

            for q in range(3):
                with act.If(fast == 1):
                    for g in range(NG):
                        if q != 1:
                            for j in range(GB // 4):
                                take(q, g, j)
                        if g > 0:
                            take_agg(q, g - 1)
                    take_agg(q, NG - 1)
                with act.Else():
                    if q == 0:
                        act.wait_ge(g_rows, 80)
                        a.activation(g_ew, g_ew, ACT.Exp, bias=tw[0:EP, 6:7], scale=tw[0:EP, 5:6]).then_inc(g_ready, 1)
                    general_take(q, q).then_inc(s_agg, NG)
                if q == 0:
                    for t in range(NT):
                        act.wait_ge(s_pdv, t + 1)
                        last = a.activation(H[:, t, :], H[:, t, :], ACT.Relu, scale=onorm[:, t:t + 1])
                    last.then_inc(s_h, 1)
            act.wait_ge(s_lnv, 2)
            a.activation(sc1, sc1, ACT.Sqrt).then_inc(s_lns, 1)
            act.wait_ge(s_lnr, 2)
            for t in range(NT):
                last = a.activation(H[:, t, :], xN[:, t, :], ACT.Relu, bias=lnbias[:, t:t + 1],
                                    scale=lnscale[:, t:t + 1])
            last.then_inc(s_h, 1)
            for t in range(NT):
                act.wait_ge(s_htp, t + 1)
                a.copy(h2T[:, t * P:(t + 1) * P], bank[4 + t % 2][:, 0:P]).then_inc(s_htd, 1)
            with act.If(fast == 1):
                act.wait_ge(s_h3, 3)
                a.copy(idxs, srcC[:, 0:BLC]).then_inc(s_idx, BLC // QU)

                def root_of(b):
                    act.wait_ge(s_var, b + 1)
                    a.activation(rowsc[:, 1:2], rowsc[:, 0:1], ACT.Sqrt).then_inc(s_rt, 1)

                def block(b, first, last):
                    for wv in range(BLW):
                        if wv == 0 and not first:
                            act.wait_ge(s_blk, b)
                        act.wait_ge(s_used, b * BLC + (RING + RJ * (wv + 1)))
                        ps = bank[wv % 2]
                        a.copy(aggn[:, :, wv * RD:(wv + 1) * RD], ps[:, 0:RC].rearrange("p (r d) -> p r d", d=RD))
                        a.copy(cnt_row[:, :, wv * RD:(wv + 1) * RD],
                               ps[0:1, RC:2 * RC].rearrange("p (r d) -> p r d", d=RD)).then_inc(s_wind, 1)
                        if wv % 2 and not last:
                            u = wv // 2
                            a.copy(idxs[:, u * QU:(u + 1) * QU], srcC[:, ds(b * BLC + (BLC + u * QU), QU)]).then_inc(s_idx, 1)
                        if wv == 2 and not first:
                            root_of(b - 1)
                    a.copy(timeT.rearrange("p k (w d) -> p w k d", d=RD),
                           bank[2][:, 0:3 * P].rearrange("p (w k d) -> p w k d", k=3, d=RD)).then_inc(s_timd, 1)
                    a.copy(h2Tt, h2T[:, ds(b * P, P)]).then_inc(s_timd, 1)

                block(0, True, False)
                with act.Fori(1, NT - 1) as b:
                    block(b, False, False)
                block(NT - 1, False, True)
                root_of(NT - 1)
            with act.Else():
                act.sem_inc(g_ycopy, 2)
                with act.Fori(0, NT) as t:
                    act.wait_ge(g_ymm, t * (R // 4) + 1)
                    act.sem_inc(s_gate3, 1)
                    a.copy(g_tile, h2T[:, ds(t * P, P)]).then_inc(g_tcopy, 1)
                    for k in range(R // 4):
                        act.wait_ge(g_ymm, t * (R // 4) + (k + 2))
                        act.wait_ge(g_yout, t * (16 * (R // 4)) + 16 * (k + 1))
                        a.copy(g_y, bank[6 + k % 2]).then_inc(g_ycopy, 1)
                general_take(3, 3).then_inc(g_taken, 1)
                act.wait_ge(g_invd, 16)
                general_take(4, 4).then_inc(g_taken, 1)
                act.wait_ge(g_rel, NT)
                general_take(5, 5).then_inc(g_taken, 1)
                with act.Fori(0, NT) as t:
                    act.wait_ge(g_var, t + 1)
                    a.activation(rowsc[:, 1:2], rowsc[:, 0:1], ACT.Sqrt).then_inc(g_rt, 1)

        @block.tensor
        def _(pe):
            t_ = nc.tensor
            pe.wait_ge(s_const, 1)
            zero = ohlo[:, 0, 0:P]
            t_.matmul(bank[0][:, 0:NT], zero, iota_rep[:, 0, 0:NT], start=True, stop=False, skip_group_check=True)
            t_.matmul(bank[1][:, 0:NT], zero, iota_rep[:, 0, 0:NT], start=True, stop=False,
                      skip_group_check=True).then_inc(s_hmm, 2)

            def histogram_step(step, par, last_step=False):
                pe.wait_ge(s_hoh, step + 1)
                for c in range(HCOL):
                    for a in range(2):
                        lo = ohlo[:, 2 * par + a, :].rearrange("p (j c) -> p j c", c=HCOL)[:, :, c]
                        hi = ohhi[:, 2 * par + a, 0:NT * HCOL].rearrange("p (j c) -> p j c", c=HCOL)[:, :, c]
                        mm = t_.matmul(bank[a][:, 0:NT], lo, hi, start=False, stop=last_step and c == HCOL - 1,
                                       skip_group_check=True)
                mm.then_inc(s_hmm, 1)

            with pe.Fori(0, HSTEPS // 2) as i:
                for par in range(2):
                    histogram_step(i * 2 + par, par)
            histogram_step(HSTEPS - 1, 0, True)
            pe.wait_ge(s_deg, 1)
            t_.matmul(bank[2][:, 0:NT], upper, degin, start=True, stop=True)
            t_.matmul(bank[2][:, 64:64 + NT], onesf, degin, start=True, stop=True).then_inc(s_cumps, 1)
            pe.wait_ge(s_start, 1)
            t_.transpose(bank[3][0:NT, 0:P], lnbias, ident).then_inc(s_cumps, 1)
            pe.wait_ge(s_match, 1)
            pe.wait_ge(s_startT, 1)
            t_.matmul(bank[3][:, 0:2], onesf, matched[:, 0:2], start=True, stop=True).then_inc(s_matchps, 1)
            pe.sem_inc(s_tpf, 4)
            u = 0
            pe.wait_ge(s_win, 1)
            for of in (key5, lo5, ew15):
                for t in range(WT):
                    pe.wait_ge(s_tpf, u + 1)
                    for h in range(HALF):
                        mm = t_.transpose(bank[4 + u % 4][:, h * P:(h + 1) * P], of[:, t, h * P:(h + 1) * P], ident)
                    mm.then_inc(s_tps, 1)
                    u += 1
            for of in (seg16, rel16, ew16, srf16):
                for t in range(RT):
                    pe.wait_ge(s_tpf, u + 1)
                    for j in range(RJ):
                        mm = t_.transpose(bank[4 + u % 4][:, j * RP:(j + 1) * RP], of[:, t, j * P:(j + 1) * P],
                                          ident[0:RP, 0:RP])
                    mm.then_inc(s_tps, 1)
                    u += 1

            fast = is_fast(pe)
            pe.sem_inc(s_built, 4)
            pe.sem_inc(s_applied, 2)
            pe.wait_ge(s_cols, 1)

            def build(q, g, j):
                for k in range(4):
                    m = (min(q, 1) * NG + g) * GB + 4 * j + k
                    pe.wait_ge(s_oh, m + 1)
                    if m >= 4:
                        pe.wait_ge(s_evac, m - 3)
                    for w in range(BW):
                        for h in range(HALF):
                            c = HALF * w + h
                            if q == 0:
                                half, at16 = (m // 2) % 2, (m % 2) * BS + c
                                lo, dh = oh_lo_b[:, half, :, at16], oh_dh_b[:, half, :, at16]
                            else:
                                lo, dh = oh_lo[:, k % 2, c, :], oh_dh[:, k % 2, c, :]
                            mm = t_.matmul(bank[k][:, w * WC:(w + 1) * WC], lo, dh,
                                           start=(h == 0), stop=(h == HALF - 1))
                    mm.then_inc(s_built, 1)

            def apply(q, n, j):
                g = ORDER[q][n]
                gg = q * NG + n
                if j == 0:
                    if q != 1:
                        pe.wait_ge(s_evac, (min(q, 1) * NG + g + 1) * GB)
                    elif g < 4:
                        pe.wait_ge(reloaded[g], 16)
                    if gg >= 2:
                        pe.wait_ge(s_agg, gg - 1)
                    if q < 2:
                        pe.wait_ge(s_h3, q + 1)
                    else:
                        pe.wait_ge(s_pdv, 2 * NT)
                to = bank[4 + n % 2][:, 0:GD]
                if q < 2:
                    blocks = ATB[:, g % 4, :].rearrange("p (d s) -> p d s", s=NT)
                    for hi in range(5 * j, 5 * j + 5):
                        for k in range(3):
                            mm = t_.matmul(to, H3[:, hi, k * F:(k + 1) * F], blocks[:, :, hi],
                                           start=(hi == 0 and k == 0), stop=(hi == NT - 1 and k == 2))
                else:
                    blocks = AT[:, g % 2, :].rearrange("p (d s) -> p d s", s=NT)
                    for hi in range(5 * j, 5 * j + 5):
                        mm = t_.matmul(to, H[:, hi, :], blocks[:, :, hi], start=(hi == 0), stop=(hi == NT - 1))
                if j == 4:
                    mm.then_inc(s_applied, 1)

            def general_pass(n, q):
                if n == 0:
                    pe.sem_inc(g_mm, 1)
                    pe.wait_ge(g_ready, 2)
                if n in (1, 2):
                    pe.wait_ge(s_pdv, n * NT)
                if n == 3:
                    pe.wait_ge(g_ycopy, NT * (R // 4) + 2)
                if n > 3:
                    pe.wait_ge(g_taken, n - 3)
                if n == 5:
                    pe.wait_ge(g_rel, NT)
                rows = g_toh if q == 3 else g_row
                m = R if q == 3 else P
                for i, w in GBANKS:
                    t_.matmul(bank[i][0:m, 0:w], g_zero[:, 0:m], g_iota[:, 0:w], start=True, stop=False,
                              skip_group_check=True)
                with pe.Fori(0, EC) as c:
                    if q != 3:
                        pe.wait_ge(g_landed[q > 2], c * 16 + (16 * EC * (n if n < 3 else n - 4) + 16))
                    pe.wait_ge(g_ohr, c + (n * EC + 1))
                    for i, w in GBANKS:
                        mm = t_.matmul(bank[i][0:m, 0:w], rows, g_oh[:, 512 * i:512 * i + w], start=False, stop=False,
                                       skip_group_check=True)
                    mm.then_inc(g_mm, 1)
                pe.wait_ge(g_mm, (n + 1) * EC + 1)
                pe.sem_inc(g_sum, 1)

            for q in range(3):
                with pe.If(fast == 1):
                    for g in range(NG + 1):
                        for j in range(GB // 4):
                            if g < NG and q != 1:
                                build(q, g, j)
                            if g > 0:
                                apply(q, g - 1, j)
                with pe.Else():
                    general_pass(q, q)
                pe.wait_ge(s_agg, (q + 1) * NG)
                for t in range(NT):
                    if q * NT + t >= 2:
                        pe.wait_ge(s_pdv, q * NT + t - 1)
                    tile = aggT[:, t * P:(t + 1) * P]
                    if q < 2:
                        mm = t_.matmul(bank[6 + t % 2][:, 0:F], tile, (W1s, W2s)[q], start=True, stop=True)
                    else:
                        mm = t_.transpose(bank[6 + t % 2][:, 0:F], tile, ident)
                    mm.then_inc(s_pmm, 1)
            pe.wait_ge(s_h, 3)
            for t in range(NT):
                if t >= 2:
                    pe.wait_ge(s_htd, t - 1)
                t_.transpose(bank[4 + t % 2][:, 0:P], H[:, t, :], ident).then_inc(s_htp, 1)

            with pe.If(fast == 1):
                pe.wait_ge(s_htd, NT)
                pe.sem_inc(s_used, RING)
                pe.sem_inc(s_wind, 2)

                def window(b, wv, first):
                    pe.wait_ge(s_wind, b * BLW + (wv + 1))
                    if wv == 0 and not first:
                        pe.wait_ge(s_timd, b * 2)
                    pe.wait_ge(s_ohr, b * BLW + (wv + 1))
                    tim = oh_tim[:, wv % 2, :].rearrange("p (k j) -> p k j", j=RJ)
                    for j in range(RJ):
                        n = wv * RJ + j
                        pe.wait_ge(landed[n % RING], b * (16 * (BLC // RING)) + 16 * (n // RING + 1))
                        seg = oh_seg[:, wv % 2, j, :]
                        for k in range(3):
                            row = ring[:, n % RING, k * F:(k + 1) * F]
                            t_.matmul(bank[wv % 2][:, 0:RC], row, seg, start=(j == 0 and k == 0),
                                      stop=(j == RJ - 1 and k == 2), skip_group_check=True)
                            t_.matmul(bank[2][:, wv * 3 * RD:(wv + 1) * 3 * RD], row, tim[:, :, j],
                                      start=(j == 0 and k == 0), stop=(j == RJ - 1 and k == 2))
                        t_.matmul(bank[wv % 2][0:1, RC:2 * RC], onesb[:, 0:1], seg, start=False, stop=(j == RJ - 1),
                                  skip_group_check=True).then_inc(s_used, 1)

                def block_product(b):
                    pe.wait_ge(s_wind, b * BLW + (BLW + 2))
                    pe.wait_ge(s_timd, b * 2 + 2)
                    pe.wait_ge(s_fin, b * FS + (R + 2))
                    mixed = bank[3]
                    t_.matmul(mixed[:, 0:F], h2Tt, roots, start=True, stop=True, skip_group_check=True)
                    for k in range(3):
                        t_.matmul(mixed[:, F:2 * F], timeT[:, k, :], tpws, start=(k == 0), stop=(k == 2),
                                  skip_group_check=True)
                    for r in range(R):
                        t_.matmul(bank[4 + r // 4][:, (r % 4) * F:(r % 4 + 1) * F], aggn[:, r, :], Wr[:, r, :],
                                  start=True, stop=True, skip_group_check=True)
                        mm = t_.matmul(mixed[:, 2 * F + r:2 * F + r + 1], cnt_row[:, r, :], onesf[0:1, 0:1],
                                       start=True, stop=True, skip_group_check=True)
                    mm.then_inc(s_blk, 1)

                for wv in range(BLW):
                    window(0, wv, True)
                with pe.Fori(1, NT) as b:
                    window(b, 0, False)
                    block_product(b - 1)
                    for wv in range(1, BLW):
                        window(b, wv, False)
                block_product(NT - 1)
            with pe.Else():
                pe.wait_ge(s_htd, NT)
                pe.sem_inc(g_ymm, 1)
                with pe.Fori(0, NT) as t:
                    pe.wait_ge(g_tcopy, t + 1)
                    for k in range(R // 4):
                        pe.wait_ge(g_ycopy, t * (R // 4) + (k + 1))
                        t_.matmul(bank[6 + k % 2], g_tile, Wr[:, 4 * k:4 * k + 4, :].rearrange("p r f -> p (r f)"),
                                  start=True, stop=True).then_inc(g_ymm, 1)
                general_pass(3, 3)
                general_pass(4, 4)
                pe.wait_ge(g_taken, 2)
                for t in range(NT):
                    pe.wait_ge(g_rel, t)
                    t_.transpose(bank[7][:, 0:F], aggT[:, t * P:(t + 1) * P], ident).then_inc(g_trn, 1)
                general_pass(5, 5)
                pe.wait_ge(g_taken, 3)
                for t in range(NT):
                    if t:
                        pe.wait_ge(g_chain, (t - 1) * 9 + 2)
                    t_.matmul(bank[7][:, 0:F], h2T[:, t * P:(t + 1) * P], roots, start=True, stop=True,
                              skip_group_check=True)
                    t_.matmul(bank[7][:, F:2 * F], aggT[:, t * P:(t + 1) * P], tpws, start=True, stop=True,
                              skip_group_check=True).then_inc(g_blk, 1)


_INS = ["x", "src", "dst", "edge_type_16", "edge_weight", "edge_weight1", "L0_gnn_W1", "L0_gnn_b1", "L0_gnn_W2",
        "L0_gnn_b2", "L1_gnn_basis", "L1_gnn_comp", "L1_gnn_root", "L1_gnn_bias", "L1_gnn_tp_w", "L1_gnn_tp_b",
        "L1_gnn_gamma", "L1_gnn_beta"]


def kernel(**inputs):
    import numpy as _np
    import concourse.bacc as _bacc
    from concourse import mybir as _mybir
    from concourse.bass_utils import run_bass_kernel_spmd as _run

    nc = _bacc.Bacc("TRN2", target_bir_lowering=False, num_devices=1)
    arrays, args = {}, []
    for name in _INS:
        a = _np.ascontiguousarray(inputs[name])
        arrays[f"in_{name}_dram"] = a
        args.append(nc.dram_tensor(f"in_{name}_dram", a.shape, _mybir.dt.from_np(a.dtype), kind="ExternalInput").ap())
    shape = _np.asarray(inputs["x"]).shape
    args.append(nc.dram_tensor("out_0_dram", shape, _mybir.dt.float32, kind="ExternalOutput").ap())
    gnn_kernel(nc, *args)
    r = _run(nc, [arrays], core_ids=[0])
    return r.results[0]["out_0_dram"]
```

```python
from contextlib import ExitStack

import concourse.bass as bass
from concourse import mybir

F32 = mybir.dt.float32
BF16 = mybir.dt.bfloat16
I32 = mybir.dt.int32
I16 = mybir.dt.int16
ALU = mybir.AluOpType
ACT = mybir.ActivationFunctionType
AX_X = mybir.AxisListType.X
RMAX = bass.bass_isa.ReduceOp.max
RADD = bass.bass_isa.ReduceOp.add
ds = bass.ds

P = 128
LN_EPS = 1e-5
TINY = 1e-8
DECAY = 0.1


class Chain:

    def __init__(self, eng, sem):
        self.eng, self.sem, self.n = eng, sem, 0

    def step(self, ins):
        self.n += 1
        ins.then_inc(self.sem, 1)

    def here(self):
        self.eng.wait_ge(self.sem, self.n)


def gnn_kernel(nc, x, src, dst, etype, eweight, eweight1, W1, b1, W2, b2, basis, comp, root, bias, tp_w, tp_b,
               gamma, beta, out):
    N, F = x.shape
    E = src.shape[0]
    NB = basis.shape[0]
    R = comp.shape[0]
    NT = (N + P - 1) // P
    NPAD = NT * P
    NLAST = N - (NT - 1) * P
    EP = 125
    EC = E // EP
    assert EP * EC == E and F == P

    WD = 5
    WC = WD * NT
    NW = NPAD // WD
    HALF = 2
    CAP = HALF * P
    WT = NW // P
    SLOTS = NW * HALF
    BW = 4
    BS = BW * HALF
    NBATCH = NW // BW
    NG = 8
    GB = NBATCH // NG
    GD = NPAD // NG
    GROUP = GB * BW * WC
    HB = 2 * BS
    ORDER = (tuple(range(NG)), (4, 5, 6, 7, 0, 1, 2, 3), tuple(range(NG)))

    RD = 16
    RC = R * RD
    PIECES = 5
    RK = 7
    BLC = PIECES * RK
    RP = PIECES * NT
    RCAP = RK * P
    RSLOTS = NT * BLC
    PER = P * N / E
    STEP = round(RK * PER)
    FIRST = [round(PER * (k + 0.5)) - RD // 2 for k in range(RK)]
    RANGE = [max(0, min(P - RD, STEP * (n // RK) + FIRST[n % RK])) for n in range(BLC)]
    LASTC = 15
    PADN = (BLC + 1) * P
    RJ = 5
    BUF = (0, 1, 2, 0, 1, 2, 1)
    assert len(BUF) * RJ == BLC and LASTC % RJ == 0 and R == 16
    QD = P // 4
    QLAST = [max(n for n in range(BLC) if RANGE[n] // QD <= q) for q in range(4)]
    QFIRST = [min(n for n in range(BLC) if (RANGE[n] + RD - 1) // QD >= q) for q in range(4)]
    assert all(QFIRST[q] > QLAST[q - 2] for q in (2, 3)) and QLAST[3] == BLC - 1
    IXEND = [QLAST[0] + 1, QLAST[1] + 1, QLAST[2] + 1, BLC]
    RING = BLC
    ND = 5
    VD = ND * GD
    V0 = VD // P * BLC + min(n for n in range(BLC) if RANGE[n] + RD > VD % P)
    VN = (NT - 1) * BLC + LASTC - V0
    VB = VD // P
    VRING = 20
    VSTEPS = ND * GB // 4 - 1
    VT = -(-VN // VSTEPS)
    VSTEPS = -(-VN // VT)
    VBASE = [(V0 + n) // BLC * P + RANGE[(V0 + n) % BLC] - VD for n in range(VN)]
    VLAST = [max(n for n in range(VN) if VBASE[n] // GD <= k) for k in range(NG - ND)]
    VFIRST = [min(n for n in range(VN) if (VBASE[n] + RD - 1) // GD >= k) for k in range(NG - ND)]
    FS = R + 9

    HCOL = 33
    HSTEPS = EC // HCOL

    padded = [nc.dram_tensor(f"padded_{n}_scratch", (E + PADN, 1), dt, kind="Internal").ap()
              for n, dt in (("dst", I32), ("src", I32), ("type", I32), ("ew", F32), ("ew1", F32))]
    start_dram = nc.dram_tensor("start_scratch", (NPAD,), F32, kind="Internal").ap()
    spill_dram = nc.dram_tensor("spill_scratch", (4, P, GROUP), BF16, kind="Internal").ap()
    table_dram = nc.dram_tensor("table_scratch", (NPAD, F), F32, kind="Internal").ap()
    y_dram = nc.dram_tensor("y_scratch", (NPAD, R * F), F32, kind="Internal").ap()
    inv_dram = nc.dram_tensor("inv_scratch", (R * NPAD,), F32, kind="Internal").ap()
    table3 = nc.dram_tensor("table3_scratch", (NPAD, 3 * F), BF16, kind="Internal").ap()

    def col(v):
        return v.rearrange("(e o) -> e o", o=1)

    src_col, dst_col, type_col, ew_col = col(src), col(dst), col(etype), col(eweight)

    with ExitStack() as ctx:
        def sb(name, shape, dt=F32):
            return ctx.enter_context(nc.sbuf_tensor(name, shape, dt))[tuple(slice(None) for _ in shape)]

        def sem(name):
            return ctx.enter_context(nc.semaphore("s_" + name))

        xN = sb("xN", [P, NT, F])
        H = sb("H", [P, NT, F])
        aggT = sb("aggT", [P, NPAD])
        H3 = sb("H3", [P, NT, 3 * F], BF16)
        loB, keyB = sb("loB", [P, SLOTS], BF16), sb("keyB", [P, SLOTS], BF16)
        ew1C = sb("ew1C", [P, SLOTS])
        colR = sb("colR", [P, RSLOTS, 4])
        srcC = sb("srcC", [P, RSLOTS], I32)
        ew1R = sb("ew1R", [P, RSLOTS - VB * BLC])
        W1s, W2s, roots, tpws = (sb(n, [P, F]) for n in ("W1s", "W2s", "roots", "tpws"))
        b1b, b2b, biasb, tpbb, gammab, betab = (sb(n, [P, F]) for n in ("b1b", "b2b", "biasb", "tpbb", "gammab", "betab"))
        Wr = sb("Wr", [P, R, F])
        ident = sb("ident", [P, P])
        onesf = sb("onesf", [P, P])
        zerob = sb("zerob", [P, P], BF16)
        upper = sb("upper", [P, P])
        iota_f = sb("iota_f", [P, P])
        iota_16 = sb("iota_16", [P, P, HB], BF16)
        nowA = sb("nowA", [P, 4 * BS, 3])
        iota_h = sb("iota_h", [P, RC], I16)
        degin, invdeg, innorm, onorm = (sb(n, [P, NT]) for n in ("degin", "invdeg", "innorm", "onorm"))
        lnscale, lnbias, sc1, sc2, sc3 = (sb(n, [P, NT]) for n in ("lnscale", "lnbias", "sc1", "sc2", "sc3"))
        stats = sb("stats", [P, NT, 6])
        aggr = sb("aggr", [P, NT, 2])
        st5, st16 = sb("st5", [P, WT]), sb("st16", [P, 1])
        ix5, ix16 = sb("ix5", [P, WT], I32), sb("ix16", [P, 1], I32)
        base5 = sb("base5", [P, WT])
        ibase = sb("ibase", [P, WT + 3], I32)
        piece = sb("piece", [P, 3])
        range16 = sb("range16", [P, RK])
        lastok = sb("lastok", [1, 1])
        compb = sb("compb", [P, R * NB])
        tw = sb("tw", [P, 12])
        matched = sb("matched", [P, 4])
        pad_dst, pad_zero = sb("pad_dst", [P, PADN // P], I32), sb("pad_zero", [P, PADN // P], I32)
        flag = sb("flag", [1, 1], I32)
        startT = sb("startT", [NT, P])
        rowstat = sb("rowstat", [P, 6])
        rowaggr = sb("rowaggr", [P, 2])
        rowsc = sb("rowsc", [P, 3])

        ARENA = 79 * 1024 // 4
        arena = sb("arena", [P, ARENA])
        at = [0]

        def carve(shape, dt=F32, reset=False):
            if reset:
                at[0] = 0
            n = 1
            for s in shape[1:]:
                n *= s
            w = n if dt in (F32, I32) else (n + 1) // 2
            v = arena[0:shape[0], at[0]:at[0] + w]
            at[0] += w
            assert at[0] <= ARENA, at[0]
            if dt is not F32:
                v = v.bitcast(dt)[:, 0:n]
            if len(shape) == 3:
                v = v.rearrange("p (a b) -> p a b", b=shape[2])
            elif len(shape) == 4:
                v = v.rearrange("p (a b c) -> p a b c", b=shape[2], c=shape[3])
            return v

        dst_rows = carve([EP, EC], I32, reset=True)
        src_rows = carve([EP, EC], I32)
        ew_rows = carve([EP, EC])
        tmp_rows = carve([EP, EC], I32)
        digits = carve([EP, 4, EC + 1], BF16)
        iota_rep = carve([EP, P, HCOL], BF16)
        ohlo = carve([EP, 4, P * HCOL], BF16)
        ohhi = carve([EP, 4, NT * HCOL + 1], BF16)
        iota_i = carve([P, RC], I32)
        ramp_i = carve([P, P], I32)
        basis_s = carve([P, NB, F])
        basis_from = at[0] - NB * F
        dst5 = carve([P, WT, CAP], I32, reset=True)
        src5 = carve([P, WT, CAP], I32)
        ew15 = carve([P, WT, CAP])
        key5 = carve([P, WT, CAP])
        tmp5 = carve([P, WT, CAP], I32)
        dst16, src16, typ16 = (carve([RP, RCAP], I32) for _ in range(3))
        ew16, ew116, rel16, seg16 = (carve([RP, RCAP]) for _ in range(4))
        assert at[0] <= basis_from
        lo5 = tmp5.bitcast(F32)
        ok5 = dst5.bitcast(F32)
        ok16 = dst16.bitcast(F32)
        srf16, tyf16 = src16.bitcast(F32), typ16.bitcast(F32)
        AT = carve([P, 2, GROUP], reset=True)
        ATB = carve([P, 4, GROUP], BF16, reset=True)
        h2T = carve([P, NPAD], reset=True)
        h2T_end = at[0]
        ring = carve([P, RING, 3 * F], BF16)
        oh_seg = carve([P, 3, RJ, RC], BF16)
        oh_tim = carve([P, 3, 3 * RD * RJ], BF16)
        oh_rel = carve([P, 3, RD * RJ], BF16)
        oh_typ = carve([P, 3, RD * RJ], BF16)
        iota_t = carve([P, RD * RJ], BF16)
        now = carve([P, BLC, 4])
        wpart = carve([P, 3, BLC], BF16)
        idxs = carve([P, BLC], I32)
        aggn = carve([P, R, P])
        cntT = carve([R, P])
        inv = carve([P, 2, R])
        timeT = carve([P, 3, P])
        h2Tt = carve([P, P])
        fin = carve([P, 5, F])
        outt = carve([P, F])

        at[0] = h2T_end
        g_src, g_dst, g_typ = (carve([EP, EC], I32) for _ in range(3))
        g_ew, g_ew1 = carve([EP, EC]), carve([EP, EC])
        g_yix, g_cix = carve([EP, EC], I32), carve([EP, EC], I32)
        g_dstf, g_typf = g_dst.bitcast(F32), g_typ.bitcast(F32)
        g_oh = carve([EP, NPAD])
        g_iota = carve([EP, NPAD])
        g_row = carve([EP, F])
        g_ix, g_cx = carve([EP, 1], I32), carve([EP, 1], I32)
        g_w = carve([EP, 1])
        g_toh = carve([EP, R])
        g_zero = carve([EP, P])
        g_tile = carve([P, P])
        g_y = carve([P, 4 * F])
        g_fin = carve([P, 5, F])
        g_out = carve([P, F])

        oh_words = sb("oh_words", [P, 2 * BS * (P + WC)])
        oh_lo = oh_words[:, 0:2 * BS * P].rearrange("p (a b c) -> p a b c", a=2, b=BS)
        oh_dh = oh_words[:, 2 * BS * P:].rearrange("p (a b c) -> p a b c", a=2, b=BS)
        oh_half = oh_words.bitcast(BF16)
        oh_lo_b = oh_half[:, 0:2 * HB * P].rearrange("p (a j c) -> p a j c", a=2, c=HB)
        oh_dh_b = oh_half[:, 2 * HB * P:].rearrange("p (a j c) -> p a j c", a=2, c=HB)

        h3_words = H3.rearrange("p t f -> p (t f)").bitcast(F32)
        v_ring = h3_words[:, 0:VRING * F].rearrange("p (n f) -> p n f", f=F)
        v_oh, v_eq, v_iota = (h3_words[:, VRING * F + a * RD * VT:VRING * F + b * RD * VT]
                              for a, b in ((0, 2), (2, 3), (3, 4)))
        v_oh = v_oh.rearrange("p (a d j) -> p a d j", a=2, j=VT)
        v_eq, v_iota = (x_.rearrange("p (d j) -> p d j", j=VT) for x_ in (v_eq, v_iota))
        v_ix = h3_words[:, VRING * F + 4 * RD * VT:VRING * F + 4 * RD * VT + 2 * VRING].bitcast(I32)

        bank = [ctx.enter_context(nc.psum_tensor(f"bank{i}", [P, 512], F32))[:, :] for i in range(8)]

        s_rows, s_x, s_w, s_basis = sem("rows"), sem("x"), sem("w"), sem("basis")
        s_pad, s_iota, s_const, s_wr, s_poolch = sem("pad"), sem("iota"), sem("const"), sem("wr"), sem("poolch")
        s_hoh, s_hmm, s_deg, s_cum, s_cumps, s_start, s_startT = (
            sem(n) for n in ("hoh", "hmm", "deg", "cum", "cumps", "start", "startT"))
        s_sout, s_sin, s_ix, s_slots = sem("sout"), sem("sin"), sem("ix"), sem("slots")
        s_dve = sem("dve")
        s_twmax, s_twred, s_twsum, s_twred2 = sem("twmax"), sem("twred"), sem("twsum"), sem("twred2")
        s_sqd, s_sqr, s_lnv, s_lns, s_lnr, s_h = (sem(n) for n in ("sqd", "sqr", "lnv", "lns", "lnr", "h"))
        s_wexp, s_win, s_tps, s_tpf, s_cols, s_wparts = (sem(n) for n in ("wexp", "win", "tps", "tpf", "cols", "wparts"))
        s_oh, s_built, s_evac, s_applied, s_agg = (sem(n) for n in ("oh", "built", "evac", "applied", "agg"))
        s_pmm, s_pdv = sem("pmm"), sem("pdv")
        s_h3, s_table, s_htp, s_htd = sem("h3"), sem("table"), sem("htp"), sem("htd")
        s_idx, s_ohr, s_used, s_wins, s_wind = (sem(n) for n in ("idx", "ohr", "used", "wins", "wind"))
        s_nowa, s_now, s_rel = sem("nowa"), sem("now"), sem("rel")
        s_gate, s_gate2, s_gate3 = sem("gate"), sem("gate2"), sem("gate3")
        s_timd, s_blk, s_fin, s_var, s_rt, s_res, s_out = (
            sem(n) for n in ("timd", "blk", "fin", "var", "rt", "res", "out"))
        v_tab, v_ixs, v_ready, v_eqs, v_ohs, v_used, v_agg = (
            sem(n) for n in ("v_tab", "v_ixs", "v_ready", "v_eqs", "v_ohs", "v_used", "v_agg"))
        v_landed = [sem(f"v_landed{i}") for i in range(VRING // RJ)]
        s_padded, s_pads = sem("padded"), sem("pads")
        landed = [sem(f"landed{i}") for i in range(RING // RJ)]
        spilled = [sem(f"spilled{i}") for i in range(4)]
        reloaded = [sem(f"reloaded{i}") for i in range(4)]
        s_match, s_matchps, s_flag = sem("match"), sem("matchps"), sem("flag")
        g_rows, g_ready, g_tab, g_init = sem("g_rows"), sem("g_ready"), sem("g_tab"), sem("g_init")
        g_landed = sem("g_landed_first"), sem("g_landed_second")
        g_wland, g_ixr, g_ohr, g_mm, g_sum = (
            sem(n) for n in ("g_wland", "g_ixr", "g_ohr", "g_mm", "g_sum"))
        g_taken, g_inv, g_invd, g_tcopy, g_ymm, g_ycopy, g_yout = (
            sem(n) for n in ("g_taken", "g_inv", "g_invd", "g_tcopy", "g_ymm", "g_ycopy", "g_yout"))
        g_res2, g_dve = sem("g_res2"), sem("g_dve")
        g_trn, g_rel, g_blk, g_chain, g_var, g_rt, g_res, g_store = (
            sem(n) for n in ("g_trn", "g_rel", "g_blk", "g_chain", "g_var", "g_rt", "g_res", "g_store"))
        block = ctx.enter_context(nc.Block())

        GBANKS = [(i, min(512, NPAD - 512 * i)) for i in range((NPAD + 511) // 512)]

        def is_fast(eng):
            eng.wait_ge(s_flag, 1)
            return eng.value_load(flag[0:1, 0:1], min_val=0, max_val=1)

        @block.sync
        def _(sp):
            for t, d in ((dst_rows, dst), (src_rows, src), (ew_rows, eweight)):
                sp.dma_start(t, d.rearrange("(p c) -> p c", p=EP)).then_inc(s_rows, 16)
            edges = (col(dst), col(src), col(etype), col(eweight), eweight1)
            for to, of in zip(padded, edges):
                sp.dma_start(to[0:E, :].rearrange("(p c) o -> p (c o)", p=EP),
                             of.rearrange("(p c) o -> p (c o)", p=EP)).then_inc(s_padded, 16)
            sp.wait_ge(s_pads, 2)
            for to, pad in zip(padded, (pad_dst, pad_zero, pad_zero, pad_zero.bitcast(F32), pad_zero.bitcast(F32))):
                sp.dma_start(to[E:E + PADN, :].rearrange("(p c) o -> p (c o)", p=P), pad).then_inc(s_padded, 16)
            sp.wait_ge(s_pad, 1)
            sp.dma_start(xN[:, 0:NT - 1, :], x[0:(NT - 1) * P, :].rearrange("(t p) f -> p t f", p=P)).then_inc(s_x, 16)
            sp.dma_start(xN[0:NLAST, NT - 1, :], x[(NT - 1) * P:N, :]).then_inc(s_x, 16)
            sp.dma_start(basis_s, basis.rearrange("b i o -> i b o")).then_inc(s_basis, 16)
            sp.dma_start(compb, comp.rearrange("r b -> (r b)").partition_broadcast(P)).then_inc(s_basis, 16)
            for t, d in ((W1s, W1), (W2s, W2), (roots, root), (tpws, tp_w)):
                sp.dma_start(t, d).then_inc(s_w, 16)
            for t, d in ((b1b, b1), (b2b, b2), (biasb, bias), (tpbb, tp_b), (gammab, gamma), (betab, beta)):
                sp.dma_start(t, d.partition_broadcast(P)).then_inc(s_w, 16)
            sp.wait_ge(s_startT, 1)
            sp.dma_start(start_dram.rearrange("(h l) -> h l", l=P), startT).then_inc(s_sout, 16)
            sp.wait_ge(s_sout, 16)
            for t in range(WT):
                sp.dma_start(st5[:, t:t + 1], start_dram[t * P * WD:(t + 1) * P * WD].rearrange(
                    "(p o) -> p o", o=WD)[:, 0:1], allow_slow_non_contiguous=True).then_inc(s_sin, 16)
            for t in range(PIECES):
                sp.dma_start(st16[t * NT:(t + 1) * NT, :], start_dram.rearrange("(p o) -> p o", o=P)[:, 0:1],
                             allow_slow_non_contiguous=True).then_inc(s_sin, 16)
            fast = is_fast(sp)
            with sp.If(fast == 1):
                for g in range(4):
                    sp.wait_ge(s_evac, (g + 1) * GB)
                    sp.dma_start(spill_dram[g], ATB[:, g, :]).then_inc(spilled[g], 16)
                for g in range(4):
                    sp.wait_ge(s_applied, 2 + NG + g + 1)
                    sp.dma_start(ATB[:, g, :], spill_dram[g]).then_inc(reloaded[g], 16)
                sp.wait_ge(s_pdv, 2 * NT)
                sp.dma_start(table_dram.rearrange("(t p) f -> p t f", p=P), H).then_inc(v_tab, 16)
                sp.wait_ge(s_h3, 3)
                sp.dma_start(table3.rearrange("(t p) f -> p t f", p=P), H3).then_inc(s_table, 16)
                sp.sem_inc(s_out, 16)
                with sp.Fori(0, NT - 1) as b:
                    sp.wait_ge(s_res, b + 1)
                    sp.dma_start(out[ds(b * P, P), :], outt).then_inc(s_out, 16)
                sp.wait_ge(s_res, NT)
                sp.dma_start(out[(NT - 1) * P:N, :], outt[0:NLAST, :]).then_inc(s_out, 16)
                sp.wait_ge(s_out, 16 + 16 * NT)
            with sp.Else():
                sp.wait_ge(s_cols, 1)
                for t, d in ((g_src, src), (g_dst, dst), (g_typ, etype), (g_ew, eweight),
                             (g_ew1, eweight1.rearrange("e o -> (e o)"))):
                    sp.dma_start(t, d.rearrange("(p c) -> p c", p=EP)).then_inc(g_rows, 16)
                nodes = table_dram.rearrange("(t p) f -> p t f", p=P)
                for q in range(4):
                    if q == 2:
                        sp.wait_ge(s_pdv, 2 * NT)
                    else:
                        sp.wait_ge(s_h, min(q, 2) + 1)
                    sp.dma_start(nodes, H).then_inc(g_tab, 16)
                sp.sem_inc(g_yout, 16)
                with sp.Fori(0, NT) as t:
                    for k in range(R // 4):
                        sp.wait_ge(g_ycopy, t * (R // 4) + (k + 3))
                        sp.dma_start(y_dram[ds(t * P, P), k * 4 * F:(k + 1) * 4 * F], g_y).then_inc(g_yout, 16)
                sp.wait_ge(g_inv, 1)
                sp.dma_start(inv_dram.rearrange("(r n) -> r n", r=R), aggT[0:R, :]).then_inc(g_invd, 16)
                sp.sem_inc(g_store, 16)
                with sp.Fori(0, NT - 1) as b:
                    sp.wait_ge(g_res, b + 2)
                    sp.dma_start(out[ds(b * P, P), :], g_out).then_inc(g_store, 16)
                sp.wait_ge(g_res, NT + 1)
                sp.dma_start(out[(NT - 1) * P:N, :], g_out[0:NLAST, :]).then_inc(g_store, 16)
                sp.wait_ge(g_store, 16 + 16 * NT)

        @block.gpsimd
        def _(pool):
            g = nc.gpsimd
            ch = Chain(pool, s_poolch)
            g.memset(xN[:, NT - 1, :], 0.0).then_inc(s_pad, 1)
            g.iota(iota_i, [[1, RC]], base=0, channel_multiplier=0).then_inc(s_iota, 1)
            g.iota(ramp_i, [[1, P]], base=0, channel_multiplier=-1).then_inc(s_iota, 1)
            g.iota(ibase[:, 0:WT], [[P * WD, WT]], base=0, channel_multiplier=WD).then_inc(s_iota, 1)
            g.iota(ibase[:, WT:WT + 1], [[0, 1]], base=0, channel_multiplier=(1 << 17) // NT + 1).then_inc(s_iota, 1)
            g.iota(ibase[:, WT + 1:WT + 2], [[0, 1]], base=0, channel_multiplier=1).then_inc(s_iota, 1)
            g.memset(pad_dst, 1 << 20).then_inc(s_pads, 1)
            g.memset(pad_zero, 0).then_inc(s_pads, 1)
            pool.wait_ge(s_basis, 32)
            prod = aggT[:, 0:R * F].rearrange("p (r f) -> p r f", f=F)
            cb = compb.rearrange("p (r b) -> p r b", b=NB)
            for b in range(NB):
                first = basis_s[:, b, :].unsqueeze(1).to_broadcast([P, R, F])
                coef = cb[:, :, b:b + 1].to_broadcast([P, R, F])
                if b == 0:
                    ch.step(g.tensor_tensor(Wr, first, coef, ALU.mult))
                    ch.here()
                    continue
                ch.step(g.tensor_tensor(prod, first, coef, ALU.mult))
                ch.here()
                ch.step(g.tensor_tensor(Wr, Wr, prod, ALU.add))
                ch.here()
                if b == 4:
                    pool.wait_ge(s_twmax, 1)
                    g.partition_all_reduce(tw[0:EP, 2:4], tw[0:EP, 0:2], EP, RMAX).then_inc(s_twred, 1)
                if b == 6:
                    pool.wait_ge(s_twsum, 1)
                    g.partition_all_reduce(tw[0:EP, 8:9], tw[0:EP, 7:8], EP, RADD).then_inc(s_twred2, 1)
            pool.sem_inc(s_wr, 1)
            pool.wait_ge(s_ix, 1)
            ew1_col = eweight1
            for t in range(WT):
                for to, of in ((dst5, dst_col), (src5, src_col), (ew15, ew1_col)):
                    g.indirect_dma_start(to[:, t, :], None, of,
                                         bass.IndirectOffsetOnAxis(ap=ix5[:, t:t + 1], axis=0)).then_inc(s_slots, 16)
            pool.wait_ge(s_padded, 16 * 10)
            for to, of in zip((dst16, src16, typ16, ew16, ew116), padded):
                g.indirect_dma_start(to, None, of,
                                     bass.IndirectOffsetOnAxis(ap=ix16[0:RP, 0:1], axis=0)).then_inc(s_slots, 16)
            fast = is_fast(pool)
            with pool.If(fast == 1):
                pool.wait_ge(v_tab, 16)

                def gather(i, half, count):
                    pool.wait_ge(v_used, i * (2 * VRING) + (half * VRING + RJ))
                    g.tensor_copy(v_ix[:, half * VRING:half * VRING + count],
                                  srcC[:, ds(i * (2 * VRING) + (V0 + half * VRING), count)]).then_inc(v_ixs, 1)
                    pool.wait_ge(v_ixs, i * 2 + (half + 1))
                    for n in range(count):
                        if n % RJ == 0:
                            pool.wait_ge(v_used, i * (2 * VRING) + (half * VRING + n + RJ))
                            pool.sem_inc(s_gate, 1)
                        g.indirect_dma_start(v_ring[:, n, :], None, table_dram, bass.IndirectOffsetOnAxis(
                            ap=v_ix[:, half * VRING + n:half * VRING + n + 1], axis=0)).then_inc(v_landed[n // RJ], 16)

                with pool.Fori(0, VN // (2 * VRING)) as i:
                    for half in range(2):
                        gather(i, half, VRING)
                whole = VN // (2 * VRING)
                for half in range(2):
                    if VN > whole * 2 * VRING + half * VRING:
                        gather(whole, half, min(VRING, VN - whole * 2 * VRING - half * VRING))
                pool.wait_ge(s_table, 16)

                def gather_block(b, chunks):
                    for n in range(chunks):
                        if n == 0 or n in IXEND:
                            pool.wait_ge(s_idx, b * 4 + (sum(n >= e for e in IXEND) + 1))
                            pool.sem_inc(s_gate, 1)
                        if n % RJ == 0:
                            pool.wait_ge(s_used, b * BLC + (n + RJ))
                            pool.sem_inc(s_gate, 1)
                        g.indirect_dma_start(ring[:, n, :], None, table3,
                                             bass.IndirectOffsetOnAxis(ap=idxs[:, n:n + 1], axis=0)
                                             ).then_inc(landed[n // RJ], 16)

                with pool.Fori(0, NT - 1) as b:
                    gather_block(b, BLC)
                gather_block(NT - 1, LASTC)
            with pool.Else():
                y_rows = y_dram.rearrange("n (r f) -> (n r) f", f=F)
                pool.wait_ge(s_cols, 1)
                g.iota(g_iota.bitcast(I32), [[1, NPAD]], base=0, channel_multiplier=0).then_inc(g_init, 1)
                for n, q in enumerate((0, 1, 2, 4, 5)):
                    if q < 4:
                        pool.wait_ge(g_tab, 16 * (q + 1))
                    elif q == 4:
                        pool.wait_ge(g_tab, 16 * 4)
                        pool.wait_ge(g_yout, 16 + 16 * NT * (R // 4))
                        pool.wait_ge(g_invd, 16)
                    with pool.Fori(0, EC) as c:
                        pool.wait_ge(g_ixr, c + (n * EC + 1))
                        pool.sem_inc(s_gate, 1)
                        if q == 4:
                            g.indirect_dma_start(g_w, None, col(inv_dram),
                                                 bass.IndirectOffsetOnAxis(ap=g_cx, axis=0)).then_inc(g_wland, 16)
                        g.indirect_dma_start(g_row, None, y_rows if q == 4 else table_dram,
                                             bass.IndirectOffsetOnAxis(ap=g_ix, axis=0)).then_inc(g_landed[q > 2], 16)

        @block.vector
        def _(dve):
            v = nc.vector
            ch, gch = Chain(dve, s_dve), Chain(dve, g_dve)
            v.memset(matched, 0.0)
            dve.wait_ge(s_iota, 5)
            v.tensor_copy(base5, ibase[:, 0:WT])
            ch.step(v.tensor_scalar(ibase[:, WT + 2:WT + 3], ibase[:, WT:WT + 1], 17, None, ALU.logical_shift_right))
            ch.here()
            v.tensor_copy(piece[:, 0:1], ibase[:, WT + 2:WT + 3])
            ch.step(v.tensor_scalar(piece[:, 1:2], ibase[:, WT + 1:WT + 2], float(P), None, ALU.mult))
            ch.here()
            for k in range(RK):
                v.tensor_scalar(range16[:, k:k + 1], piece[:, 0:1], float(STEP), float(FIRST[k]), ALU.mult, ALU.add)
            ch.step(v.scalar_tensor_tensor(piece[:, 2:3], piece[:, 0:1], -float(NT * P), piece[:, 1:2],
                                           ALU.mult, ALU.add))
            ch.here()
            ch.step(v.tensor_scalar(range16, range16, 0.0, float(P - RD), ALU.max, ALU.min))
            ch.here()
            ch.step(v.tensor_scalar(range16, range16, piece[:, 2:3], None, ALU.add))
            ch.here()
            v.tensor_copy(iota_f, iota_i[:, 0:P])
            v.tensor_copy(iota_16, iota_i[:, 0:P].unsqueeze(2).to_broadcast([P, P, HB]))
            v.tensor_copy(iota_h, iota_i)
            v.memset(onesf, 1.0)
            v.memset(zerob, 0.0)
            v.memset(ohlo[:, 0, 0:P], 0.0)
            v.tensor_copy(iota_rep, iota_i[0:EP, 0:P].unsqueeze(2).to_broadcast([EP, P, HCOL]))
            v.tensor_scalar(ident, ramp_i, 0, None, ALU.is_equal)
            v.tensor_scalar(upper, ramp_i, 0, None, ALU.is_gt).then_inc(s_const, 1)
            dve.wait_ge(s_rows, 48)
            for a, rows in enumerate((dst_rows, src_rows)):
                ch.step(v.tensor_scalar(tmp_rows, rows, P - 1, None, ALU.bitwise_and))
                ch.here()
                ch.step(v.tensor_copy(digits[:, 2 * a, 0:EC], tmp_rows))
                ch.here()
                ch.step(v.tensor_scalar(tmp_rows, rows, 7, None, ALU.logical_shift_right))
                ch.here()
                ch.step(v.tensor_copy(digits[:, 2 * a + 1, 0:EC], tmp_rows))
                ch.here()
            v.tensor_reduce(tw[0:EP, 0:1], ew_rows, AX_X, ALU.max)
            ch.step(v.tensor_reduce(tw[0:EP, 1:2], ew_rows, AX_X, ALU.min))
            ch.here()
            v.tensor_scalar(tw[0:EP, 1:2], tw[0:EP, 1:2], -1.0, None, ALU.mult).then_inc(s_twmax, 1)

            def histogram_step(step, par):
                dve.wait_ge(s_hmm, step + 1)
                for a in range(2):
                    lo = digits[:, 2 * a, ds(step * HCOL, HCOL)]
                    hi = digits[:, 2 * a + 1, ds(step * HCOL, HCOL)]
                    v.tensor_tensor(ohlo[:, 2 * par + a, :].rearrange("p (j c) -> p j c", c=HCOL), iota_rep,
                                    lo.unsqueeze(1).to_broadcast([EP, P, HCOL]), ALU.is_equal)
                    last = v.tensor_tensor(ohhi[:, 2 * par + a, 0:NT * HCOL].rearrange("p (j c) -> p j c", c=HCOL),
                                           iota_rep[:, 0:NT, :], hi.unsqueeze(1).to_broadcast([EP, NT, HCOL]),
                                           ALU.is_equal)
                last.then_inc(s_hoh, 1)

            with dve.Fori(0, HSTEPS // 2) as i:
                for par in range(2):
                    histogram_step(i * 2 + par, par)
            histogram_step(HSTEPS - 1, 0)

            dve.wait_ge(s_twred, 1)
            ch.step(v.tensor_tensor(tw[0:EP, 4:5], tw[0:EP, 2:3], tw[0:EP, 3:4], ALU.add))
            ch.here()
            ch.step(v.tensor_scalar(tw[0:EP, 4:5], tw[0:EP, 4:5], TINY, None, ALU.add))
            ch.here()
            ch.step(v.reciprocal(tw[0:EP, 4:5], tw[0:EP, 4:5]))
            ch.here()
            ch.step(v.tensor_scalar(tw[0:EP, 5:6], tw[0:EP, 4:5], DECAY, None, ALU.mult))
            ch.here()
            v.scalar_tensor_tensor(tw[0:EP, 6:7], tw[0:EP, 5:6], -1.0, tw[0:EP, 2:3], ALU.mult,
                                   ALU.mult).then_inc(s_wexp, 1)

            dve.wait_ge(s_x, 32)
            for t in range(NT):
                last = v.bn_stats(stats[:, t, :], xN[:, t, :])
            ch.step(last)
            ch.here()
            for t in range(NT):
                last = v.bn_aggr(aggr[:, t, :], stats[:, t, :])
            ch.step(last)
            ch.here()
            v.tensor_scalar(sc1, aggr[:, :, 1], LN_EPS, None, ALU.add).then_inc(s_lnv, 1)

            dve.wait_ge(s_hmm, 2 + HSTEPS)
            v.tensor_copy(degin, bank[0][:, 0:NT]).then_inc(s_deg, 1)
            v.tensor_scalar(sc2, bank[0][:, 0:NT], 1.0, None, ALU.max)
            ch.step(v.tensor_scalar(sc3, bank[1][:, 0:NT], 1.0, None, ALU.max))
            ch.here()
            v.reciprocal(invdeg, sc2).then_inc(s_sqd, 1)
            dve.wait_ge(s_cumps, 1)
            ch.step(v.tensor_copy(innorm, bank[2][:, 64:64 + NT]))
            ch.here()
            ch.step(v.tensor_tensor_scan(onorm, onesf[:, 0:NT], innorm, 0.0, ALU.mult, ALU.add))
            ch.here()
            ch.step(v.tensor_tensor(onorm, onorm, innorm, ALU.subtract))
            ch.here()
            v.tensor_tensor(lnbias, onorm, bank[2][:, 0:NT], ALU.add).then_inc(s_start, 1)
            dve.wait_ge(s_start, 1)
            v.tensor_scalar(lastok, lnbias[0:1, NT - 1:NT], float(E - LASTC * P), None, ALU.is_ge)
            dve.wait_ge(s_cumps, 2)
            v.tensor_copy(startT, bank[3][0:NT, 0:P]).then_inc(s_startT, 1)
            dve.wait_ge(s_sqr, 1)
            v.reciprocal(innorm, sc2)
            dve.wait_ge(s_lns, 1)
            v.reciprocal(onorm, sc3)
            ch.step(v.reciprocal(sc1, sc1))
            ch.here()
            ch.step(v.tensor_tensor(lnscale, sc1, onorm, ALU.mult))
            ch.here()
            v.scalar_tensor_tensor(lnbias, aggr[:, :, 0], -1.0, lnscale, ALU.mult, ALU.mult).then_inc(s_lnr, 1)

            dve.wait_ge(s_sin, 16 * (WT + PIECES))
            v.tensor_scalar(ix5, st5, float(E - CAP), None, ALU.min)
            ch.step(v.scalar_tensor_tensor(st16[0:RP, :], piece[0:RP, 0:1], float(RCAP), st16[0:RP, :],
                                           ALU.mult, ALU.add))
            ch.here()
            v.tensor_scalar(ix16[0:RP, :], st16[0:RP, :], float(E + PADN - RCAP), None, ALU.min).then_inc(s_ix, 1)

            dve.wait_ge(s_slots, 16 * (3 * WT + 5))
            for t in range(WT):
                last = v.tensor_scalar(key5[:, t, :], dst5[:, t, :], base5[:, t:t + 1], float(NT),
                                       ALU.subtract, ALU.mult)
            v.tensor_scalar(tmp5, src5, 7, None, ALU.logical_shift_right)
            for k in range(RK):
                v.tensor_scalar(rel16[:, k * P:(k + 1) * P], dst16[:, k * P:(k + 1) * P], range16[0:RP, k:k + 1], None,
                                ALU.subtract)
            ch.step(v.tensor_scalar(src5, src5, P - 1, None, ALU.bitwise_and))
            ch.here()
            v.scalar_tensor_tensor(seg16, rel16, float(R), typ16, ALU.mult, ALU.add)
            v.tensor_scalar(ok16, rel16, 0.0, None, ALU.is_ge)
            ch.step(v.tensor_tensor(key5, key5, tmp5, ALU.add))
            ch.here()
            v.scalar_tensor_tensor(ok16, rel16, float(RD), ok16, ALU.is_lt, ALU.mult)
            v.tensor_copy(srf16, src16)
            v.tensor_copy(tyf16, typ16)
            v.tensor_scalar(ok5, key5, 0.0, None, ALU.is_ge)
            ch.step(v.tensor_copy(lo5, src5))
            ch.here()
            v.scalar_tensor_tensor(ok5, key5, float(WC), ok5, ALU.is_lt, ALU.mult)
            ch.step(v.scalar_tensor_tensor(seg16, seg16, 1.0, ok16, ALU.add, ALU.mult))
            ch.here()
            v.scalar_tensor_tensor(key5, key5, 1.0, ok5, ALU.add, ALU.mult)
            v.tensor_reduce(matched[:, 0:1], ok5.rearrange("p t c -> p (t c)"), AX_X, ALU.add)
            v.tensor_reduce(matched[0:RP, 1:2], ok16, AX_X, ALU.add).then_inc(s_match, 1)
            ch.step(v.tensor_scalar(seg16, seg16, -1.0, None, ALU.add))
            ch.here()
            ch.step(v.tensor_scalar(key5, key5, -1.0, None, ALU.add))
            ch.here()
            dve.wait_ge(s_twred2, 1)
            ch.step(v.tensor_scalar(tw[0:EP, 9:10], tw[0:EP, 8:9], TINY, None, ALU.add))
            ch.here()
            ch.step(v.reciprocal(tw[0:EP, 10:11], tw[0:EP, 9:10]))
            ch.here()
            dve.wait_ge(s_wexp, 2)
            v.tensor_scalar(ew16, ew16, tw[0:RP, 10:11], None, ALU.mult).then_inc(s_win, 1)
            dve.wait_ge(s_matchps, 1)
            ch.step(v.tensor_scalar(matched[0:1, 2:4], bank[3][0:1, 0:2], float(E), None, ALU.is_equal))
            ch.here()
            ch.step(v.tensor_tensor(lastok, lastok, matched[0:1, 2:3], ALU.mult))
            ch.here()
            v.tensor_tensor(flag, lastok, matched[0:1, 3:4], ALU.mult).then_inc(s_flag, 1)
            fast = is_fast(dve)

            left = aggT.rearrange("p (t f) -> p t f", f=F)

            def split(t0, t1):
                w, r = H[:, t0:t1, :], left[:, t0:t1, :]
                ch.step(v.tensor_copy(H3[:, t0:t1, 0:F], w))
                ch.here()
                ch.step(v.tensor_tensor(r, w, H3[:, t0:t1, 0:F], ALU.subtract))
                ch.here()
                ch.step(v.tensor_copy(H3[:, t0:t1, F:2 * F], r))
                ch.here()
                ch.step(v.tensor_tensor(r, r, H3[:, t0:t1, F:2 * F], ALU.subtract))
                ch.here()
                return v.tensor_copy(H3[:, t0:t1, 2 * F:3 * F], r)

            def onehots_bf16(c0, half, n):
                dve.wait_ge(s_built, n)
                v.tensor_tensor(oh_lo_b[:, half], iota_16, loB[:, ds(c0, HB)].unsqueeze(1).to_broadcast([P, P, HB]),
                                ALU.is_equal)
                v.tensor_tensor(oh_dh_b[:, half], iota_16[:, 0:WC, :],
                                keyB[:, ds(c0, HB)].unsqueeze(1).to_broadcast([P, WC, HB]),
                                ALU.is_equal).then_inc(s_oh, 2)

            def onehots_f32(b, k):
                dve.wait_ge(s_built, b * 4 + (NBATCH + 4 + k - 1))
                for s in range(BS):
                    c = k * BS + s
                    v.tensor_scalar(oh_lo[:, k % 2, s, :], iota_f, nowA[:, c, 0:1], None, ALU.is_equal)
                    last = v.tensor_scalar(oh_dh[:, k % 2, s, :], iota_f[:, 0:WC], nowA[:, c, 1:2],
                                           nowA[:, c, 2:3], ALU.is_equal, ALU.mult)
                last.then_inc(s_oh, 1)

            dve.wait_ge(s_cols, 1)
            dve.wait_ge(s_h, 1)
            dve.wait_ge(s_wr, 1)
            split(0, NT).then_inc(s_h3, 1)

            def general_onehots(n, q):
                with dve.Fori(0, EC) as c:
                    dve.wait_ge(g_mm, c + (n * EC + 1))
                    if q == 4:
                        v.tensor_copy(g_cx, g_cix[:, ds(c, 1)])
                    if q != 3:
                        v.tensor_copy(g_ix, (g_yix if q == 4 else g_src)[:, ds(c, 1)]).then_inc(
                            g_ixr, 1)
                    else:
                        v.tensor_scalar(g_toh, iota_f[0:EP, 0:R], g_typf[:, ds(c, 1)], None, ALU.is_equal)
                    here = g_dstf[:, ds(c, 1)]
                    if q in (0, 1, 3):
                        last = v.tensor_scalar(g_oh, g_iota, here, None, ALU.is_equal)
                    elif q == 4:
                        dve.wait_ge(g_wland, c * 16 + 16)
                        last = v.tensor_scalar(g_oh, g_iota, here, g_w, ALU.is_equal, ALU.mult)
                    else:
                        weight = (g_ew1 if q == 2 else g_ew)[:, ds(c, 1)]
                        last = v.tensor_scalar(g_oh, g_iota, here, weight, ALU.is_equal, ALU.mult)
                    last.then_inc(g_ohr, 1)

            def general_start():
                dve.wait_ge(g_rows, 80)
                dve.wait_ge(g_init, 1)
                v.memset(g_zero, 0.0)
                v.scalar_tensor_tensor(g_yix, g_src, float(R), g_typ, ALU.mult, ALU.add)
                gch.step(v.scalar_tensor_tensor(g_cix, g_typ, float(NPAD), g_dst, ALU.mult, ALU.add))
                gch.here()
                v.tensor_copy(g_iota, g_iota.bitcast(I32))
                v.tensor_copy(g_dstf, g_dst)
                gch.step(v.tensor_copy(g_typf, g_typ))
                gch.here()
                dve.wait_ge(g_ready, 1)
                v.tensor_scalar(g_ew, g_ew, tw[0:EP, 10:11], None, ALU.mult).then_inc(g_ready, 1)

            def fast_onehots():
                with dve.Fori(0, NBATCH // 4) as b:
                    for k in range(2):
                        onehots_bf16(b * (2 * HB) + k * HB, k, b * 4 + (2 * k + 2))

            def fast_weighted_onehots():
                dve.wait_ge(s_built, NBATCH + 4)
                dve.wait_ge(s_pdv, 2 * NT)
                v.tensor_copy(v_iota, iota_16[:, 0:RD, 0:VT]).then_inc(v_ready, 1)
                dve.wait_ge(v_ready, 1)

                def step(b, half):
                    dve.wait_ge(s_oh, b * 4 + NBATCH)
                    for f, of in enumerate((loB, keyB, ew1C)):
                        last = v.tensor_copy(nowA[:, :, f], of[:, ds(b * (4 * BS), 4 * BS)])
                    last.then_inc(s_nowa, 1)
                    dve.wait_ge(s_nowa, b + 1)
                    for k in range(4):
                        onehots_f32(b, k)
                    if half is None:
                        return
                    dve.wait_ge(v_used, b * VT + (VRING - VT))
                    v.tensor_tensor(v_eq, v_iota, colR[:, ds(b * VT + V0, VT), 1].unsqueeze(1).to_broadcast(
                        [P, RD, VT]), ALU.is_equal).then_inc(v_eqs, 1)
                    dve.wait_ge(v_eqs, b + 1)
                    v.tensor_tensor(v_oh[:, half], v_eq, ew1R[:, ds(b * VT + (V0 - VB * BLC), VT)].unsqueeze(
                        1).to_broadcast([P, RD, VT]), ALU.mult).then_inc(v_ohs, 1)

                with dve.Fori(0, VSTEPS // 2) as i:
                    for half in range(2):
                        step(i * 2 + half, half)
                for b in range(VSTEPS, ND * GB // 4):
                    step(b, None)

            for q in range(3):
                with dve.If(fast == 1):
                    if q == 0:
                        fast_onehots()
                    if q == 1:
                        dve.wait_ge(s_h3, 2)
                    if q == 2:
                        fast_weighted_onehots()
                with dve.Else():
                    if q == 0:
                        general_start()
                    general_onehots(q, q)
                for t in range(NT):
                    dve.wait_ge(s_pmm, q * NT + t + 1)
                    ps = bank[6 + t % 2][:, 0:F]
                    if q < 2:
                        v.scalar_tensor_tensor(H[:, t, :], ps, innorm[:, t:t + 1], (b1b, b2b)[q],
                                               ALU.mult, ALU.add).then_inc(s_pdv, 1)
                    else:
                        v.tensor_tensor(xN[:, t, :], xN[:, t, :], ps, ALU.add).then_inc(s_pdv, 1)
                if q == 0:
                    dve.wait_ge(s_h, 2)
                    split(0, NT).then_inc(s_h3, 1)

            dve.wait_ge(s_pdv, 3 * NT)
            for t in range(NT):
                last = v.bn_stats(stats[:, t, :], xN[:, t, :])
            ch.step(last)
            ch.here()
            for t in range(NT):
                last = v.bn_aggr(aggr[:, t, :], stats[:, t, :])
            ch.step(last)
            ch.here()
            v.tensor_scalar(sc1, aggr[:, :, 1], LN_EPS, None, ALU.add).then_inc(s_lnv, 1)
            dve.wait_ge(s_lns, 2)
            ch.step(v.reciprocal(lnscale, sc1))
            ch.here()
            v.scalar_tensor_tensor(lnbias, aggr[:, :, 0], -1.0, lnscale, ALU.mult, ALU.mult).then_inc(s_lnr, 1)
            dve.wait_ge(s_h, 3)
            split(0, NT).then_inc(s_h3, 1)
            v.tensor_tensor(biasb, biasb, tpbb, ALU.add).then_inc(s_wparts, 1)

            with dve.If(fast == 1):
                dve.wait_ge(s_table, 16)
                v.tensor_copy(iota_t.rearrange("p (d j) -> p d j", j=RJ), iota_16[:, 0:RD, 0:RJ]).then_inc(s_wparts, 1)
                dve.wait_ge(s_wparts, 2)

                def block_columns(b):
                    dve.wait_ge(s_ohr, b * len(BUF))
                    v.tensor_copy(now, colR[:, ds(b * BLC, BLC), :]).then_inc(s_now, 1)
                    dve.wait_ge(s_now, b * 5 + 1)
                    rest = now[:, :, 2]
                    for k in range(2):
                        v.tensor_copy(wpart[:, k, :], rest).then_inc(s_now, 1)
                        dve.wait_ge(s_now, b * 5 + (2 * k + 2))
                        v.tensor_tensor(rest, rest, wpart[:, k, :], ALU.subtract).then_inc(s_now, 1)
                        dve.wait_ge(s_now, b * 5 + (2 * k + 3))
                    v.tensor_copy(wpart[:, 2, :], rest)

                def onehots(b, u):
                    dve.wait_ge(s_used, b * BLC + (RING + RJ * (u - 1)))
                    n, to = u * RJ, BUF[u]
                    five = iota_t.rearrange("p (d j) -> p d j", j=RJ)
                    for oh, f in ((oh_typ, 3), (oh_rel, 1)):
                        last = v.tensor_tensor(oh[:, to, :].rearrange("p (d j) -> p d j", j=RJ), five,
                                               now[:, n:n + RJ, f].unsqueeze(1).to_broadcast([P, RD, RJ]), ALU.is_equal)
                    last.then_inc(s_rel, 1)
                    for j in range(RJ):
                        v.tensor_scalar(oh_seg[:, to, j, :], iota_h, now[:, n + j, 0:1], None, ALU.is_equal)
                    dve.wait_ge(s_rel, b * len(BUF) + (u + 1))
                    for k in range(3):
                        last = v.tensor_tensor(
                            oh_tim[:, to, k * RD * RJ:(k + 1) * RD * RJ].rearrange("p (d j) -> p d j", j=RJ),
                            oh_rel[:, to, :].rearrange("p (d j) -> p d j", j=RJ),
                            wpart[:, k, n:n + RJ].unsqueeze(1).to_broadcast([P, RD, RJ]), ALU.mult)
                    last.then_inc(s_ohr, 1)

                def result(b):
                    def there(k):
                        dve.wait_ge(s_fin, b * FS + (FS + k))
                        return k
                    dve.wait_ge(s_blk, b + 1)
                    mixed = bank[3]
                    v.scalar_tensor_tensor(fin[:, 0, :], mixed[:, F:2 * F], invdeg[:, ds(b, 1)], biasb, ALU.mult, ALU.add)
                    v.tensor_scalar(inv[:, 0, :], mixed[:, 2 * F:2 * F + R], 1.0, None, ALU.max).then_inc(s_fin, 1)
                    there(1)
                    v.tensor_tensor(fin[:, 1, :], mixed[:, 0:F], fin[:, 0, :], ALU.add)
                    v.reciprocal(inv[:, 1, :], inv[:, 0, :]).then_inc(s_fin, 1)
                    for r in range(R):
                        there(2 + r)
                        v.scalar_tensor_tensor(fin[:, r % 2, :], bank[4 + r // 4][:, (r % 4) * F:(r % 4 + 1) * F],
                                               inv[:, 1, r:r + 1], fin[:, (r + 1) % 2, :], ALU.mult,
                                               ALU.add).then_inc(s_fin, 1)
                    k = there(2 + R)
                    v.tensor_scalar(fin[:, 2, :], fin[:, (R - 1) % 2, :], 0.0, None, ALU.max).then_inc(s_fin, 1)
                    there(k + 1)
                    v.bn_stats(rowstat, fin[:, 2, :]).then_inc(s_fin, 1)
                    there(k + 2)
                    dve.sem_inc(s_gate2, 1)
                    v.bn_aggr(rowaggr, rowstat).then_inc(s_fin, 1)
                    there(k + 3)
                    v.tensor_scalar(rowsc[:, 0:1], rowaggr[:, 1:2], LN_EPS, None, ALU.add).then_inc(s_var, 1)
                    dve.wait_ge(s_rt, b + 1)
                    v.reciprocal(rowsc[:, 2:3], rowsc[:, 1:2]).then_inc(s_fin, 1)
                    there(k + 4)
                    v.tensor_scalar(fin[:, 3, :], fin[:, 2, :], rowaggr[:, 0:1], rowsc[:, 2:3], ALU.subtract,
                                    ALU.mult).then_inc(s_fin, 1)
                    there(k + 5)
                    v.tensor_tensor(fin[:, 4, :], fin[:, 3, :], gammab, ALU.mult).then_inc(s_fin, 1)
                    there(k + 6)
                    v.tensor_tensor(fin[:, 3, :], fin[:, 4, :], betab, ALU.add).then_inc(s_fin, 1)
                    assert there(k + 7) == FS

                def store(b):
                    dve.wait_ge(s_out, b * 16 + 16)
                    v.tensor_tensor(outt, fin[:, 3, :], xN[:, ds(b, 1), :].rearrange("p o f -> p (o f)"),
                                    ALU.add).then_inc(s_res, 1)

                dve.sem_inc(s_fin, FS)
                block_columns(0)
                for u in range(len(BUF)):
                    onehots(0, u)

                def onehots_block(b, chunks):
                    block_columns(b)
                    for u in range(chunks // RJ):
                        onehots(b, u)
                        if u == 2:
                            result(b - 1)
                            store(b - 1)

                with dve.Fori(1, NT - 1) as b:
                    onehots_block(b, BLC)
                onehots_block(NT - 1, LASTC)
                result(NT - 1)
                store(NT - 1)
            with dve.Else():
                GS = 9
                general_onehots(3, 3)
                dve.wait_ge(g_taken, 1)
                gch.step(v.tensor_scalar(aggT[0:R, :], aggT[0:R, :], 1.0, None, ALU.max))
                gch.here()
                v.reciprocal(aggT[0:R, :], aggT[0:R, :]).then_inc(g_inv, 1)
                general_onehots(4, 4)
                dve.wait_ge(g_tab, 64)
                for t in range(NT):
                    dve.wait_ge(g_trn, t + 1)
                    v.tensor_copy(H[:, t, :], bank[7][:, 0:F]).then_inc(g_rel, 1)
                general_onehots(5, 5)
                dve.sem_inc(g_res, 1)
                with dve.Fori(0, NT) as t:
                    def there(k):
                        dve.wait_ge(g_chain, t * GS + k)
                    dve.wait_ge(g_res, t + 1)
                    dve.wait_ge(g_blk, t + 1)
                    v.scalar_tensor_tensor(g_fin[:, 0, :], bank[7][:, F:2 * F], invdeg[:, ds(t, 1)], biasb, ALU.mult,
                                           ALU.add).then_inc(g_chain, 1)
                    there(1)
                    v.tensor_tensor(g_fin[:, 1, :], bank[7][:, 0:F], g_fin[:, 0, :], ALU.add).then_inc(g_chain, 1)
                    there(2)
                    v.tensor_tensor(g_fin[:, 2, :], g_fin[:, 1, :], H[:, ds(t, 1), :].rearrange("p o f -> p (o f)"),
                                    ALU.add).then_inc(g_chain, 1)
                    there(3)
                    v.tensor_scalar(g_fin[:, 3, :], g_fin[:, 2, :], 0.0, None, ALU.max).then_inc(g_chain, 1)
                    there(4)
                    v.bn_stats(rowstat, g_fin[:, 3, :]).then_inc(g_chain, 1)
                    there(5)
                    dve.sem_inc(s_gate2, 1)
                    v.bn_aggr(rowaggr, rowstat).then_inc(g_chain, 1)
                    there(6)
                    v.tensor_scalar(rowsc[:, 0:1], rowaggr[:, 1:2], LN_EPS, None, ALU.add).then_inc(g_var, 1)
                    dve.wait_ge(g_rt, t + 1)
                    v.reciprocal(rowsc[:, 2:3], rowsc[:, 1:2]).then_inc(g_chain, 1)
                    there(7)
                    v.tensor_scalar(g_fin[:, 4, :], g_fin[:, 3, :], rowaggr[:, 0:1], rowsc[:, 2:3], ALU.subtract,
                                    ALU.mult).then_inc(g_chain, 1)
                    there(8)
                    v.tensor_tensor(g_fin[:, 4, :], g_fin[:, 4, :], gammab, ALU.mult).then_inc(g_chain, 1)
                    there(9)
                    v.tensor_tensor(g_fin[:, 0, :], g_fin[:, 4, :], betab, ALU.add).then_inc(g_res2, 1)
                    dve.wait_ge(g_res2, t + 1)
                    dve.wait_ge(g_store, t * 16 + 16)
                    v.tensor_tensor(g_out, g_fin[:, 0, :], xN[:, ds(t, 1), :].rearrange("p o f -> p (o f)"),
                                    ALU.add).then_inc(g_res, 1)

        @block.scalar
        def _(act):
            a = nc.scalar
            act.wait_ge(s_wexp, 1)
            a.activation(tmp_rows.bitcast(F32), ew_rows, ACT.Exp, bias=tw[0:EP, 6:7], scale=tw[0:EP, 5:6],
                         accum_out=tw[0:EP, 7:8]).then_inc(s_twsum, 1)
            act.wait_ge(s_lnv, 1)
            act.wait_ge(s_sqd, 1)
            a.activation(sc2, sc2, ACT.Sqrt).then_inc(s_sqr, 1)
            a.activation(sc3, sc3, ACT.Sqrt)
            a.activation(sc1, sc1, ACT.Sqrt).then_inc(s_lns, 1)
            act.wait_ge(s_lnr, 1)
            for t in range(NT):
                last = a.activation(H[:, t, :], xN[:, t, :], ACT.Relu, bias=lnbias[:, t:t + 1],
                                    scale=lnscale[:, t:t + 1])
            last.then_inc(s_h, 1)
            act.wait_ge(s_slots, 16 * (3 * WT + 5))
            a.activation(ew16, ew16, ACT.Exp, bias=tw[0:RP, 6:7], scale=tw[0:RP, 5:6]).then_inc(s_wexp, 1)
            u = 0
            for to in (keyB, loB, ew1C):
                for t in range(WT):
                    act.wait_ge(s_tps, u + 1)
                    a.copy(to[:, t * CAP:(t + 1) * CAP].rearrange("p (w h) -> p h w", h=HALF),
                           bank[4 + u % 4][:, 0:CAP].rearrange("p (h w) -> p h w", h=HALF)).then_inc(s_tpf, 1)
                    u += 1
            for to in (colR[:, :, 0], colR[:, :, 1], colR[:, :, 2], colR[:, :, 3], srcC, ew1R):
                for k0 in range(0, RK, 4):
                    kn = min(4, RK - k0)
                    act.wait_ge(s_tps, u + 1)
                    for k in range(kn):
                        first = VB if to is ew1R else 0
                        last = a.copy(to.rearrange("p (b c k) -> p k c b", c=PIECES, k=RK)[:, k0 + k],
                                      bank[4 + u % 4][:, k * RP:(k + 1) * RP].rearrange(
                                          "p (c b) -> p c b", b=NT)[:, :, first:])
                    last.then_inc(s_tpf, 1)
                    u += 1
            act.wait_ge(s_tpf, 4 + u)
            act.sem_inc(s_cols, 1)
            act.wait_ge(s_wr, 1)
            fast = is_fast(act)

            def take(q, g, j):
                for k in range(4):
                    m = (min(q, 1) * NG + g) * GB + 4 * j + k
                    act.wait_ge(s_built, m + 5)
                    if j == 0 and k == 0 and q == 0 and g >= 4:
                        act.wait_ge(s_applied, 2 + g - 3)
                        act.wait_ge(spilled[g - 4], 16)
                    if j == 0 and k == 0 and q == 2:
                        act.wait_ge(s_applied, 2 * NG + max(g - 1, 0) + 2)
                    to = ATB[:, g % 4, :] if q == 0 else AT[:, g % 2, :]
                    a.copy(to[:, (4 * j + k) * BW * WC:(4 * j + k + 1) * BW * WC],
                           bank[k][:, 0:BW * WC]).then_inc(s_evac, 1)

            def take_agg(q, n):
                g = ORDER[q][n]
                act.wait_ge(s_applied, q * NG + n + 3)
                if q == 0 and n == 0:
                    act.wait_ge(s_h3, 1)
                if q == 1 and n == 0:
                    act.wait_ge(s_h3, 2)
                a.copy(aggT[:, g * GD:(g + 1) * GD], bank[4 + n % 2][:, 0:GD]).then_inc(s_agg, 1)

            def general_take(n, q):
                act.wait_ge(g_sum, n + 1)
                if q < 2:
                    act.wait_ge(s_h3, q + 1)
                rows = R if q == 3 else P
                for i, w in GBANKS:
                    last = a.copy(aggT[0:rows, 512 * i:512 * i + w], bank[i][0:rows, 0:w])
                return last

            def take_gathered(k):
                act.wait_ge(v_used, VRING + VLAST[k] + 1)
                a.copy(aggT[:, (ND + k) * GD:(ND + k + 1) * GD], bank[6 + k % 2][:, 0:GD]).then_inc(v_agg, 1)

            for q in range(3):
                with act.If(fast == 1):
                    groups = ND if q == 2 else NG
                    for g in range(groups):
                        for j in range(GB // 4):
                            if q != 1:
                                take(q, g, j)
                            for k in range(NG - ND - 1):
                                if q == 2 and g * (GB // 4) + j == VLAST[k] // VT + 1:
                                    take_gathered(k)
                        if g > 0:
                            take_agg(q, g - 1)
                    take_agg(q, groups - 1)
                    if q == 2:
                        take_gathered(NG - ND - 1)
                with act.Else():
                    if q == 0:
                        act.wait_ge(g_rows, 80)
                        a.activation(g_ew, g_ew, ACT.Exp, bias=tw[0:EP, 6:7], scale=tw[0:EP, 5:6]).then_inc(g_ready, 1)
                    general_take(q, q).then_inc(s_agg, ND if q == 2 else NG)
                    if q == 2:
                        act.sem_inc(v_agg, NG - ND)
                if q == 0:
                    for t in range(NT):
                        act.wait_ge(s_pdv, t + 1)
                        last = a.activation(H[:, t, :], H[:, t, :], ACT.Relu, scale=onorm[:, t:t + 1])
                    last.then_inc(s_h, 1)
            act.wait_ge(s_lnv, 2)
            a.activation(sc1, sc1, ACT.Sqrt).then_inc(s_lns, 1)
            act.wait_ge(s_lnr, 2)
            for t in range(NT):
                last = a.activation(H[:, t, :], xN[:, t, :], ACT.Relu, bias=lnbias[:, t:t + 1],
                                    scale=lnscale[:, t:t + 1])
            last.then_inc(s_h, 1)
            for t in range(NT):
                act.wait_ge(s_htp, t + 1)
                a.copy(h2T[:, t * P:(t + 1) * P], bank[4 + t % 2][:, 0:P]).then_inc(s_htd, 1)
            with act.If(fast == 1):
                act.wait_ge(s_h3, 3)
                a.copy(idxs, srcC[:, 0:BLC]).then_inc(s_idx, 4)

                def root_of(b):
                    act.wait_ge(s_var, b + 1)
                    a.activation(rowsc[:, 1:2], rowsc[:, 0:1], ACT.Sqrt).then_inc(s_rt, 1)

                def block(b, first, chunks):
                    for q in range(4):
                        if QFIRST[q] >= chunks:
                            break
                        if q == 0 and not first:
                            act.wait_ge(s_blk, b)
                        end = min(QLAST[q] + 1, chunks)
                        act.wait_ge(s_used, b * BLC + (RING + end))
                        a.copy(aggn[:, :, q * QD:(q + 1) * QD],
                               bank[q % 2].rearrange("p (d r) -> p r d", r=R)).then_inc(s_wind, 1)
                        if chunks == BLC:
                            i0 = IXEND[q - 1] if q else 0
                            a.copy(idxs[:, i0:IXEND[q]], srcC[:, ds(b * BLC + (BLC + i0), IXEND[q] - i0)]).then_inc(s_idx, 1)
                        if q == 0 and not first:
                            root_of(b - 1)
                    a.copy(timeT.rearrange("p k d -> p (k d)"), bank[2][:, 0:3 * P])
                    a.copy(cntT, bank[2][0:R, 3 * P:4 * P]).then_inc(s_timd, 1)
                    a.copy(h2Tt, h2T[:, ds(b * P, P)]).then_inc(s_timd, 1)

                block(0, True, BLC)
                with act.Fori(1, NT - 1) as b:
                    block(b, False, BLC)
                block(NT - 1, False, LASTC)
                root_of(NT - 1)
            with act.Else():
                act.sem_inc(g_ycopy, 2)
                with act.Fori(0, NT) as t:
                    act.wait_ge(g_ymm, t * (R // 4) + 1)
                    act.sem_inc(s_gate3, 1)
                    a.copy(g_tile, h2T[:, ds(t * P, P)]).then_inc(g_tcopy, 1)
                    for k in range(R // 4):
                        act.wait_ge(g_ymm, t * (R // 4) + (k + 2))
                        act.wait_ge(g_yout, t * (16 * (R // 4)) + 16 * (k + 1))
                        a.copy(g_y, bank[6 + k % 2]).then_inc(g_ycopy, 1)
                general_take(3, 3).then_inc(g_taken, 1)
                act.wait_ge(g_invd, 16)
                general_take(4, 4).then_inc(g_taken, 1)
                act.wait_ge(g_rel, NT)
                general_take(5, 5).then_inc(g_taken, 1)
                with act.Fori(0, NT) as t:
                    act.wait_ge(g_var, t + 1)
                    a.activation(rowsc[:, 1:2], rowsc[:, 0:1], ACT.Sqrt).then_inc(g_rt, 1)

        @block.tensor
        def _(pe):
            t_ = nc.tensor
            pe.wait_ge(s_const, 1)
            zero = ohlo[:, 0, 0:P]
            t_.matmul(bank[0][:, 0:NT], zero, iota_rep[:, 0, 0:NT], start=True, stop=False, skip_group_check=True)
            t_.matmul(bank[1][:, 0:NT], zero, iota_rep[:, 0, 0:NT], start=True, stop=False,
                      skip_group_check=True).then_inc(s_hmm, 2)

            def histogram_step(step, par, last_step=False):
                pe.wait_ge(s_hoh, step + 1)
                for c in range(HCOL):
                    for a in range(2):
                        lo = ohlo[:, 2 * par + a, :].rearrange("p (j c) -> p j c", c=HCOL)[:, :, c]
                        hi = ohhi[:, 2 * par + a, 0:NT * HCOL].rearrange("p (j c) -> p j c", c=HCOL)[:, :, c]
                        mm = t_.matmul(bank[a][:, 0:NT], lo, hi, start=False, stop=last_step and c == HCOL - 1,
                                       skip_group_check=True)
                mm.then_inc(s_hmm, 1)

            with pe.Fori(0, HSTEPS // 2) as i:
                for par in range(2):
                    histogram_step(i * 2 + par, par)
            histogram_step(HSTEPS - 1, 0, True)
            pe.wait_ge(s_deg, 1)
            t_.matmul(bank[2][:, 0:NT], upper, degin, start=True, stop=True)
            t_.matmul(bank[2][:, 64:64 + NT], onesf, degin, start=True, stop=True).then_inc(s_cumps, 1)
            pe.wait_ge(s_start, 1)
            t_.transpose(bank[3][0:NT, 0:P], lnbias, ident).then_inc(s_cumps, 1)
            pe.wait_ge(s_match, 1)
            pe.wait_ge(s_startT, 1)
            t_.matmul(bank[3][:, 0:2], onesf, matched[:, 0:2], start=True, stop=True).then_inc(s_matchps, 1)
            pe.sem_inc(s_tpf, 4)
            u = 0
            pe.wait_ge(s_win, 1)
            for of in (key5, lo5, ew15):
                for t in range(WT):
                    pe.wait_ge(s_tpf, u + 1)
                    for h in range(HALF):
                        mm = t_.transpose(bank[4 + u % 4][:, h * P:(h + 1) * P], of[:, t, h * P:(h + 1) * P], ident)
                    mm.then_inc(s_tps, 1)
                    u += 1
            for of in (seg16, rel16, ew16, tyf16, srf16, ew116):
                for k0 in range(0, RK, 4):
                    pe.wait_ge(s_tpf, u + 1)
                    for k in range(min(4, RK - k0)):
                        mm = t_.transpose(bank[4 + u % 4][:, k * RP:(k + 1) * RP], of[:, (k0 + k) * P:(k0 + k + 1) * P],
                                          ident[0:RP, 0:RP])
                    mm.then_inc(s_tps, 1)
                    u += 1

            fast = is_fast(pe)
            clear = iota_16.rearrange("p j c -> p (j c)")
            pe.sem_inc(s_built, 4)
            pe.sem_inc(s_applied, 2)
            pe.sem_inc(v_used, VRING)
            pe.wait_ge(s_cols, 1)

            def build(q, g, j):
                for k in range(4):
                    m = (min(q, 1) * NG + g) * GB + 4 * j + k
                    pe.wait_ge(s_oh, m + 1)
                    if m >= 4:
                        pe.wait_ge(s_evac, m - 3)
                    for w in range(BW):
                        for h in range(HALF):
                            c = HALF * w + h
                            if q == 0:
                                half, at16 = (m // 2) % 2, (m % 2) * BS + c
                                lo, dh = oh_lo_b[:, half, :, at16], oh_dh_b[:, half, :, at16]
                            else:
                                lo, dh = oh_lo[:, k % 2, c, :], oh_dh[:, k % 2, c, :]
                            mm = t_.matmul(bank[k][:, w * WC:(w + 1) * WC], lo, dh,
                                           start=(h == 0), stop=(h == HALF - 1))
                    mm.then_inc(s_built, 1)

            def apply(q, n, j):
                g = ORDER[q][n]
                gg = q * NG + n
                if j == 0:
                    if q != 1:
                        pe.wait_ge(s_evac, (min(q, 1) * NG + g + 1) * GB)
                    elif g < 4:
                        pe.wait_ge(reloaded[g], 16)
                    if gg >= 2:
                        pe.wait_ge(s_agg, gg - 1)
                    if q < 2:
                        pe.wait_ge(s_h3, q + 1)
                    else:
                        pe.wait_ge(s_pdv, 2 * NT)
                to = bank[4 + n % 2][:, 0:GD]
                if q < 2:
                    blocks = ATB[:, g % 4, :].rearrange("p (d s) -> p d s", s=NT)
                    for hi in range(5 * j, 5 * j + 5):
                        for k in range(3):
                            mm = t_.matmul(to, H3[:, hi, k * F:(k + 1) * F], blocks[:, :, hi],
                                           start=(hi == 0 and k == 0), stop=(hi == NT - 1 and k == 2))
                else:
                    blocks = AT[:, g % 2, :].rearrange("p (d s) -> p d s", s=NT)
                    for hi in range(5 * j, 5 * j + 5):
                        mm = t_.matmul(to, H[:, hi, :], blocks[:, :, hi], start=(hi == 0), stop=(hi == NT - 1))
                if j == 4:
                    mm.then_inc(s_applied, 1)

            def general_pass(n, q):
                if n == 0:
                    pe.sem_inc(g_mm, 1)
                    pe.wait_ge(g_ready, 2)
                if n in (1, 2):
                    pe.wait_ge(s_pdv, n * NT)
                if n == 3:
                    pe.wait_ge(g_ycopy, NT * (R // 4) + 2)
                if n > 3:
                    pe.wait_ge(g_taken, n - 3)
                if n == 5:
                    pe.wait_ge(g_rel, NT)
                rows = g_toh if q == 3 else g_row
                m = R if q == 3 else P
                for i, w in GBANKS:
                    t_.matmul(bank[i][0:m, 0:w], g_zero[:, 0:m], g_iota[:, 0:w], start=True, stop=False,
                              skip_group_check=True)
                with pe.Fori(0, EC) as c:
                    if q != 3:
                        pe.wait_ge(g_landed[q > 2], c * 16 + (16 * EC * (n if n < 3 else n - 4) + 16))
                    pe.wait_ge(g_ohr, c + (n * EC + 1))
                    for i, w in GBANKS:
                        mm = t_.matmul(bank[i][0:m, 0:w], rows, g_oh[:, 512 * i:512 * i + w], start=False, stop=False,
                                       skip_group_check=True)
                    mm.then_inc(g_mm, 1)
                pe.wait_ge(g_mm, (n + 1) * EC + 1)
                pe.sem_inc(g_sum, 1)

            def gathered(step):
                pe.wait_ge(v_ohs, step + 1)
                for n in range(step * VT, min((step + 1) * VT, VN)):
                    for k in range(NG - ND):
                        if VFIRST[k] == n:
                            if k == 2:
                                pe.wait_ge(v_agg, 1)
                            t_.matmul(bank[6 + k % 2][:, 0:GD], zerob, clear[:, 0:GD], start=True, stop=False,
                                      skip_group_check=True)
                    if n % RJ == 0:
                        pe.wait_ge(v_landed[n % VRING // RJ], 16 * (n // VRING * RJ + min(RJ, VN - n)))
                    for k in range(NG - ND):
                        d0, d1 = max(VBASE[n], k * GD), min(VBASE[n] + RD, (k + 1) * GD)
                        if d0 < d1:
                            mm = t_.matmul(bank[6 + k % 2][:, d0 - k * GD:d1 - k * GD], v_ring[:, n % VRING, :],
                                           v_oh[:, step % 2, d0 - VBASE[n]:d1 - VBASE[n], n - step * VT],
                                           start=False, stop=False, skip_group_check=True)
                    mm.then_inc(v_used, 1)

            for q in range(3):
                with pe.If(fast == 1):
                    groups = ND if q == 2 else NG
                    for g in range(groups + 1):
                        for j in range(GB // 4):
                            if g < groups and q != 1:
                                build(q, g, j)
                            if g > 0:
                                apply(q, g - 1, j)
                            if q == 2 and g * (GB // 4) + j < VSTEPS:
                                gathered(g * (GB // 4) + j)
                with pe.Else():
                    general_pass(q, q)
                pe.wait_ge(s_agg, q * NG + (ND if q == 2 else NG))
                if q == 2:
                    pe.wait_ge(v_agg, NG - ND)
                for t in range(NT):
                    if q * NT + t >= 2:
                        pe.wait_ge(s_pdv, q * NT + t - 1)
                    tile = aggT[:, t * P:(t + 1) * P]
                    if q < 2:
                        mm = t_.matmul(bank[6 + t % 2][:, 0:F], tile, (W1s, W2s)[q], start=True, stop=True)
                    else:
                        mm = t_.transpose(bank[6 + t % 2][:, 0:F], tile, ident)
                    mm.then_inc(s_pmm, 1)
            pe.wait_ge(s_h, 3)
            for t in range(NT):
                if t >= 2:
                    pe.wait_ge(s_htd, t - 1)
                t_.transpose(bank[4 + t % 2][:, 0:P], H[:, t, :], ident).then_inc(s_htp, 1)

            with pe.If(fast == 1):
                pe.wait_ge(s_htd, NT)
                pe.sem_inc(s_used, RING)
                pe.sem_inc(s_wind, 2)

                def chunk(b, n, first):
                    u, j = n // RJ, n % RJ
                    if j == 0:
                        pe.wait_ge(s_ohr, b * len(BUF) + (u + 1))
                    if n == 0:
                        if not first:
                            pe.wait_ge(s_timd, b * 2)
                        t_.matmul(bank[2], zerob, clear[:, 0:512], start=True, stop=False, skip_group_check=True)
                    for q in range(4):
                        if QFIRST[q] == n:
                            pe.wait_ge(s_wind, b * 4 + (q + 1))
                            t_.matmul(bank[q % 2], zerob, clear[:, 0:512], start=True, stop=False, skip_group_check=True)
                    if j == 0:
                        pe.wait_ge(landed[u], b * (16 * RJ) + 16 * RJ)
                    seg, d0 = oh_seg[:, BUF[u], j, :], RANGE[n]
                    tim = oh_tim[:, BUF[u], :].rearrange("p (k d j) -> p k d j", k=3, j=RJ)[:, :, :, j]
                    rel, typ = (oh[:, BUF[u], :].rearrange("p (d j) -> p d j", j=RJ)[:, :, j] for oh in (oh_rel, oh_typ))
                    for k in range(3):
                        row = ring[:, n, k * F:(k + 1) * F]
                        for q in range(4):
                            a0, a1 = max(d0, q * QD), min(d0 + RD, (q + 1) * QD)
                            if a0 < a1:
                                t_.matmul(bank[q % 2][:, (a0 - q * QD) * R:(a1 - q * QD) * R], row,
                                          seg[:, (a0 - d0) * R:(a1 - d0) * R], start=False, stop=False,
                                          skip_group_check=True)
                        t_.matmul(bank[2][:, 0:3 * P].rearrange("p (k d) -> p k d", d=P)[:, :, d0:d0 + RD], row, tim,
                                  start=False, stop=False, skip_group_check=True)
                    t_.matmul(bank[2][0:R, 3 * P + d0:3 * P + d0 + RD], typ, rel, start=False, stop=False,
                              skip_group_check=True).then_inc(s_used, 1)

                def block_product(b, chunks):
                    quarters = 4 if chunks == BLC else sum(n < chunks for n in QFIRST)
                    pe.wait_ge(s_wind, b * 4 + (quarters + 2))
                    pe.wait_ge(s_timd, b * 2 + 2)
                    pe.wait_ge(s_fin, b * FS + (R + 2))
                    mixed = bank[3]
                    t_.matmul(mixed[:, 0:F], h2Tt, roots, start=True, stop=True, skip_group_check=True)
                    for k in range(3):
                        t_.matmul(mixed[:, F:2 * F], timeT[:, k, :], tpws, start=(k == 0), stop=(k == 2),
                                  skip_group_check=True)
                    for r in range(R):
                        t_.matmul(bank[4 + r // 4][:, (r % 4) * F:(r % 4 + 1) * F], aggn[:, r, :], Wr[:, r, :],
                                  start=True, stop=True, skip_group_check=True)
                    mm = t_.matmul(mixed[:, 2 * F:2 * F + R], cntT, ident[0:R, 0:R], start=True, stop=True,
                                   skip_group_check=True)
                    mm.then_inc(s_blk, 1)

                def block(b, chunks):
                    for n in range(chunks):
                        chunk(b, n, False)
                        if n == RJ - 1:
                            block_product(b - 1, BLC)

                for n in range(BLC):
                    chunk(0, n, True)
                with pe.Fori(1, NT - 1) as b:
                    block(b, BLC)
                block(NT - 1, LASTC)
                block_product(NT - 1, LASTC)
            with pe.Else():
                pe.wait_ge(s_htd, NT)
                pe.sem_inc(g_ymm, 1)
                with pe.Fori(0, NT) as t:
                    pe.wait_ge(g_tcopy, t + 1)
                    for k in range(R // 4):
                        pe.wait_ge(g_ycopy, t * (R // 4) + (k + 1))
                        t_.matmul(bank[6 + k % 2], g_tile, Wr[:, 4 * k:4 * k + 4, :].rearrange("p r f -> p (r f)"),
                                  start=True, stop=True).then_inc(g_ymm, 1)
                general_pass(3, 3)
                general_pass(4, 4)
                pe.wait_ge(g_taken, 2)
                for t in range(NT):
                    pe.wait_ge(g_rel, t)
                    t_.transpose(bank[7][:, 0:F], aggT[:, t * P:(t + 1) * P], ident).then_inc(g_trn, 1)
                general_pass(5, 5)
                pe.wait_ge(g_taken, 3)
                for t in range(NT):
                    if t:
                        pe.wait_ge(g_chain, (t - 1) * 9 + 2)
                    t_.matmul(bank[7][:, 0:F], h2T[:, t * P:(t + 1) * P], roots, start=True, stop=True,
                              skip_group_check=True)
                    t_.matmul(bank[7][:, F:2 * F], aggT[:, t * P:(t + 1) * P], tpws, start=True, stop=True,
                              skip_group_check=True).then_inc(g_blk, 1)


_INS = ["x", "src", "dst", "edge_type_16", "edge_weight", "edge_weight1", "L0_gnn_W1", "L0_gnn_b1", "L0_gnn_W2",
        "L0_gnn_b2", "L1_gnn_basis", "L1_gnn_comp", "L1_gnn_root", "L1_gnn_bias", "L1_gnn_tp_w", "L1_gnn_tp_b",
        "L1_gnn_gamma", "L1_gnn_beta"]


def kernel(**inputs):
    import numpy as _np
    import concourse.bacc as _bacc
    from concourse import mybir as _mybir
    from concourse.bass_utils import run_bass_kernel_spmd as _run

    nc = _bacc.Bacc("TRN2", target_bir_lowering=False, num_devices=1)
    arrays, args = {}, []
    for name in _INS:
        a = _np.ascontiguousarray(inputs[name])
        arrays[f"in_{name}_dram"] = a
        args.append(nc.dram_tensor(f"in_{name}_dram", a.shape, _mybir.dt.from_np(a.dtype), kind="ExternalInput").ap())
    shape = _np.asarray(inputs["x"]).shape
    args.append(nc.dram_tensor("out_0_dram", shape, _mybir.dt.float32, kind="ExternalOutput").ap())
    gnn_kernel(nc, *args)
    r = _run(nc, [arrays], core_ids=[0])
    return r.results[0]["out_0_dram"]
```

```python
from contextlib import ExitStack

import concourse.bass as bass
from concourse import mybir

F32 = mybir.dt.float32
BF16 = mybir.dt.bfloat16
I32 = mybir.dt.int32
I16 = mybir.dt.int16
ALU = mybir.AluOpType
ACT = mybir.ActivationFunctionType
AX_X = mybir.AxisListType.X
RMAX = bass.bass_isa.ReduceOp.max
RADD = bass.bass_isa.ReduceOp.add
ds = bass.ds

P = 128
LN_EPS = 1e-5
TINY = 1e-8
DECAY = 0.1


class Chain:

    def __init__(self, eng, sem):
        self.eng, self.sem, self.n = eng, sem, 0

    def step(self, ins):
        self.n += 1
        ins.then_inc(self.sem, 1)

    def here(self):
        self.eng.wait_ge(self.sem, self.n)


def gnn_kernel(nc, x, src, dst, etype, eweight, eweight1, W1, b1, W2, b2, basis, comp, root, bias, tp_w, tp_b,
               gamma, beta, out):
    N, F = x.shape
    E = src.shape[0]
    NB = basis.shape[0]
    R = comp.shape[0]
    NT = (N + P - 1) // P
    NPAD = NT * P
    TP = NT // 5
    assert NT % 5 == 0
    POOLS = 1
    NLAST = N - (NT - 1) * P
    EP = 125
    EC = E // EP
    assert EP * EC == E and F == P

    WD = 5
    WC = WD * NT
    NW = NPAD // WD
    HALF = 2
    CAP = HALF * P
    WT = NW // P
    SLOTS = NW * HALF
    BW = 4
    BS = BW * HALF
    NBATCH = NW // BW
    NG = 8
    GB = NBATCH // NG
    GD = NPAD // NG
    GROUP = GB * BW * WC
    HB = 2 * BS
    ORDER = (tuple(range(NG)), (4, 5, 6, 7, 0, 1, 2, 3), tuple(range(NG)))

    RD = 16
    RC = R * RD
    PIECES = 5
    RK = 7
    BLC = PIECES * RK - 1
    RP = PIECES * NT
    RCAP = RK * P
    RSLOTS = NT * BLC
    PER = P * N / E
    STEP = round(RK * PER)
    FIRST = [round(PER * (k + 0.5)) - RD // 2 for k in range(RK)]
    RANGE = [max(0, min(P - RD, STEP * (n // RK) + FIRST[n % RK])) for n in range(BLC)]
    LASTC = 15
    PADN = (PIECES * RK + 1) * P
    RJ = 5
    BUF = (0, 1, 2, 0, 1, 2, 1)
    assert len(BUF) == -(-BLC // RJ) and LASTC % RJ == 0 and R == 16
    QD = P // 4
    QLAST = [max(n for n in range(BLC) if RANGE[n] // QD <= q) for q in range(4)]
    QFIRST = [min(n for n in range(BLC) if (RANGE[n] + RD - 1) // QD >= q) for q in range(4)]
    assert all(QFIRST[q] > QLAST[q - 2] for q in (2, 3)) and QLAST[3] == BLC - 1
    IXEND = [QLAST[0] + 1, QLAST[1] + 1, QLAST[2] + 1, BLC]
    RING = BLC
    ND = 5
    VD = ND * GD
    V0 = VD // P * BLC + min(n for n in range(BLC) if RANGE[n] + RD > VD % P)
    VN = (NT - 1) * BLC + LASTC - V0
    VB = VD // P
    VRING = 20
    DSTEPS = ND * GB // 4
    VT = VN // DSTEPS
    VSTEPS = DSTEPS + 1
    assert DSTEPS % 2 == 1 and VN <= VSTEPS * VT and V0 + VSTEPS * VT <= RSLOTS
    VBASE = [(V0 + n) // BLC * P + RANGE[(V0 + n) % BLC] - VD for n in range(VN)]
    VLAST = [max(n for n in range(VN) if VBASE[n] // GD <= k) for k in range(NG - ND)]
    VFIRST = [min(n for n in range(VN) if (VBASE[n] + RD - 1) // GD >= k) for k in range(NG - ND)]
    FS = R + 9

    HCOL = 33
    HSTEPS = EC // HCOL
    HL, HH = P // 2, 2 * NT

    padded = [nc.dram_tensor(f"padded_{n}_scratch", (E + PADN, 1), dt, kind="Internal").ap()
              for n, dt in (("dst", I32), ("src", I32), ("type", I32), ("ew", F32), ("ew1", F32))]
    start_dram = nc.dram_tensor("start_scratch", (NPAD,), F32, kind="Internal").ap()
    spill_dram = nc.dram_tensor("spill_scratch", (4, P, GROUP), BF16, kind="Internal").ap()
    table_dram = nc.dram_tensor("table_scratch", (NPAD, F), F32, kind="Internal").ap()
    y_dram = nc.dram_tensor("y_scratch", (NPAD, R * F), F32, kind="Internal").ap()
    inv_dram = nc.dram_tensor("inv_scratch", (R * NPAD,), F32, kind="Internal").ap()
    table3 = nc.dram_tensor("table3_scratch", (NPAD, 3 * F), BF16, kind="Internal").ap()

    def col(v):
        return v.rearrange("(e o) -> e o", o=1)

    src_col, dst_col = col(src), col(dst)

    with ExitStack() as ctx:
        def sb(name, shape, dt=F32):
            return ctx.enter_context(nc.sbuf_tensor(name, shape, dt))[tuple(slice(None) for _ in shape)]

        def sem(name):
            return ctx.enter_context(nc.semaphore("s_" + name))

        xN = sb("xN", [P, NT, F])
        H = sb("H", [P, NT, F])
        aggT = sb("aggT", [P, NPAD])
        H3 = sb("H3", [P, NT, 3 * F], BF16)
        loB, keyB = sb("loB", [P, SLOTS], BF16), sb("keyB", [P, SLOTS], BF16)
        ew1C = sb("ew1C", [P, SLOTS])
        colR = sb("colR", [P, RSLOTS, 4])
        srcC = sb("srcC", [P, RSLOTS], I32)
        ew1R = sb("ew1R", [P, RSLOTS - VB * BLC])
        W1s, W2s, roots, tpws = (sb(n, [P, F]) for n in ("W1s", "W2s", "roots", "tpws"))
        b1b, b2b, biasb, tpbb, gammab, betab = (sb(n, [P, F]) for n in ("b1b", "b2b", "biasb", "tpbb", "gammab", "betab"))
        Wr = sb("Wr", [P, R, F])
        ident = sb("ident", [P, P])
        onesf = sb("onesf", [P, P])
        zerob = sb("zerob", [P, P], BF16)
        upper = sb("upper", [P, P])
        hist = sb("hist", [HL, 2, HH])
        shifted = sb("shifted", [HL, P])
        iota_f = sb("iota_f", [P, P])
        iota_16 = sb("iota_16", [P, P, HB], BF16)
        iota_h = sb("iota_h", [P, RC], I16)
        degin, invdeg, innorm, onorm = (sb(n, [P, NT]) for n in ("degin", "invdeg", "innorm", "onorm"))
        lnscale, lnbias, sc1, sc2, sc3 = (sb(n, [P, NT]) for n in ("lnscale", "lnbias", "sc1", "sc2", "sc3"))
        stats = sb("stats", [P, NT, 6])
        aggr = sb("aggr", [P, NT, 2])
        st5, st16 = sb("st5", [P, WT]), sb("st16", [P, 1])
        ix5, ix16 = sb("ix5", [P, WT], I32), sb("ix16", [P, 1], I32)
        base5 = sb("base5", [P, WT])
        ibase = sb("ibase", [P, WT + 3], I32)
        piece = sb("piece", [P, 3])
        range16 = sb("range16", [P, RK])
        lastok = sb("lastok", [1, 1])
        compb = sb("compb", [P, R * NB])
        tw = sb("tw", [P, 12])
        matched = sb("matched", [P, 4])
        pad_dst, pad_zero = sb("pad_dst", [P, PADN // P], I32), sb("pad_zero", [P, PADN // P], I32)
        flag = sb("flag", [1, 1], I32)
        startT = sb("startT", [NT, P])
        rowstat = sb("rowstat", [P, 6])
        rowaggr = sb("rowaggr", [P, 2])
        rowsc = sb("rowsc", [P, 3])

        ARENA = 79 * 1024 // 4
        arena = sb("arena", [P, ARENA])
        at = [0]

        def carve(shape, dt=F32, reset=False):
            if reset:
                at[0] = 0
            n = 1
            for s in shape[1:]:
                n *= s
            w = n if dt in (F32, I32) else (n + 1) // 2
            v = arena[0:shape[0], at[0]:at[0] + w]
            at[0] += w
            assert at[0] <= ARENA, at[0]
            if dt is not F32:
                v = v.bitcast(dt)[:, 0:n]
            if len(shape) == 3:
                v = v.rearrange("p (a b) -> p a b", b=shape[2])
            elif len(shape) == 4:
                v = v.rearrange("p (a b c) -> p a b c", b=shape[2], c=shape[3])
            return v

        dst_rows = carve([EP, EC], I32, reset=True)
        src_rows = carve([EP, EC], I32)
        ew_rows = carve([EP, EC])
        tmp_rows = carve([EP, EC], I32)
        digits = carve([EP, 4, EC + 1], BF16)
        iota_rep = carve([EP, HL, HCOL], BF16)
        ohlo = carve([EP, 4, HL * HCOL], BF16)
        ohhi = carve([EP, 4, HH * HCOL], BF16)
        iota_i = carve([P, RC], I32)
        ramp_i = carve([P, P], I32)
        basis_s = carve([P, NB, F])
        basis_from = at[0] - NB * F
        dst5 = carve([P, WT, CAP], I32, reset=True)
        src5 = carve([P, WT, CAP], I32)
        ew15 = carve([P, WT, CAP])
        key5 = carve([P, WT, CAP])
        tmp5 = carve([P, WT, CAP], I32)
        dst16, src16, typ16 = (carve([RP, RCAP], I32) for _ in range(3))
        ew16, ew116, rel16, seg16 = (carve([RP, RCAP]) for _ in range(4))
        assert at[0] <= basis_from
        lo5 = tmp5.bitcast(F32)
        ok5 = dst5.bitcast(F32)
        ok16 = dst16.bitcast(F32)
        srf16, tyf16 = src16.bitcast(F32), typ16.bitcast(F32)
        AT = carve([P, 2, GROUP], reset=True)
        ATB = carve([P, 4, GROUP], BF16, reset=True)
        h2T = carve([P, NPAD], reset=True)
        h2T_end = at[0]
        ring = carve([P, RING, 3 * F], BF16)
        oh_seg = carve([P, 3, RJ, RC], BF16)
        oh_tim = carve([P, 3, 3 * RD * RJ], BF16)
        oh_rel = carve([P, 3, RD * RJ], BF16)
        oh_typ = carve([P, 3, RD * RJ], BF16)
        iota_t = carve([P, RD * RJ], BF16)
        now = carve([P, BLC, 4])
        wpart = carve([P, 3, BLC], BF16)
        idxs = carve([P, BLC], I32)
        aggn = carve([P, R, P])
        cntT = carve([R, P])
        inv = carve([P, 2, R])
        timeT = carve([P, 3, P])
        h2Tt = carve([P, P])
        fin = carve([P, 5, F])
        outt = carve([P, F])

        at[0] = h2T_end
        g_src, g_dst, g_typ = (carve([EP, EC], I32) for _ in range(3))
        g_ew, g_ew1 = carve([EP, EC]), carve([EP, EC])
        g_yix, g_cix = carve([EP, EC], I32), carve([EP, EC], I32)
        g_dstf, g_typf = g_dst.bitcast(F32), g_typ.bitcast(F32)
        g_oh = carve([EP, NPAD])
        g_iota = carve([EP, NPAD])
        g_row = carve([EP, F])
        g_ix, g_cx = carve([EP, 1], I32), carve([EP, 1], I32)
        g_w = carve([EP, 1])
        g_toh = carve([EP, R])
        g_zero = carve([EP, P])
        g_tile = carve([P, P])
        g_y = carve([P, 4 * F])
        g_fin = carve([P, 5, F])
        g_out = carve([P, F])

        oh_words = sb("oh_words", [P, 2 * BS * (P + WC)])
        oh_half = oh_words.bitcast(BF16)
        oh_lo_b = oh_half[:, 0:2 * HB * P].rearrange("p (a j c) -> p a j c", a=2, c=HB)
        oh_dh_b = oh_half[:, 2 * HB * P:].rearrange("p (a j c) -> p a j c", a=2, c=HB)

        w_lo = oh_half[:, 0:2 * BS * P].rearrange("p (a j c) -> p a j c", a=2, c=BS)
        w_dh = oh_half[:, 2 * BS * P:2 * BS * (P + 3 * WC)].rearrange("p (a k j c) -> p a k j c", a=2, k=3, c=BS)
        w_eq = sb("w_eq", [P, 2, WC * BS], BF16).rearrange("p a (j c) -> p a j c", c=BS)
        h3_words = H3.rearrange("p t f -> p (t f)").bitcast(F32)
        v_ring = h3_words[:, 0:VRING * F].rearrange("p (n f) -> p n f", f=F)
        v_oh, v_eq, v_iota = (h3_words[:, VRING * F + a * RD * VT:VRING * F + b * RD * VT]
                              for a, b in ((0, 2), (2, 3), (3, 4)))
        v_oh = v_oh.rearrange("p (a d j) -> p a d j", a=2, j=VT)
        v_eq, v_iota = (x_.rearrange("p (d j) -> p d j", j=VT) for x_ in (v_eq, v_iota))
        v_end = VRING * F + 4 * RD * VT + 2 * VRING
        v_ix = h3_words[:, v_end - 2 * VRING:v_end].bitcast(I32)
        WN = ND * GB * BS
        w_part = h3_words[:, v_end:v_end + 3 * WN // 2].bitcast(BF16).rearrange("p (k c) -> p k c", k=3)

        bank = [ctx.enter_context(nc.psum_tensor(f"bank{i}", [P, 512], F32))[:, :] for i in range(8)]

        s_rows, s_x, s_w, s_basis = sem("rows"), sem("x"), sem("w"), sem("basis")
        s_pad, s_iota, s_const, s_wr, s_poolch = sem("pad"), sem("iota"), sem("const"), sem("wr"), sem("poolch")
        s_hoh, s_hmm, s_deg, s_cum, s_cumps, s_start, s_startT = (
            sem(n) for n in ("hoh", "hmm", "deg", "cum", "cumps", "start", "startT"))
        s_sout, s_sin, s_ix, s_slots = sem("sout"), sem("sin"), sem("ix"), sem("slots")
        s_dve = sem("dve")
        s_twmax, s_twred, s_twsum, s_twred2 = sem("twmax"), sem("twred"), sem("twsum"), sem("twred2")
        s_sqd, s_sqr, s_lnv, s_lns, s_lnr, s_h = (sem(n) for n in ("sqd", "sqr", "lnv", "lns", "lnr", "h"))
        s_wexp, s_win, s_tps, s_tpf, s_cols, s_wparts = (sem(n) for n in ("wexp", "win", "tps", "tpf", "cols", "wparts"))
        s_oh, s_built, s_evac, s_applied, s_agg = (sem(n) for n in ("oh", "built", "evac", "applied", "agg"))
        s_pmm, s_pdv = sem("pmm"), sem("pdv")
        s_h3, s_table, s_htp, s_htd = sem("h3"), sem("table"), sem("htp"), sem("htd")
        s_idx, s_ohr, s_used, s_wind = (sem(n) for n in ("idx", "ohr", "used", "wind"))
        s_weq, s_wpart, s_now, s_rel = sem("weq"), sem("wpart"), sem("now"), sem("rel")
        s_gate, s_gate2, s_gate3 = sem("gate"), sem("gate2"), sem("gate3")
        s_timd, s_blk, s_fin, s_var, s_rt, s_res, s_out = (
            sem(n) for n in ("timd", "blk", "fin", "var", "rt", "res", "out"))
        v_tab, v_ixs, v_ready, v_eqs, v_ohs, v_used, v_agg = (
            sem(n) for n in ("v_tab", "v_ixs", "v_ready", "v_eqs", "v_ohs", "v_used", "v_agg"))
        v_landed = [sem(f"v_landed{i}") for i in range(VRING // RJ)]
        s_poolsplit, s_h3p = sem("poolsplit"), sem("h3p")
        s_hist, s_histps = sem("hist"), sem("histps")
        s_padded, s_pads = sem("padded"), sem("pads")
        landed = [sem(f"landed{i}") for i in range(len(BUF))]
        spilled = [sem(f"spilled{i}") for i in range(4)]
        reloaded = [sem(f"reloaded{i}") for i in range(4)]
        s_match, s_matchps, s_flag = sem("match"), sem("matchps"), sem("flag")
        g_rows, g_ready, g_tab, g_init = sem("g_rows"), sem("g_ready"), sem("g_tab"), sem("g_init")
        g_landed = sem("g_landed_first"), sem("g_landed_second")
        g_wland, g_ixr, g_ohr, g_mm, g_sum = (
            sem(n) for n in ("g_wland", "g_ixr", "g_ohr", "g_mm", "g_sum"))
        g_taken, g_inv, g_invd, g_tcopy, g_ymm, g_ycopy, g_yout = (
            sem(n) for n in ("g_taken", "g_inv", "g_invd", "g_tcopy", "g_ymm", "g_ycopy", "g_yout"))
        g_res2, g_dve = sem("g_res2"), sem("g_dve")
        g_trn, g_rel, g_blk, g_chain, g_var, g_rt, g_res, g_store = (
            sem(n) for n in ("g_trn", "g_rel", "g_blk", "g_chain", "g_var", "g_rt", "g_res", "g_store"))
        block = ctx.enter_context(nc.Block())

        GBANKS = [(i, min(512, NPAD - 512 * i)) for i in range((NPAD + 511) // 512)]

        def is_fast(eng):
            eng.wait_ge(s_flag, 1)
            return eng.value_load(flag[0:1, 0:1], min_val=0, max_val=1)

        left = aggT.rearrange("p (t f) -> p t f", f=F)

        def split(ch, e, t0, t1):
            w, r = H[:, t0:t1, :], left[:, t0:t1, :]
            ch.step(e.tensor_copy(H3[:, t0:t1, 0:F], w))
            ch.here()
            ch.step(e.tensor_tensor(r, w, H3[:, t0:t1, 0:F], ALU.subtract))
            ch.here()
            ch.step(e.tensor_copy(H3[:, t0:t1, F:2 * F], r))
            ch.here()
            ch.step(e.tensor_tensor(r, r, H3[:, t0:t1, F:2 * F], ALU.subtract))
            ch.here()
            return e.tensor_copy(H3[:, t0:t1, 2 * F:3 * F], r)

        @block.sync
        def _(sp):
            for t, d in ((dst_rows, dst), (src_rows, src), (ew_rows, eweight)):
                sp.dma_start(t, d.rearrange("(p c) -> p c", p=EP)).then_inc(s_rows, 16)
            edges = (col(dst), col(src), col(etype), col(eweight), eweight1)
            for to, of in zip(padded, edges):
                sp.dma_start(to[0:E, :].rearrange("(p c) o -> p (c o)", p=EP),
                             of.rearrange("(p c) o -> p (c o)", p=EP)).then_inc(s_padded, 16)
            sp.wait_ge(s_pads, 2)
            for to, pad in zip(padded, (pad_dst, pad_zero, pad_zero, pad_zero.bitcast(F32), pad_zero.bitcast(F32))):
                sp.dma_start(to[E:E + PADN, :].rearrange("(p c) o -> p (c o)", p=P), pad).then_inc(s_padded, 16)
            sp.wait_ge(s_pad, 1)
            sp.dma_start(xN[:, 0:NT - 1, :], x[0:(NT - 1) * P, :].rearrange("(t p) f -> p t f", p=P)).then_inc(s_x, 16)
            sp.dma_start(xN[0:NLAST, NT - 1, :], x[(NT - 1) * P:N, :]).then_inc(s_x, 16)
            sp.dma_start(basis_s, basis.rearrange("b i o -> i b o")).then_inc(s_basis, 16)
            sp.dma_start(compb, comp.rearrange("r b -> (r b)").partition_broadcast(P)).then_inc(s_basis, 16)
            for t, d in ((W1s, W1), (W2s, W2), (roots, root), (tpws, tp_w)):
                sp.dma_start(t, d).then_inc(s_w, 16)
            for t, d in ((b1b, b1), (b2b, b2), (biasb, bias), (tpbb, tp_b), (gammab, gamma), (betab, beta)):
                sp.dma_start(t, d.partition_broadcast(P)).then_inc(s_w, 16)
            sp.wait_ge(s_startT, 1)
            sp.dma_start(start_dram.rearrange("(h l) -> h l", l=P), startT).then_inc(s_sout, 16)
            sp.wait_ge(s_sout, 16)
            for t in range(WT):
                sp.dma_start(st5[:, t:t + 1], start_dram[t * P * WD:(t + 1) * P * WD].rearrange(
                    "(p o) -> p o", o=WD)[:, 0:1], allow_slow_non_contiguous=True).then_inc(s_sin, 16)
            for t in range(PIECES):
                sp.dma_start(st16[t * NT:(t + 1) * NT, :], start_dram.rearrange("(p o) -> p o", o=P)[:, 0:1],
                             allow_slow_non_contiguous=True).then_inc(s_sin, 16)
            fast = is_fast(sp)
            with sp.If(fast == 1):
                for g in range(4):
                    sp.wait_ge(s_evac, (g + 1) * GB)
                    sp.dma_start(spill_dram[g], ATB[:, g, :]).then_inc(spilled[g], 16)
                for g in range(4):
                    sp.wait_ge(s_applied, 2 + NG + g + 1)
                    sp.dma_start(ATB[:, g, :], spill_dram[g]).then_inc(reloaded[g], 16)
                sp.wait_ge(s_pdv, 2 * NT)
                sp.dma_start(table_dram.rearrange("(t p) f -> p t f", p=P), H).then_inc(v_tab, 16)
                for i in range(5):
                    if i == POOLS:
                        continue
                    sp.wait_ge(s_h3, 2 * 5 + i + 1 - (i > POOLS))
                    sp.dma_start(table3.rearrange("(t p) f -> p t f", p=P)[:, i * TP:(i + 1) * TP, :],
                                 H3[:, i * TP:(i + 1) * TP, :]).then_inc(s_table, 16)
                sp.wait_ge(s_h3p, 1)
                sp.dma_start(table3.rearrange("(t p) f -> p t f", p=P)[:, POOLS * TP:(POOLS + 1) * TP, :],
                             H3[:, POOLS * TP:(POOLS + 1) * TP, :]).then_inc(s_table, 16)
                sp.sem_inc(s_out, 16)
                with sp.Fori(0, NT - 1) as b:
                    sp.wait_ge(s_res, b + 1)
                    sp.dma_start(out[ds(b * P, P), :], outt).then_inc(s_out, 16)
                sp.wait_ge(s_res, NT)
                sp.dma_start(out[(NT - 1) * P:N, :], outt[0:NLAST, :]).then_inc(s_out, 16)
                sp.wait_ge(s_out, 16 + 16 * NT)
            with sp.Else():
                sp.wait_ge(s_cols, 1)
                for t, d in ((g_src, src), (g_dst, dst), (g_typ, etype), (g_ew, eweight),
                             (g_ew1, eweight1.rearrange("e o -> (e o)"))):
                    sp.dma_start(t, d.rearrange("(p c) -> p c", p=EP)).then_inc(g_rows, 16)
                nodes = table_dram.rearrange("(t p) f -> p t f", p=P)
                for q in range(4):
                    if q == 2:
                        sp.wait_ge(s_pdv, 2 * NT)
                    else:
                        sp.wait_ge(s_h, 5 * (min(q, 2) + 1))
                    sp.dma_start(nodes, H).then_inc(g_tab, 16)
                sp.sem_inc(g_yout, 16)
                with sp.Fori(0, NT) as t:
                    for k in range(R // 4):
                        sp.wait_ge(g_ycopy, t * (R // 4) + (k + 3))
                        sp.dma_start(y_dram[ds(t * P, P), k * 4 * F:(k + 1) * 4 * F], g_y).then_inc(g_yout, 16)
                sp.wait_ge(g_inv, 1)
                sp.dma_start(inv_dram.rearrange("(r n) -> r n", r=R), aggT[0:R, :]).then_inc(g_invd, 16)
                sp.sem_inc(g_store, 16)
                with sp.Fori(0, NT - 1) as b:
                    sp.wait_ge(g_res, b + 2)
                    sp.dma_start(out[ds(b * P, P), :], g_out).then_inc(g_store, 16)
                sp.wait_ge(g_res, NT + 1)
                sp.dma_start(out[(NT - 1) * P:N, :], g_out[0:NLAST, :]).then_inc(g_store, 16)
                sp.wait_ge(g_store, 16 + 16 * NT)

        @block.gpsimd
        def _(pool):
            g = nc.gpsimd
            ch = Chain(pool, s_poolch)
            g.memset(xN[:, NT - 1, :], 0.0).then_inc(s_pad, 1)
            g.iota(iota_i, [[1, RC]], base=0, channel_multiplier=0).then_inc(s_iota, 1)
            g.iota(ramp_i, [[1, P]], base=0, channel_multiplier=-1).then_inc(s_iota, 1)
            g.iota(ibase[:, 0:WT], [[P * WD, WT]], base=0, channel_multiplier=WD).then_inc(s_iota, 1)
            g.iota(ibase[:, WT:WT + 1], [[0, 1]], base=0, channel_multiplier=(1 << 17) // NT + 1).then_inc(s_iota, 1)
            g.iota(ibase[:, WT + 1:WT + 2], [[0, 1]], base=0, channel_multiplier=1).then_inc(s_iota, 1)
            g.memset(pad_dst, 1 << 20).then_inc(s_pads, 1)
            g.memset(pad_zero, 0).then_inc(s_pads, 1)
            pool.wait_ge(s_basis, 32)
            prod = aggT[:, 0:R * F].rearrange("p (r f) -> p r f", f=F)
            cb = compb.rearrange("p (r b) -> p r b", b=NB)
            for b in range(NB):
                first = basis_s[:, b, :].unsqueeze(1).to_broadcast([P, R, F])
                coef = cb[:, :, b:b + 1].to_broadcast([P, R, F])
                if b == 0:
                    ch.step(g.tensor_tensor(Wr, first, coef, ALU.mult))
                    ch.here()
                    continue
                ch.step(g.tensor_tensor(prod, first, coef, ALU.mult))
                ch.here()
                ch.step(g.tensor_tensor(Wr, Wr, prod, ALU.add))
                ch.here()
                if b == 4:
                    pool.wait_ge(s_twmax, 1)
                    g.partition_all_reduce(tw[0:EP, 2:4], tw[0:EP, 0:2], EP, RMAX).then_inc(s_twred, 1)
                if b == 6:
                    pool.wait_ge(s_twsum, 1)
                    g.partition_all_reduce(tw[0:EP, 8:9], tw[0:EP, 7:8], EP, RADD).then_inc(s_twred2, 1)
            pool.sem_inc(s_wr, 1)
            pool.wait_ge(s_ix, 1)
            for t in range(WT):
                for to, of in ((dst5, dst_col), (src5, src_col), (ew15, eweight1)):
                    g.indirect_dma_start(to[:, t, :], None, of,
                                         bass.IndirectOffsetOnAxis(ap=ix5[:, t:t + 1], axis=0)).then_inc(s_slots, 16)
            pool.wait_ge(s_padded, 16 * 10)
            for to, of in zip((dst16, src16, typ16, ew16, ew116), padded):
                g.indirect_dma_start(to, None, of,
                                     bass.IndirectOffsetOnAxis(ap=ix16[0:RP, 0:1], axis=0)).then_inc(s_slots, 16)
            fast = is_fast(pool)
            with pool.If(fast == 1):
                pool.wait_ge(v_tab, 16)

                def gather(i, half, count):
                    pool.wait_ge(v_used, i * (2 * VRING) + (half * VRING + RJ))
                    g.tensor_copy(v_ix[:, half * VRING:half * VRING + count],
                                  srcC[:, ds(i * (2 * VRING) + (V0 + half * VRING), count)]).then_inc(v_ixs, 1)
                    pool.wait_ge(v_ixs, i * 2 + (half + 1))
                    for n in range(count):
                        if n % RJ == 0:
                            pool.wait_ge(v_used, i * (2 * VRING) + (half * VRING + n + RJ))
                            pool.sem_inc(s_gate, 1)
                        g.indirect_dma_start(v_ring[:, n, :], None, table_dram, bass.IndirectOffsetOnAxis(
                            ap=v_ix[:, half * VRING + n:half * VRING + n + 1], axis=0)).then_inc(v_landed[n // RJ], 16)

                with pool.Fori(0, VN // (2 * VRING)) as i:
                    for half in range(2):
                        gather(i, half, VRING)
                whole = VN // (2 * VRING)
                for half in range(2):
                    if VN > whole * 2 * VRING + half * VRING:
                        gather(whole, half, min(VRING, VN - whole * 2 * VRING - half * VRING))
                pool.wait_ge(s_h, 2 * 5 + POOLS + 1)
                split(Chain(pool, s_poolsplit), g, POOLS * TP, (POOLS + 1) * TP).then_inc(s_h3p, 1)
                pool.wait_ge(s_table, 16 * 5)

                def gather_block(b, chunks):
                    for n in range(chunks):
                        if n == 0 or n in IXEND:
                            pool.wait_ge(s_idx, b * 4 + (sum(n >= e for e in IXEND) + 1))
                            pool.sem_inc(s_gate, 1)
                        if n % RJ == 0:
                            pool.wait_ge(s_used, b * BLC + min(n + RJ, BLC))
                            pool.sem_inc(s_gate, 1)
                        g.indirect_dma_start(ring[:, n, :], None, table3,
                                             bass.IndirectOffsetOnAxis(ap=idxs[:, n:n + 1], axis=0)
                                             ).then_inc(landed[n // RJ], 16)

                with pool.Fori(0, NT - 1) as b:
                    gather_block(b, BLC)
                gather_block(NT - 1, LASTC)
            with pool.Else():
                y_rows = y_dram.rearrange("n (r f) -> (n r) f", f=F)
                pool.wait_ge(s_cols, 1)
                g.iota(g_iota.bitcast(I32), [[1, NPAD]], base=0, channel_multiplier=0).then_inc(g_init, 1)
                for n, q in enumerate((0, 1, 2, 4, 5)):
                    if q < 4:
                        pool.wait_ge(g_tab, 16 * (q + 1))
                    elif q == 4:
                        pool.wait_ge(g_tab, 16 * 4)
                        pool.wait_ge(g_yout, 16 + 16 * NT * (R // 4))
                        pool.wait_ge(g_invd, 16)
                    with pool.Fori(0, EC) as c:
                        pool.wait_ge(g_ixr, c + (n * EC + 1))
                        pool.sem_inc(s_gate, 1)
                        if q == 4:
                            g.indirect_dma_start(g_w, None, col(inv_dram),
                                                 bass.IndirectOffsetOnAxis(ap=g_cx, axis=0)).then_inc(g_wland, 16)
                        g.indirect_dma_start(g_row, None, y_rows if q == 4 else table_dram,
                                             bass.IndirectOffsetOnAxis(ap=g_ix, axis=0)).then_inc(g_landed[q > 2], 16)

        @block.vector
        def _(dve):
            v = nc.vector
            ch, gch = Chain(dve, s_dve), Chain(dve, g_dve)
            v.memset(matched, 0.0)
            dve.wait_ge(s_iota, 5)
            v.tensor_copy(base5, ibase[:, 0:WT])
            ch.step(v.tensor_scalar(ibase[:, WT + 2:WT + 3], ibase[:, WT:WT + 1], 17, None, ALU.logical_shift_right))
            ch.here()
            v.tensor_copy(piece[:, 0:1], ibase[:, WT + 2:WT + 3])
            ch.step(v.tensor_scalar(piece[:, 1:2], ibase[:, WT + 1:WT + 2], float(P), None, ALU.mult))
            ch.here()
            for k in range(RK):
                v.tensor_scalar(range16[:, k:k + 1], piece[:, 0:1], float(STEP), float(FIRST[k]), ALU.mult, ALU.add)
            ch.step(v.scalar_tensor_tensor(piece[:, 2:3], piece[:, 0:1], -float(NT * P), piece[:, 1:2],
                                           ALU.mult, ALU.add))
            ch.here()
            ch.step(v.tensor_scalar(range16, range16, 0.0, float(P - RD), ALU.max, ALU.min))
            ch.here()
            ch.step(v.tensor_scalar(piece[:, 1:2], piece[:, 0:1], float(PIECES - 1), float(1 << 21), ALU.is_equal,
                                    ALU.mult))
            ch.here()
            ch.step(v.tensor_scalar(range16, range16, piece[:, 2:3], None, ALU.add))
            ch.here()
            v.tensor_tensor(range16[:, RK - 1:RK], range16[:, RK - 1:RK], piece[:, 1:2], ALU.add)
            v.tensor_copy(iota_f, iota_i[:, 0:P])
            v.tensor_copy(iota_16, iota_i[:, 0:P].unsqueeze(2).to_broadcast([P, P, HB]))
            v.tensor_copy(iota_h, iota_i)
            v.memset(onesf, 1.0)
            v.memset(zerob, 0.0)
            v.memset(ohlo[:, 0, 0:HL], 0.0)
            v.tensor_copy(iota_rep, iota_i[0:EP, 0:HL].unsqueeze(2).to_broadcast([EP, HL, HCOL]))
            v.tensor_scalar(shifted, ramp_i[0:HL, :], HL, None, ALU.is_equal)
            v.tensor_scalar(ident, ramp_i, 0, None, ALU.is_equal)
            v.tensor_scalar(upper, ramp_i, 0, None, ALU.is_gt).then_inc(s_const, 1)
            dve.wait_ge(s_rows, 48)
            for a, rows in enumerate((dst_rows, src_rows)):
                ch.step(v.tensor_scalar(tmp_rows, rows, HL - 1, None, ALU.bitwise_and))
                ch.here()
                ch.step(v.tensor_copy(digits[:, 2 * a, 0:EC], tmp_rows))
                ch.here()
                ch.step(v.tensor_scalar(tmp_rows, rows, 6, None, ALU.logical_shift_right))
                ch.here()
                ch.step(v.tensor_copy(digits[:, 2 * a + 1, 0:EC], tmp_rows))
                ch.here()
            v.tensor_reduce(tw[0:EP, 0:1], ew_rows, AX_X, ALU.max)
            ch.step(v.tensor_reduce(tw[0:EP, 1:2], ew_rows, AX_X, ALU.min))
            ch.here()
            v.tensor_scalar(tw[0:EP, 1:2], tw[0:EP, 1:2], -1.0, None, ALU.mult).then_inc(s_twmax, 1)

            def histogram_step(step, par):
                dve.wait_ge(s_hmm, step + 1)
                for a in range(2):
                    lo = digits[:, 2 * a, ds(step * HCOL, HCOL)]
                    hi = digits[:, 2 * a + 1, ds(step * HCOL, HCOL)]
                    v.tensor_tensor(ohlo[:, 2 * par + a, :].rearrange("p (j c) -> p j c", c=HCOL), iota_rep,
                                    lo.unsqueeze(1).to_broadcast([EP, HL, HCOL]), ALU.is_equal)
                    last = v.tensor_tensor(ohhi[:, 2 * par + a, :].rearrange("p (j c) -> p j c", c=HCOL),
                                           iota_rep[:, 0:HH, :], hi.unsqueeze(1).to_broadcast([EP, HH, HCOL]),
                                           ALU.is_equal)
                last.then_inc(s_hoh, 1)

            with dve.Fori(0, HSTEPS // 2) as i:
                for par in range(2):
                    histogram_step(i * 2 + par, par)
            histogram_step(HSTEPS - 1, 0)

            dve.wait_ge(s_twred, 1)
            ch.step(v.tensor_tensor(tw[0:EP, 4:5], tw[0:EP, 2:3], tw[0:EP, 3:4], ALU.add))
            ch.here()
            ch.step(v.tensor_scalar(tw[0:EP, 4:5], tw[0:EP, 4:5], TINY, None, ALU.add))
            ch.here()
            ch.step(v.reciprocal(tw[0:EP, 4:5], tw[0:EP, 4:5]))
            ch.here()
            ch.step(v.tensor_scalar(tw[0:EP, 5:6], tw[0:EP, 4:5], DECAY, None, ALU.mult))
            ch.here()
            v.scalar_tensor_tensor(tw[0:EP, 6:7], tw[0:EP, 5:6], -1.0, tw[0:EP, 2:3], ALU.mult,
                                   ALU.mult).then_inc(s_wexp, 1)

            dve.wait_ge(s_x, 32)
            for t in range(NT):
                last = v.bn_stats(stats[:, t, :], xN[:, t, :])
            ch.step(last)
            ch.here()
            for t in range(NT):
                last = v.bn_aggr(aggr[:, t, :], stats[:, t, :])
            ch.step(last)
            ch.here()
            v.tensor_scalar(sc1, aggr[:, :, 1], LN_EPS, None, ALU.add).then_inc(s_lnv, 1)

            dve.wait_ge(s_hmm, 2 + HSTEPS)
            for a in range(2):
                last = v.tensor_copy(hist[:, a, :], bank[a][0:HL, 0:HH])
            last.then_inc(s_hist, 1)
            dve.wait_ge(s_histps, 1)
            v.tensor_copy(degin, bank[4][:, 0:NT]).then_inc(s_deg, 1)
            v.tensor_scalar(sc2, bank[4][:, 0:NT], 1.0, None, ALU.max)
            ch.step(v.tensor_scalar(sc3, bank[4][:, NT:2 * NT], 1.0, None, ALU.max))
            ch.here()
            v.reciprocal(invdeg, sc2).then_inc(s_sqd, 1)
            dve.wait_ge(s_cumps, 1)
            ch.step(v.tensor_copy(innorm, bank[2][:, 64:64 + NT]))
            ch.here()
            ch.step(v.tensor_tensor_scan(onorm, onesf[:, 0:NT], innorm, 0.0, ALU.mult, ALU.add))
            ch.here()
            ch.step(v.tensor_tensor(onorm, onorm, innorm, ALU.subtract))
            ch.here()
            v.tensor_tensor(lnbias, onorm, bank[2][:, 0:NT], ALU.add).then_inc(s_start, 1)
            dve.wait_ge(s_start, 1)
            v.tensor_scalar(lastok, lnbias[0:1, NT - 1:NT], float(E - LASTC * P), None, ALU.is_ge)
            dve.wait_ge(s_cumps, 2)
            v.tensor_copy(startT, bank[3][0:NT, 0:P]).then_inc(s_startT, 1)
            dve.wait_ge(s_sqr, 1)
            v.reciprocal(innorm, sc2)
            dve.wait_ge(s_lns, 1)
            v.reciprocal(onorm, sc3)
            ch.step(v.reciprocal(sc1, sc1))
            ch.here()
            ch.step(v.tensor_tensor(lnscale, sc1, onorm, ALU.mult))
            ch.here()
            v.scalar_tensor_tensor(lnbias, aggr[:, :, 0], -1.0, lnscale, ALU.mult, ALU.mult).then_inc(s_lnr, 1)

            dve.wait_ge(s_sin, 16 * (WT + PIECES))
            v.tensor_scalar(ix5, st5, float(E - CAP), None, ALU.min)
            ch.step(v.scalar_tensor_tensor(st16[0:RP, :], piece[0:RP, 0:1], float(RCAP), st16[0:RP, :],
                                           ALU.mult, ALU.add))
            ch.here()
            v.tensor_scalar(ix16[0:RP, :], st16[0:RP, :], float(E + PADN - RCAP), None, ALU.min).then_inc(s_ix, 1)

            def split_pieces(table):
                for i in range(5):
                    dve.wait_ge(s_h, 5 * table + i + 1)
                    split(ch, v, i * TP, (i + 1) * TP).then_inc(s_h3, 1)

            dve.wait_ge(s_wr, 1)
            split_pieces(0)

            dve.wait_ge(s_slots, 16 * (3 * WT + 5))
            for t in range(WT):
                last = v.tensor_scalar(key5[:, t, :], dst5[:, t, :], base5[:, t:t + 1], float(NT),
                                       ALU.subtract, ALU.mult)
            v.tensor_scalar(tmp5, src5, 7, None, ALU.logical_shift_right)
            for k in range(RK):
                v.tensor_scalar(rel16[:, k * P:(k + 1) * P], dst16[:, k * P:(k + 1) * P], range16[0:RP, k:k + 1], None,
                                ALU.subtract)
            ch.step(v.tensor_scalar(src5, src5, P - 1, None, ALU.bitwise_and))
            ch.here()
            v.scalar_tensor_tensor(seg16, rel16, float(R), typ16, ALU.mult, ALU.add)
            v.tensor_scalar(ok16, rel16, 0.0, None, ALU.is_ge)
            ch.step(v.tensor_tensor(key5, key5, tmp5, ALU.add))
            ch.here()
            v.scalar_tensor_tensor(ok16, rel16, float(RD), ok16, ALU.is_lt, ALU.mult)
            v.tensor_copy(srf16, src16)
            v.tensor_copy(tyf16, typ16)
            v.tensor_scalar(ok5, key5, 0.0, None, ALU.is_ge)
            ch.step(v.tensor_copy(lo5, src5))
            ch.here()
            v.scalar_tensor_tensor(ok5, key5, float(WC), ok5, ALU.is_lt, ALU.mult)
            ch.step(v.scalar_tensor_tensor(seg16, seg16, 1.0, ok16, ALU.add, ALU.mult))
            ch.here()
            v.scalar_tensor_tensor(key5, key5, 1.0, ok5, ALU.add, ALU.mult)
            v.tensor_reduce(matched[:, 0:1], ok5.rearrange("p t c -> p (t c)"), AX_X, ALU.add)
            v.tensor_reduce(matched[0:RP, 1:2], ok16, AX_X, ALU.add).then_inc(s_match, 1)
            ch.step(v.tensor_scalar(seg16, seg16, -1.0, None, ALU.add))
            ch.here()
            ch.step(v.tensor_scalar(key5, key5, -1.0, None, ALU.add))
            ch.here()
            dve.wait_ge(s_twred2, 1)
            ch.step(v.tensor_scalar(tw[0:EP, 9:10], tw[0:EP, 8:9], TINY, None, ALU.add))
            ch.here()
            ch.step(v.reciprocal(tw[0:EP, 10:11], tw[0:EP, 9:10]))
            ch.here()
            dve.wait_ge(s_wexp, 2)
            v.tensor_scalar(ew16, ew16, tw[0:RP, 10:11], None, ALU.mult).then_inc(s_win, 1)
            dve.wait_ge(s_matchps, 1)
            ch.step(v.tensor_scalar(matched[0:1, 2:4], bank[3][0:1, 0:2], float(E), None, ALU.is_equal))
            ch.here()
            ch.step(v.tensor_tensor(lastok, lastok, matched[0:1, 2:3], ALU.mult))
            ch.here()
            v.tensor_tensor(flag, lastok, matched[0:1, 3:4], ALU.mult).then_inc(s_flag, 1)
            fast = is_fast(dve)

            def onehots_bf16(c0, half, n):
                dve.wait_ge(s_built, n)
                v.tensor_tensor(oh_lo_b[:, half], iota_16, loB[:, ds(c0, HB)].unsqueeze(1).to_broadcast([P, P, HB]),
                                ALU.is_equal)
                v.tensor_tensor(oh_dh_b[:, half], iota_16[:, 0:WC, :],
                                keyB[:, ds(c0, HB)].unsqueeze(1).to_broadcast([P, WC, HB]),
                                ALU.is_equal).then_inc(s_oh, 2)

            def onehots_weighted(b, k):
                c0 = b * (4 * BS) + k * BS
                small = iota_16[:, :, 0:BS]
                dve.wait_ge(s_built, b * 4 + (NBATCH + 4 + k - 1))
                dve.wait_ge(s_oh, b * 4 + (NBATCH + k - 1))
                v.tensor_tensor(w_eq[:, k % 2], small[:, 0:WC, :],
                                keyB[:, ds(c0, BS)].unsqueeze(1).to_broadcast([P, WC, BS]),
                                ALU.is_equal).then_inc(s_weq, 1)
                v.tensor_tensor(w_lo[:, k % 2], small, loB[:, ds(c0, BS)].unsqueeze(1).to_broadcast([P, P, BS]),
                                ALU.is_equal)
                dve.wait_ge(s_weq, b * 4 + (k + 1))
                for part in range(3):
                    last = v.tensor_tensor(w_dh[:, k % 2, part], w_eq[:, k % 2], w_part[:, part, ds(c0, BS)].unsqueeze(
                        1).to_broadcast([P, WC, BS]), ALU.mult)
                last.then_inc(s_oh, 1)

            dve.wait_ge(s_cols, 1)

            def general_onehots(n, q):
                with dve.Fori(0, EC) as c:
                    dve.wait_ge(g_mm, c + (n * EC + 1))
                    if q == 4:
                        v.tensor_copy(g_cx, g_cix[:, ds(c, 1)])
                    if q != 3:
                        v.tensor_copy(g_ix, (g_yix if q == 4 else g_src)[:, ds(c, 1)]).then_inc(
                            g_ixr, 1)
                    else:
                        v.tensor_scalar(g_toh, iota_f[0:EP, 0:R], g_typf[:, ds(c, 1)], None, ALU.is_equal)
                    here = g_dstf[:, ds(c, 1)]
                    if q in (0, 1, 3):
                        last = v.tensor_scalar(g_oh, g_iota, here, None, ALU.is_equal)
                    elif q == 4:
                        dve.wait_ge(g_wland, c * 16 + 16)
                        last = v.tensor_scalar(g_oh, g_iota, here, g_w, ALU.is_equal, ALU.mult)
                    else:
                        weight = (g_ew1 if q == 2 else g_ew)[:, ds(c, 1)]
                        last = v.tensor_scalar(g_oh, g_iota, here, weight, ALU.is_equal, ALU.mult)
                    last.then_inc(g_ohr, 1)

            def general_start():
                dve.wait_ge(g_rows, 80)
                dve.wait_ge(g_init, 1)
                v.memset(g_zero, 0.0)
                v.scalar_tensor_tensor(g_yix, g_src, float(R), g_typ, ALU.mult, ALU.add)
                gch.step(v.scalar_tensor_tensor(g_cix, g_typ, float(NPAD), g_dst, ALU.mult, ALU.add))
                gch.here()
                v.tensor_copy(g_iota, g_iota.bitcast(I32))
                v.tensor_copy(g_dstf, g_dst)
                gch.step(v.tensor_copy(g_typf, g_typ))
                gch.here()
                dve.wait_ge(g_ready, 1)
                v.tensor_scalar(g_ew, g_ew, tw[0:EP, 10:11], None, ALU.mult).then_inc(g_ready, 1)

            def fast_onehots():
                with dve.Fori(0, NBATCH // 4) as b:
                    for k in range(2):
                        onehots_bf16(b * (2 * HB) + k * HB, k, b * 4 + (2 * k + 2))

            def fast_weighted_onehots():
                dve.wait_ge(s_built, NBATCH + 4)
                dve.wait_ge(s_pdv, 2 * NT)
                rest = ew1C[:, 0:WN]
                for k in range(2):
                    v.tensor_copy(w_part[:, k, :], rest).then_inc(s_wpart, 1)
                    dve.wait_ge(s_wpart, 2 * k + 1)
                    v.tensor_tensor(rest, rest, w_part[:, k, :], ALU.subtract).then_inc(s_wpart, 1)
                    dve.wait_ge(s_wpart, 2 * k + 2)
                v.tensor_copy(w_part[:, 2, :], rest)
                v.tensor_copy(v_iota, iota_16[:, 0:RD, 0:VT]).then_inc(v_ready, 1)
                dve.wait_ge(v_ready, 1)

                def gathered_onehots(b, half):
                    dve.wait_ge(v_used, b * VT + (VRING - VT))
                    v.tensor_tensor(v_eq, v_iota, colR[:, ds(b * VT + V0, VT), 1].unsqueeze(1).to_broadcast(
                        [P, RD, VT]), ALU.is_equal).then_inc(v_eqs, 1)
                    dve.wait_ge(v_eqs, b + 1)
                    v.tensor_tensor(v_oh[:, half], v_eq, ew1R[:, ds(b * VT + (V0 - VB * BLC), VT)].unsqueeze(
                        1).to_broadcast([P, RD, VT]), ALU.mult).then_inc(v_ohs, 1)

                def step(b, half):
                    gathered_onehots(b, half)
                    for k in range(4):
                        onehots_weighted(b, k)

                with dve.Fori(0, DSTEPS // 2) as i:
                    for half in range(2):
                        step(i * 2 + half, half)
                step(DSTEPS - 1, 0)
                gathered_onehots(DSTEPS, 1)

            for q in range(3):
                with dve.If(fast == 1):
                    if q == 0:
                        fast_onehots()
                    if q == 1:
                        dve.wait_ge(s_h3, 10)
                    if q == 2:
                        fast_weighted_onehots()
                with dve.Else():
                    if q == 0:
                        general_start()
                    general_onehots(q, q)
                for t in range(NT):
                    dve.wait_ge(s_pmm, q * NT + t + 1)
                    ps = bank[6 + t % 2][:, 0:F]
                    if q < 2:
                        v.scalar_tensor_tensor(H[:, t, :], ps, innorm[:, t:t + 1], (b1b, b2b)[q],
                                               ALU.mult, ALU.add).then_inc(s_pdv, 1)
                    else:
                        v.tensor_tensor(xN[:, t, :], xN[:, t, :], ps, ALU.add).then_inc(s_pdv, 1)
                        if t:
                            dve.wait_ge(s_pdv, 2 * NT + t)
                            v.bn_stats(stats[:, t - 1, :], xN[:, t - 1, :])
                if q == 0:
                    split_pieces(1)

            dve.wait_ge(s_pdv, 3 * NT)
            ch.step(v.bn_stats(stats[:, NT - 1, :], xN[:, NT - 1, :]))
            ch.here()
            for t in range(NT):
                last = v.bn_aggr(aggr[:, t, :], stats[:, t, :])
            ch.step(last)
            ch.here()
            v.tensor_scalar(sc1, aggr[:, :, 1], LN_EPS, None, ALU.add).then_inc(s_lnv, 1)
            dve.wait_ge(s_lns, 2)
            ch.step(v.reciprocal(lnscale, sc1))
            ch.here()
            v.scalar_tensor_tensor(lnbias, aggr[:, :, 0], -1.0, lnscale, ALU.mult, ALU.mult).then_inc(s_lnr, 1)
            for i in range(5):
                if i != POOLS:
                    dve.wait_ge(s_h, 2 * 5 + i + 1)
                    split(ch, v, i * TP, (i + 1) * TP).then_inc(s_h3, 1)
            v.tensor_tensor(biasb, biasb, tpbb, ALU.add).then_inc(s_wparts, 1)

            with dve.If(fast == 1):
                dve.wait_ge(s_table, 16 * 5)
                v.tensor_copy(iota_t.rearrange("p (d j) -> p d j", j=RJ), iota_16[:, 0:RD, 0:RJ]).then_inc(s_wparts, 1)
                dve.wait_ge(s_wparts, 2)

                def block_columns(b):
                    dve.wait_ge(s_ohr, b * len(BUF))
                    v.tensor_copy(now, colR[:, ds(b * BLC, BLC), :]).then_inc(s_now, 1)
                    dve.wait_ge(s_now, b * 5 + 1)
                    rest = now[:, :, 2]
                    for k in range(2):
                        v.tensor_copy(wpart[:, k, :], rest).then_inc(s_now, 1)
                        dve.wait_ge(s_now, b * 5 + (2 * k + 2))
                        v.tensor_tensor(rest, rest, wpart[:, k, :], ALU.subtract).then_inc(s_now, 1)
                        dve.wait_ge(s_now, b * 5 + (2 * k + 3))
                    v.tensor_copy(wpart[:, 2, :], rest)

                def onehots(b, u):
                    dve.wait_ge(s_used, b * BLC + (RING + RJ * (u - 1)))
                    n, to = u * RJ, BUF[u]
                    cn = min(RJ, BLC - n)

                    def view(words):
                        return words.rearrange("p (d j) -> p d j", j=RJ)[:, :, 0:cn]

                    for oh, f in ((oh_typ, 3), (oh_rel, 1)):
                        last = v.tensor_tensor(view(oh[:, to, :]), view(iota_t),
                                               now[:, n:n + cn, f].unsqueeze(1).to_broadcast([P, RD, cn]), ALU.is_equal)
                    last.then_inc(s_rel, 1)
                    for j in range(cn):
                        v.tensor_scalar(oh_seg[:, to, j, :], iota_h, now[:, n + j, 0:1], None, ALU.is_equal)
                    dve.wait_ge(s_rel, b * len(BUF) + (u + 1))
                    for k in range(3):
                        last = v.tensor_tensor(view(oh_tim[:, to, k * RD * RJ:(k + 1) * RD * RJ]), view(oh_rel[:, to, :]),
                                               wpart[:, k, n:n + cn].unsqueeze(1).to_broadcast([P, RD, cn]), ALU.mult)
                    last.then_inc(s_ohr, 1)

                def result(b):
                    def there(k):
                        dve.wait_ge(s_fin, b * FS + (FS + k))
                        return k
                    dve.wait_ge(s_blk, b + 1)
                    mixed = bank[3]
                    v.scalar_tensor_tensor(fin[:, 0, :], mixed[:, F:2 * F], invdeg[:, ds(b, 1)], biasb, ALU.mult, ALU.add)
                    v.tensor_scalar(inv[:, 0, :], mixed[:, 2 * F:2 * F + R], 1.0, None, ALU.max).then_inc(s_fin, 1)
                    there(1)
                    v.tensor_tensor(fin[:, 1, :], mixed[:, 0:F], fin[:, 0, :], ALU.add)
                    v.reciprocal(inv[:, 1, :], inv[:, 0, :]).then_inc(s_fin, 1)
                    for r in range(R):
                        there(2 + r)
                        v.scalar_tensor_tensor(fin[:, r % 2, :], bank[4 + r // 4][:, (r % 4) * F:(r % 4 + 1) * F],
                                               inv[:, 1, r:r + 1], fin[:, (r + 1) % 2, :], ALU.mult,
                                               ALU.add).then_inc(s_fin, 1)
                    k = there(2 + R)
                    v.tensor_scalar(fin[:, 2, :], fin[:, (R - 1) % 2, :], 0.0, None, ALU.max).then_inc(s_fin, 1)
                    there(k + 1)
                    v.bn_stats(rowstat, fin[:, 2, :]).then_inc(s_fin, 1)
                    there(k + 2)
                    dve.sem_inc(s_gate2, 1)
                    v.bn_aggr(rowaggr, rowstat).then_inc(s_fin, 1)
                    there(k + 3)
                    v.tensor_scalar(rowsc[:, 0:1], rowaggr[:, 1:2], LN_EPS, None, ALU.add).then_inc(s_var, 1)
                    dve.wait_ge(s_rt, b + 1)
                    v.reciprocal(rowsc[:, 2:3], rowsc[:, 1:2]).then_inc(s_fin, 1)
                    there(k + 4)
                    v.tensor_scalar(fin[:, 3, :], fin[:, 2, :], rowaggr[:, 0:1], rowsc[:, 2:3], ALU.subtract,
                                    ALU.mult).then_inc(s_fin, 1)
                    there(k + 5)
                    v.tensor_tensor(fin[:, 4, :], fin[:, 3, :], gammab, ALU.mult).then_inc(s_fin, 1)
                    there(k + 6)
                    v.tensor_tensor(fin[:, 3, :], fin[:, 4, :], betab, ALU.add).then_inc(s_fin, 1)
                    assert there(k + 7) == FS

                def store(b):
                    dve.wait_ge(s_out, b * 16 + 16)
                    v.tensor_tensor(outt, fin[:, 3, :], xN[:, ds(b, 1), :].rearrange("p o f -> p (o f)"),
                                    ALU.add).then_inc(s_res, 1)

                dve.sem_inc(s_fin, FS)
                block_columns(0)
                for u in range(len(BUF)):
                    onehots(0, u)

                def onehots_block(b, chunks):
                    block_columns(b)
                    for u in range(-(-chunks // RJ)):
                        onehots(b, u)
                        if u == 2:
                            result(b - 1)
                            store(b - 1)

                with dve.Fori(1, NT - 1) as b:
                    onehots_block(b, BLC)
                onehots_block(NT - 1, LASTC)
                result(NT - 1)
                store(NT - 1)
            with dve.Else():
                GS = 9
                general_onehots(3, 3)
                dve.wait_ge(g_taken, 1)
                gch.step(v.tensor_scalar(aggT[0:R, :], aggT[0:R, :], 1.0, None, ALU.max))
                gch.here()
                v.reciprocal(aggT[0:R, :], aggT[0:R, :]).then_inc(g_inv, 1)
                general_onehots(4, 4)
                dve.wait_ge(g_tab, 64)
                for t in range(NT):
                    dve.wait_ge(g_trn, t + 1)
                    v.tensor_copy(H[:, t, :], bank[7][:, 0:F]).then_inc(g_rel, 1)
                general_onehots(5, 5)
                dve.sem_inc(g_res, 1)
                with dve.Fori(0, NT) as t:
                    def there(k):
                        dve.wait_ge(g_chain, t * GS + k)
                    dve.wait_ge(g_res, t + 1)
                    dve.wait_ge(g_blk, t + 1)
                    v.scalar_tensor_tensor(g_fin[:, 0, :], bank[7][:, F:2 * F], invdeg[:, ds(t, 1)], biasb, ALU.mult,
                                           ALU.add).then_inc(g_chain, 1)
                    there(1)
                    v.tensor_tensor(g_fin[:, 1, :], bank[7][:, 0:F], g_fin[:, 0, :], ALU.add).then_inc(g_chain, 1)
                    there(2)
                    v.tensor_tensor(g_fin[:, 2, :], g_fin[:, 1, :], H[:, ds(t, 1), :].rearrange("p o f -> p (o f)"),
                                    ALU.add).then_inc(g_chain, 1)
                    there(3)
                    v.tensor_scalar(g_fin[:, 3, :], g_fin[:, 2, :], 0.0, None, ALU.max).then_inc(g_chain, 1)
                    there(4)
                    v.bn_stats(rowstat, g_fin[:, 3, :]).then_inc(g_chain, 1)
                    there(5)
                    dve.sem_inc(s_gate2, 1)
                    v.bn_aggr(rowaggr, rowstat).then_inc(g_chain, 1)
                    there(6)
                    v.tensor_scalar(rowsc[:, 0:1], rowaggr[:, 1:2], LN_EPS, None, ALU.add).then_inc(g_var, 1)
                    dve.wait_ge(g_rt, t + 1)
                    v.reciprocal(rowsc[:, 2:3], rowsc[:, 1:2]).then_inc(g_chain, 1)
                    there(7)
                    v.tensor_scalar(g_fin[:, 4, :], g_fin[:, 3, :], rowaggr[:, 0:1], rowsc[:, 2:3], ALU.subtract,
                                    ALU.mult).then_inc(g_chain, 1)
                    there(8)
                    v.tensor_tensor(g_fin[:, 4, :], g_fin[:, 4, :], gammab, ALU.mult).then_inc(g_chain, 1)
                    there(9)
                    v.tensor_tensor(g_fin[:, 0, :], g_fin[:, 4, :], betab, ALU.add).then_inc(g_res2, 1)
                    dve.wait_ge(g_res2, t + 1)
                    dve.wait_ge(g_store, t * 16 + 16)
                    v.tensor_tensor(g_out, g_fin[:, 0, :], xN[:, ds(t, 1), :].rearrange("p o f -> p (o f)"),
                                    ALU.add).then_inc(g_res, 1)

        @block.scalar
        def _(act):
            a = nc.scalar
            act.wait_ge(s_wexp, 1)
            a.activation(tmp_rows.bitcast(F32), ew_rows, ACT.Exp, bias=tw[0:EP, 6:7], scale=tw[0:EP, 5:6],
                         accum_out=tw[0:EP, 7:8]).then_inc(s_twsum, 1)
            act.wait_ge(s_lnv, 1)
            act.wait_ge(s_sqd, 1)
            a.activation(sc2, sc2, ACT.Sqrt).then_inc(s_sqr, 1)
            a.activation(sc3, sc3, ACT.Sqrt)
            a.activation(sc1, sc1, ACT.Sqrt).then_inc(s_lns, 1)
            act.wait_ge(s_lnr, 1)
            for t in range(NT):
                last = a.activation(H[:, t, :], xN[:, t, :], ACT.Relu, bias=lnbias[:, t:t + 1],
                                    scale=lnscale[:, t:t + 1])
                if t % TP == TP - 1:
                    last.then_inc(s_h, 1)
            act.wait_ge(s_slots, 16 * (3 * WT + 5))
            a.activation(ew16, ew16, ACT.Exp, bias=tw[0:RP, 6:7], scale=tw[0:RP, 5:6]).then_inc(s_wexp, 1)
            u = 0
            for to in (keyB, loB, ew1C):
                for t in range(WT):
                    act.wait_ge(s_tps, u + 1)
                    a.copy(to[:, t * CAP:(t + 1) * CAP].rearrange("p (w h) -> p h w", h=HALF),
                           bank[4 + u % 4][:, 0:CAP].rearrange("p (h w) -> p h w", h=HALF)).then_inc(s_tpf, 1)
                    u += 1
            for to in (colR[:, :, 0], colR[:, :, 1], colR[:, :, 2], colR[:, :, 3], srcC, ew1R):
                for k0 in range(0, RK, 4):
                    kn = min(4, RK - k0)
                    act.wait_ge(s_tps, u + 1)
                    for k in range(kn):
                        first = VB if to is ew1R else 0
                        place = to.rearrange("p (b n) -> p n b", n=BLC)[:, k0 + k::RK]
                        last = a.copy(place, bank[4 + u % 4][:, k * RP:(k + 1) * RP].rearrange(
                            "p (c b) -> p c b", b=NT)[:, 0:place.shape[1], first:])
                    last.then_inc(s_tpf, 1)
                    u += 1
            act.wait_ge(s_tpf, 4 + u)
            act.sem_inc(s_cols, 1)
            act.wait_ge(s_wr, 1)
            fast = is_fast(act)

            def take(q, g, j):
                for k in range(4):
                    m = (min(q, 1) * NG + g) * GB + 4 * j + k
                    act.wait_ge(s_built, m + 5)
                    if j == 0 and k == 0 and q == 0 and g >= 4:
                        act.wait_ge(s_applied, 2 + g - 3)
                        act.wait_ge(spilled[g - 4], 16)
                    if j == 0 and k == 0 and q == 2:
                        act.wait_ge(s_applied, 2 * NG + max(g - 1, 0) + 2)
                    to = ATB[:, g % 4, :] if q == 0 else AT[:, g % 2, :]
                    a.copy(to[:, (4 * j + k) * BW * WC:(4 * j + k + 1) * BW * WC],
                           bank[k][:, 0:BW * WC]).then_inc(s_evac, 1)

            def take_agg(q, n):
                g = ORDER[q][n]
                act.wait_ge(s_applied, q * NG + n + 3)
                if q == 0 and n == 0:
                    act.wait_ge(s_h3, 5)
                if q == 1 and n == 0:
                    act.wait_ge(s_h3, 10)
                a.copy(aggT[:, g * GD:(g + 1) * GD], bank[4 + n % 2][:, 0:GD]).then_inc(s_agg, 1)

            def general_take(n, q):
                act.wait_ge(g_sum, n + 1)
                if q < 2:
                    act.wait_ge(s_h3, 5 * (q + 1))
                rows = R if q == 3 else P
                for i, w in GBANKS:
                    last = a.copy(aggT[0:rows, 512 * i:512 * i + w], bank[i][0:rows, 0:w])
                return last

            def take_gathered(k):
                act.wait_ge(v_used, VRING + VLAST[k] + 1)
                a.copy(aggT[:, (ND + k) * GD:(ND + k + 1) * GD], bank[6 + k % 2][:, 0:GD]).then_inc(v_agg, 1)

            for q in range(3):
                with act.If(fast == 1):
                    groups = ND if q == 2 else NG
                    for g in range(groups):
                        for j in range(GB // 4):
                            if q != 1:
                                take(q, g, j)
                            for k in range(NG - ND - 1):
                                if q == 2 and g * (GB // 4) + j == VLAST[k] // VT + 1:
                                    take_gathered(k)
                        if g > 0:
                            take_agg(q, g - 1)
                    take_agg(q, groups - 1)
                    if q == 2:
                        take_gathered(NG - ND - 1)
                with act.Else():
                    if q == 0:
                        act.wait_ge(g_rows, 80)
                        a.activation(g_ew, g_ew, ACT.Exp, bias=tw[0:EP, 6:7], scale=tw[0:EP, 5:6]).then_inc(g_ready, 1)
                    general_take(q, q).then_inc(s_agg, ND if q == 2 else NG)
                    if q == 2:
                        act.sem_inc(v_agg, NG - ND)
                if q == 0:
                    for t in range(NT):
                        act.wait_ge(s_pdv, t + 1)
                        last = a.activation(H[:, t, :], H[:, t, :], ACT.Relu, scale=onorm[:, t:t + 1])
                        if t % TP == TP - 1:
                            last.then_inc(s_h, 1)
            act.wait_ge(s_lnv, 2)
            a.activation(sc1, sc1, ACT.Sqrt).then_inc(s_lns, 1)
            act.wait_ge(s_lnr, 2)
            for t in range(NT):
                last = a.activation(H[:, t, :], xN[:, t, :], ACT.Relu, bias=lnbias[:, t:t + 1],
                                    scale=lnscale[:, t:t + 1])
                if t % TP == TP - 1:
                    last.then_inc(s_h, 1)
            for t in range(NT):
                act.wait_ge(s_htp, t + 1)
                a.copy(h2T[:, t * P:(t + 1) * P], bank[4 + t % 2][:, 0:P]).then_inc(s_htd, 1)
            with act.If(fast == 1):
                a.copy(idxs, srcC[:, 0:BLC]).then_inc(s_idx, 4)

                def root_of(b):
                    act.wait_ge(s_var, b + 1)
                    a.activation(rowsc[:, 1:2], rowsc[:, 0:1], ACT.Sqrt).then_inc(s_rt, 1)

                def block(b, first, chunks):
                    for q in range(4):
                        if QFIRST[q] >= chunks:
                            break
                        if q == 0 and not first:
                            act.wait_ge(s_blk, b)
                        end = min(QLAST[q] + 1, chunks)
                        act.wait_ge(s_used, b * BLC + (RING + end))
                        a.copy(aggn[:, :, q * QD:(q + 1) * QD],
                               bank[q % 2].rearrange("p (d r) -> p r d", r=R)).then_inc(s_wind, 1)
                        if chunks == BLC:
                            i0 = IXEND[q - 1] if q else 0
                            a.copy(idxs[:, i0:IXEND[q]],
                                   srcC[:, ds(b * BLC + (BLC + i0), IXEND[q] - i0)]).then_inc(s_idx, 1)
                        if q == 0 and not first:
                            root_of(b - 1)
                    a.copy(timeT.rearrange("p k d -> p (k d)"), bank[2][:, 0:3 * P])
                    a.copy(cntT, bank[2][0:R, 3 * P:4 * P]).then_inc(s_timd, 1)
                    a.copy(h2Tt, h2T[:, ds(b * P, P)]).then_inc(s_timd, 1)

                block(0, True, BLC)
                with act.Fori(1, NT - 1) as b:
                    block(b, False, BLC)
                block(NT - 1, False, LASTC)
                root_of(NT - 1)
            with act.Else():
                act.sem_inc(g_ycopy, 2)
                with act.Fori(0, NT) as t:
                    act.wait_ge(g_ymm, t * (R // 4) + 1)
                    act.sem_inc(s_gate3, 1)
                    a.copy(g_tile, h2T[:, ds(t * P, P)]).then_inc(g_tcopy, 1)
                    for k in range(R // 4):
                        act.wait_ge(g_ymm, t * (R // 4) + (k + 2))
                        act.wait_ge(g_yout, t * (16 * (R // 4)) + 16 * (k + 1))
                        a.copy(g_y, bank[6 + k % 2]).then_inc(g_ycopy, 1)
                general_take(3, 3).then_inc(g_taken, 1)
                act.wait_ge(g_invd, 16)
                general_take(4, 4).then_inc(g_taken, 1)
                act.wait_ge(g_rel, NT)
                general_take(5, 5).then_inc(g_taken, 1)
                with act.Fori(0, NT) as t:
                    act.wait_ge(g_var, t + 1)
                    a.activation(rowsc[:, 1:2], rowsc[:, 0:1], ACT.Sqrt).then_inc(g_rt, 1)

        @block.tensor
        def _(pe):
            t_ = nc.tensor
            pe.wait_ge(s_const, 1)
            zero = ohlo[:, 0, 0:HL]
            clear_h = iota_rep.rearrange("p j c -> p (j c)")[:, 0:HH]
            t_.matmul(bank[0][0:HL, 0:HH], zero, clear_h, start=True, stop=False, skip_group_check=True)
            t_.matmul(bank[1][0:HL, 0:HH], zero, clear_h, start=True, stop=False,
                      skip_group_check=True).then_inc(s_hmm, 2)

            def histogram_step(step, par, last_step=False):
                pe.wait_ge(s_hoh, step + 1)
                for c in range(HCOL):
                    for a in range(2):
                        lo = ohlo[:, 2 * par + a, :].rearrange("p (j c) -> p j c", c=HCOL)[:, :, c]
                        hi = ohhi[:, 2 * par + a, :].rearrange("p (j c) -> p j c", c=HCOL)[:, :, c]
                        mm = t_.matmul(bank[a][0:HL, 0:HH], lo, hi, start=False, stop=last_step and c == HCOL - 1,
                                       skip_group_check=True)
                mm.then_inc(s_hmm, 1)

            with pe.Fori(0, HSTEPS // 2) as i:
                for par in range(2):
                    histogram_step(i * 2 + par, par)
            histogram_step(HSTEPS - 1, 0, True)
            pe.wait_ge(s_hist, 1)
            for a in range(2):
                halves = hist[:, a, :].rearrange("p (t o) -> p o t", o=2)
                for o, place in enumerate((ident[0:HL, :], shifted)):
                    mm = t_.matmul(bank[4][:, a * NT:(a + 1) * NT], place, halves[:, o], start=(o == 0), stop=(o == 1))
            mm.then_inc(s_histps, 1)
            pe.wait_ge(s_deg, 1)
            t_.matmul(bank[2][:, 0:NT], upper, degin, start=True, stop=True)
            t_.matmul(bank[2][:, 64:64 + NT], onesf, degin, start=True, stop=True).then_inc(s_cumps, 1)
            pe.wait_ge(s_start, 1)
            t_.transpose(bank[3][0:NT, 0:P], lnbias, ident).then_inc(s_cumps, 1)
            pe.wait_ge(s_match, 1)
            pe.wait_ge(s_startT, 1)
            t_.matmul(bank[3][:, 0:2], onesf, matched[:, 0:2], start=True, stop=True).then_inc(s_matchps, 1)
            pe.sem_inc(s_tpf, 4)
            u = 0
            pe.wait_ge(s_win, 1)
            for of in (key5, lo5, ew15):
                for t in range(WT):
                    pe.wait_ge(s_tpf, u + 1)
                    for h in range(HALF):
                        mm = t_.transpose(bank[4 + u % 4][:, h * P:(h + 1) * P], of[:, t, h * P:(h + 1) * P], ident)
                    mm.then_inc(s_tps, 1)
                    u += 1
            for of in (seg16, rel16, ew16, tyf16, srf16, ew116):
                for k0 in range(0, RK, 4):
                    pe.wait_ge(s_tpf, u + 1)
                    for k in range(min(4, RK - k0)):
                        mm = t_.transpose(bank[4 + u % 4][:, k * RP:(k + 1) * RP], of[:, (k0 + k) * P:(k0 + k + 1) * P],
                                          ident[0:RP, 0:RP])
                    mm.then_inc(s_tps, 1)
                    u += 1

            fast = is_fast(pe)
            clear = iota_16.rearrange("p j c -> p (j c)")
            pe.sem_inc(s_built, 4)
            pe.sem_inc(s_applied, 2)
            pe.sem_inc(v_used, VRING)
            pe.wait_ge(s_cols, 1)

            def build(q, g, i):
                m = (min(q, 1) * NG + g) * GB + i
                pe.wait_ge(s_oh, m + 1)
                if m >= 4:
                    pe.wait_ge(s_evac, m - 3)
                for w in range(BW):
                    for h in range(HALF):
                        c = HALF * w + h
                        to = bank[i % 4][:, w * WC:(w + 1) * WC]
                        if q == 0:
                            half, at16 = (m // 2) % 2, (m % 2) * BS + c
                            mm = t_.matmul(to, oh_lo_b[:, half, :, at16], oh_dh_b[:, half, :, at16],
                                           start=(h == 0), stop=(h == HALF - 1))
                        else:
                            for part in range(3):
                                mm = t_.matmul(to, w_lo[:, i % 2, :, c], w_dh[:, i % 2, part, :, c],
                                               start=(h == 0 and part == 0), stop=(h == HALF - 1 and part == 2))
                mm.then_inc(s_built, 1)

            def apply(q, n, hi):
                g = ORDER[q][n]
                gg = q * NG + n
                if hi == 0:
                    if q != 1:
                        pe.wait_ge(s_evac, (min(q, 1) * NG + g + 1) * GB)
                    elif g < 4:
                        pe.wait_ge(reloaded[g], 16)
                    if gg >= 2:
                        pe.wait_ge(s_agg, gg - 1)
                    if q == 2:
                        pe.wait_ge(s_pdv, 2 * NT)
                if q < 2 and n == 0 and hi % (NT // 5) == 0:
                    pe.wait_ge(s_h3, q * 5 + hi // (NT // 5) + 1)
                to = bank[4 + n % 2][:, 0:GD]
                if q < 2:
                    block = ATB[:, g % 4, :].rearrange("p (d s) -> p d s", s=NT)[:, :, hi]
                    for k in range(3):
                        mm = t_.matmul(to, H3[:, hi, k * F:(k + 1) * F], block,
                                       start=(hi == 0 and k == 0), stop=(hi == NT - 1 and k == 2))
                else:
                    block = AT[:, g % 2, :].rearrange("p (d s) -> p d s", s=NT)[:, :, hi]
                    mm = t_.matmul(to, H[:, hi, :], block, start=(hi == 0), stop=(hi == NT - 1))
                if hi == NT - 1:
                    mm.then_inc(s_applied, 1)

            def apply_part(part, hi):
                n = ND - 1
                if hi == 0:
                    pe.wait_ge(s_evac, (NG + n) * GB + (part + 1) * (GB // 4))
                    if part == 0:
                        pe.wait_ge(s_agg, 2 * NG + n - 1)
                c0, c1 = part * GD // 4, (part + 1) * GD // 4
                block = AT[:, n % 2, :].rearrange("p (d s) -> p d s", s=NT)[:, c0:c1, hi]
                mm = t_.matmul(bank[4 + n % 2][:, c0:c1], H[:, hi, :], block, start=(hi == 0), stop=(hi == NT - 1))
                if hi == NT - 1 and part == 3:
                    mm.then_inc(s_applied, 1)

            def general_pass(n, q):
                if n == 0:
                    pe.sem_inc(g_mm, 1)
                    pe.wait_ge(g_ready, 2)
                if n in (1, 2):
                    pe.wait_ge(s_pdv, n * NT)
                if n == 3:
                    pe.wait_ge(g_ycopy, NT * (R // 4) + 2)
                if n > 3:
                    pe.wait_ge(g_taken, n - 3)
                if n == 5:
                    pe.wait_ge(g_rel, NT)
                rows = g_toh if q == 3 else g_row
                m = R if q == 3 else P
                for i, w in GBANKS:
                    t_.matmul(bank[i][0:m, 0:w], g_zero[:, 0:m], g_iota[:, 0:w], start=True, stop=False,
                              skip_group_check=True)
                with pe.Fori(0, EC) as c:
                    if q != 3:
                        pe.wait_ge(g_landed[q > 2], c * 16 + (16 * EC * (n if n < 3 else n - 4) + 16))
                    pe.wait_ge(g_ohr, c + (n * EC + 1))
                    for i, w in GBANKS:
                        mm = t_.matmul(bank[i][0:m, 0:w], rows, g_oh[:, 512 * i:512 * i + w], start=False, stop=False,
                                       skip_group_check=True)
                    mm.then_inc(g_mm, 1)
                pe.wait_ge(g_mm, (n + 1) * EC + 1)
                pe.sem_inc(g_sum, 1)

            def gathered(n):
                step = n // VT
                if n % VT == 0:
                    pe.wait_ge(v_ohs, step + 1)
                for k in range(NG - ND):
                    if VFIRST[k] == n:
                        if k == 2:
                            pe.wait_ge(v_agg, 1)
                        t_.matmul(bank[6 + k % 2][:, 0:GD], zerob, clear[:, 0:GD], start=True, stop=False,
                                  skip_group_check=True)
                if n % RJ == 0:
                    pe.wait_ge(v_landed[n % VRING // RJ], 16 * (n // VRING * RJ + min(RJ, VN - n)))
                for k in range(NG - ND):
                    d0, d1 = max(VBASE[n], k * GD), min(VBASE[n] + RD, (k + 1) * GD)
                    if d0 < d1:
                        mm = t_.matmul(bank[6 + k % 2][:, d0 - k * GD:d1 - k * GD], v_ring[:, n % VRING, :],
                                       v_oh[:, step % 2, d0 - VBASE[n]:d1 - VBASE[n], n % VT],
                                       start=False, stop=False, skip_group_check=True)
                mm.then_inc(v_used, 1)

            for q in range(3):
                with pe.If(fast == 1):
                    groups = ND if q == 2 else NG
                    for g in range(groups + 1):
                        for i in range(GB):
                            if g < groups and q != 1:
                                build(q, g, i)
                            part, piece_ = divmod(i - 6, 5)
                            if q == 2 and g == ND - 1 and 0 <= part:
                                for hi in range(piece_ * TP, (piece_ + 1) * TP):
                                    apply_part(part, hi)
                            if q == 2 and g == ND and i == 0:
                                for part, first in ((2, 4 * TP), (3, 0)):
                                    for hi in range(first, NT):
                                        apply_part(part, hi)
                            if g > 0 and not (q == 2 and g == ND):
                                for hi in range(NT * max(i - 1, 0) // (GB - 1), NT * i // (GB - 1)):
                                    apply(q, g - 1, hi)
                            if q == 2:
                                batch = g * GB + i
                                for n in range(VT * batch // 4, min(VT * (batch + 1) // 4, VN)):
                                    gathered(n)
                with pe.Else():
                    general_pass(q, q)
                pe.wait_ge(s_agg, q * NG + (ND if q == 2 else NG))
                if q == 2:
                    pe.wait_ge(v_agg, NG - ND)
                for t in range(NT):
                    if q * NT + t >= 2:
                        pe.wait_ge(s_pdv, q * NT + t - 1)
                    tile = aggT[:, t * P:(t + 1) * P]
                    if q < 2:
                        mm = t_.matmul(bank[6 + t % 2][:, 0:F], tile, (W1s, W2s)[q], start=True, stop=True)
                    else:
                        mm = t_.transpose(bank[6 + t % 2][:, 0:F], tile, ident)
                    mm.then_inc(s_pmm, 1)
            for t in range(NT):
                if t % TP == 0:
                    pe.wait_ge(s_h, 2 * 5 + t // TP + 1)
                if t >= 2:
                    pe.wait_ge(s_htd, t - 1)
                t_.transpose(bank[4 + t % 2][:, 0:P], H[:, t, :], ident).then_inc(s_htp, 1)

            with pe.If(fast == 1):
                pe.wait_ge(s_htd, NT)
                pe.sem_inc(s_used, RING)
                pe.sem_inc(s_wind, 2)

                def chunk(b, n, first):
                    u, j = n // RJ, n % RJ
                    if j == 0:
                        pe.wait_ge(s_ohr, b * len(BUF) + (u + 1))
                    if n == 0:
                        if not first:
                            pe.wait_ge(s_timd, b * 2)
                        t_.matmul(bank[2], zerob, clear[:, 0:512], start=True, stop=False, skip_group_check=True)
                    for q in range(4):
                        if QFIRST[q] == n:
                            pe.wait_ge(s_wind, b * 4 + (q + 1))
                            t_.matmul(bank[q % 2], zerob, clear[:, 0:512], start=True, stop=False, skip_group_check=True)
                    if j == 0:
                        size = 16 * min(RJ, BLC - n)
                        pe.wait_ge(landed[u], b * size + size)
                    seg, d0 = oh_seg[:, BUF[u], j, :], RANGE[n]
                    tim = oh_tim[:, BUF[u], :].rearrange("p (k d j) -> p k d j", k=3, j=RJ)[:, :, :, j]
                    rel, typ = (oh[:, BUF[u], :].rearrange("p (d j) -> p d j", j=RJ)[:, :, j] for oh in (oh_rel, oh_typ))
                    for k in range(3):
                        row = ring[:, n, k * F:(k + 1) * F]
                        for q in range(4):
                            a0, a1 = max(d0, q * QD), min(d0 + RD, (q + 1) * QD)
                            if a0 < a1:
                                t_.matmul(bank[q % 2][:, (a0 - q * QD) * R:(a1 - q * QD) * R], row,
                                          seg[:, (a0 - d0) * R:(a1 - d0) * R], start=False, stop=False,
                                          skip_group_check=True)
                        t_.matmul(bank[2][:, 0:3 * P].rearrange("p (k d) -> p k d", d=P)[:, :, d0:d0 + RD], row, tim,
                                  start=False, stop=False, skip_group_check=True)
                    t_.matmul(bank[2][0:R, 3 * P + d0:3 * P + d0 + RD], typ, rel, start=False, stop=False,
                              skip_group_check=True).then_inc(s_used, 1)

                def block_product(b, chunks):
                    quarters = 4 if chunks == BLC else sum(n < chunks for n in QFIRST)
                    pe.wait_ge(s_wind, b * 4 + (quarters + 2))
                    pe.wait_ge(s_timd, b * 2 + 2)
                    pe.wait_ge(s_fin, b * FS + (R + 2))
                    mixed = bank[3]
                    t_.matmul(mixed[:, 0:F], h2Tt, roots, start=True, stop=True, skip_group_check=True)
                    for k in range(3):
                        t_.matmul(mixed[:, F:2 * F], timeT[:, k, :], tpws, start=(k == 0), stop=(k == 2),
                                  skip_group_check=True)
                    for r in range(R):
                        t_.matmul(bank[4 + r // 4][:, (r % 4) * F:(r % 4 + 1) * F], aggn[:, r, :], Wr[:, r, :],
                                  start=True, stop=True, skip_group_check=True)
                    mm = t_.matmul(mixed[:, 2 * F:2 * F + R], cntT, ident[0:R, 0:R], start=True, stop=True,
                                   skip_group_check=True)
                    mm.then_inc(s_blk, 1)

                def block(b, chunks):
                    for n in range(chunks):
                        chunk(b, n, False)
                        if n == RJ - 1:
                            block_product(b - 1, BLC)

                for n in range(BLC):
                    chunk(0, n, True)
                with pe.Fori(1, NT - 1) as b:
                    block(b, BLC)
                block(NT - 1, LASTC)
                block_product(NT - 1, LASTC)
            with pe.Else():
                pe.wait_ge(s_htd, NT)
                pe.sem_inc(g_ymm, 1)
                with pe.Fori(0, NT) as t:
                    pe.wait_ge(g_tcopy, t + 1)
                    for k in range(R // 4):
                        pe.wait_ge(g_ycopy, t * (R // 4) + (k + 1))
                        t_.matmul(bank[6 + k % 2], g_tile, Wr[:, 4 * k:4 * k + 4, :].rearrange("p r f -> p (r f)"),
                                  start=True, stop=True).then_inc(g_ymm, 1)
                general_pass(3, 3)
                general_pass(4, 4)
                pe.wait_ge(g_taken, 2)
                for t in range(NT):
                    pe.wait_ge(g_rel, t)
                    t_.transpose(bank[7][:, 0:F], aggT[:, t * P:(t + 1) * P], ident).then_inc(g_trn, 1)
                general_pass(5, 5)
                pe.wait_ge(g_taken, 3)
                for t in range(NT):
                    if t:
                        pe.wait_ge(g_chain, (t - 1) * 9 + 2)
                    t_.matmul(bank[7][:, 0:F], h2T[:, t * P:(t + 1) * P], roots, start=True, stop=True,
                              skip_group_check=True)
                    t_.matmul(bank[7][:, F:2 * F], aggT[:, t * P:(t + 1) * P], tpws, start=True, stop=True,
                              skip_group_check=True).then_inc(g_blk, 1)


_INS = ["x", "src", "dst", "edge_type_16", "edge_weight", "edge_weight1", "L0_gnn_W1", "L0_gnn_b1", "L0_gnn_W2",
        "L0_gnn_b2", "L1_gnn_basis", "L1_gnn_comp", "L1_gnn_root", "L1_gnn_bias", "L1_gnn_tp_w", "L1_gnn_tp_b",
        "L1_gnn_gamma", "L1_gnn_beta"]


def kernel(**inputs):
    import numpy as _np
    import concourse.bacc as _bacc
    from concourse import mybir as _mybir
    from concourse.bass_utils import run_bass_kernel_spmd as _run

    nc = _bacc.Bacc("TRN2", target_bir_lowering=False, num_devices=1)
    arrays, args = {}, []
    for name in _INS:
        a = _np.ascontiguousarray(inputs[name])
        arrays[f"in_{name}_dram"] = a
        args.append(nc.dram_tensor(f"in_{name}_dram", a.shape, _mybir.dt.from_np(a.dtype), kind="ExternalInput").ap())
    shape = _np.asarray(inputs["x"]).shape
    args.append(nc.dram_tensor("out_0_dram", shape, _mybir.dt.float32, kind="ExternalOutput").ap())
    gnn_kernel(nc, *args)
    r = _run(nc, [arrays], core_ids=[0])
    return r.results[0]["out_0_dram"]
```
